# Optimizing a Trainium2 kernel written in Bass

```python
import numpy as np
import jax
import jax.numpy as jnp

def _softmax(x, axis=-1):
    return jax.nn.softmax(x, axis=axis)

def _gelu(x):
    return jax.nn.gelu(x, approximate=True)

def _silu(x):
    return jax.nn.silu(x)

def _sigmoid(x):
    return jax.nn.sigmoid(x)

def _layernorm(x, axis=-1, eps=1e-05):
    m = jnp.mean(x, axis=axis, keepdims=True)
    v = jnp.var(x, axis=axis, keepdims=True)
    return (x - m) / jnp.sqrt(v + eps)

def _scatter_add(tgt, idx, src, axis=0):
    return tgt.at[idx].add(src)

def _segment_sum(src, seg, n):
    return jax.ops.segment_sum(src, seg, n)
kernel_name = 'mk_seq_postln_d1_jaxref_r8_8badb9'

def setup_inputs(seed: int=0):
    np.random.seed(seed)
    _w = jnp.asarray

    def _L0_attn_setup():
        import jax, jax.numpy as jnp
        import numpy as np
        from jax import lax
        B, L, D = (4, 256, 128)
        DSTATE, DCONV, EXPAND, NGROUPS, CHUNK = (128, 4, 2, 1, 32)
        HEADDIM = 64
        DINNER = EXPAND * D
        NHEADS = DINNER // HEADDIM
        CONVDIM = DINNER + 2 * NGROUPS * DSTATE
        DINPROJ = 2 * DINNER + 2 * NGROUPS * DSTATE + NHEADS
        EPS_OUT = 1.1920929e-07
        EPS_GATE = 1e-05

        def rmsnorm(x, eps):
            return x * lax.rsqrt(jnp.mean(x * x, -1, keepdims=True) + eps)

        def segsum(x):
            c = x.shape[-1]
            xc = jnp.cumsum(x, -1)
            d = xc[..., :, None] - xc[..., None, :]
            mask = jnp.tril(jnp.ones((c, c), bool))
            return jnp.where(mask, d, -jnp.inf)

        def mamba2(xn, w_in, conv_w, conv_b, dt_bias, a_log, d_skip, norm_w, w_out):
            b, l, _ = xn.shape
            zxbcdt = xn @ w_in
            z = zxbcdt[..., :DINNER]
            xbc = zxbcdt[..., DINNER:DINNER + CONVDIM]
            dt_raw = zxbcdt[..., DINNER + CONVDIM:]
            xp = jnp.pad(xbc, ((0, 0), (DCONV - 1, 0), (0, 0)))
            xc = sum((xp[:, k:k + l, :] * conv_w[:, k] for k in range(DCONV))) + conv_b
            xc = jax.nn.silu(xc)
            xh = xc[..., :DINNER].reshape(b, l, NHEADS, HEADDIM)
            Bm = xc[..., DINNER:DINNER + NGROUPS * DSTATE].reshape(b, l, NGROUPS, DSTATE)
            Cm = xc[..., DINNER + NGROUPS * DSTATE:].reshape(b, l, NGROUPS, DSTATE)
            hpg = NHEADS // NGROUPS
            Bh = jnp.repeat(Bm, hpg, 2)
            Ch = jnp.repeat(Cm, hpg, 2)
            dt = jax.nn.softplus(dt_raw + dt_bias)
            a = dt * -jnp.exp(a_log)
            u = dt[..., None] * xh
            nc = l // CHUNK
            uc = u.reshape(b, nc, CHUNK, NHEADS, HEADDIM)
            Bc = Bh.reshape(b, nc, CHUNK, NHEADS, DSTATE)
            Cc = Ch.reshape(b, nc, CHUNK, NHEADS, DSTATE)
            ac = a.reshape(b, nc, CHUNK, NHEADS).transpose(0, 3, 1, 2)
            a_cum = jnp.cumsum(ac, -1)
            Lmat = jnp.exp(segsum(ac))
            y_diag = jnp.einsum('bclhn,bcshn,bhcls,bcshp->bclhp', Cc, Bc, Lmat, uc)
            decay_states = jnp.exp(a_cum[..., -1:] - a_cum)
            states = jnp.einsum('bclhn,bhcl,bclhp->bchpn', Bc, decay_states, uc)
            chunk_decay = jnp.exp(a_cum[..., -1])

            def step(s, inp):
                dec, st = inp
                return (s * dec[..., None, None] + st, s)
            xs = (jnp.moveaxis(chunk_decay, -1, 0), jnp.moveaxis(states, 1, 0))
            s0 = jnp.zeros((b, NHEADS, HEADDIM, DSTATE), xn.dtype)
            _, prev = lax.scan(step, s0, xs)
            prev = jnp.moveaxis(prev, 0, 1)
            y_off = jnp.einsum('bclhn,bchpn,bhcl->bclhp', Cc, prev, jnp.exp(a_cum))
            y = (y_diag + y_off).reshape(b, l, NHEADS, HEADDIM) + d_skip[:, None] * xh
            y = y.reshape(b, l, DINNER)
            g = rmsnorm(y * jax.nn.silu(z), EPS_GATE) * norm_w
            return g @ w_out
        key = jax.random.key(seed)
        ks = jax.random.split(key, 10)
        sc = lambda k, sh, s: jax.random.normal(k, sh, jnp.float32) * s
        return {'x': sc(ks[0], (B, L, D), 1.0), 'w_in': sc(ks[1], (D, DINPROJ), D ** (-0.5)), 'conv_w': sc(ks[2], (CONVDIM, DCONV), DCONV ** (-0.5)), 'conv_b': jnp.zeros((CONVDIM,), jnp.float32), 'dt_bias': sc(ks[3], (NHEADS,), 0.5), 'a_log': jnp.log(jax.random.uniform(ks[4], (NHEADS,), jnp.float32, 1.0, 16.0)), 'd_skip': jnp.ones((NHEADS,), jnp.float32), 'norm_w': jnp.ones((DINNER,), jnp.float32), 'w_out': sc(ks[5], (DINNER, D), DINNER ** (-0.5)), 'w_fc': sc(ks[6], (D, 4 * D), D ** (-0.5)), 'w_proj': sc(ks[7], (4 * D, D), (4 * D) ** (-0.5))}
    _L0_attn_in = _L0_attn_setup()

    def _L0_ffn_setup():
        import jax, jax.numpy as jnp
        import numpy as np
        B, S, D, H, M, E, K = (4, 128, 128, 16, 2, 8, 2)
        KD = D // H
        F = 2 * D
        EPS = 1e-06

        def _ln(x, g, b):
            m = jnp.mean(x, axis=-1, keepdims=True)
            v = jnp.mean(jnp.square(x - m), axis=-1, keepdims=True)
            return (x - m) * jax.lax.rsqrt(v + EPS) * g + b
        key = jax.random.key(seed)
        ks = jax.random.split(key, 12)
        r = lambda i, shape: jax.random.normal(ks[i], shape, jnp.float32) * 0.02
        return {'x': jax.random.normal(ks[0], (B, S, D), jnp.float32), 'ln1_g': jnp.ones((D,), jnp.float32), 'ln1_b': jnp.zeros((D,), jnp.float32), 'ln2_g': jnp.ones((D,), jnp.float32), 'ln2_b': jnp.zeros((D,), jnp.float32), 'mha_wq': r(1, (M, D, H, KD)), 'mha_bq': jnp.zeros((M, H, KD), jnp.float32), 'mha_wk': r(2, (M, D, H, KD)), 'mha_bk': jnp.zeros((M, H, KD), jnp.float32), 'mha_wv': r(3, (M, D, H, KD)), 'mha_bv': jnp.zeros((M, H, KD), jnp.float32), 'mha_wo': r(4, (M, H, KD, D)), 'mha_bo': jnp.zeros((M, D), jnp.float32), 'mha_rw': r(5, (D, M)), 'mha_rb': jnp.zeros((M,), jnp.float32), 'ffn_rw': r(6, (D, E)), 'ffn_rb': jnp.zeros((E,), jnp.float32), 'fw1': r(7, (E, D, F)), 'fw2': r(8, (E, F, D))}
    _L0_ffn_in = _L0_ffn_setup()
    _d = {'L0_attn_x': _L0_attn_in['x'], 'L0_attn_w_in': _L0_attn_in['w_in'], 'L0_attn_conv_w': _L0_attn_in['conv_w'], 'L0_attn_conv_b': _L0_attn_in['conv_b'], 'L0_attn_dt_bias': _L0_attn_in['dt_bias'], 'L0_attn_a_log': _L0_attn_in['a_log'], 'L0_attn_d_skip': _L0_attn_in['d_skip'], 'L0_attn_norm_w': _L0_attn_in['norm_w'], 'L0_attn_w_out': _L0_attn_in['w_out'], 'L0_attn_w_fc': _L0_attn_in['w_fc'], 'L0_attn_w_proj': _L0_attn_in['w_proj'], 'L0_ffn_ln1_g': _L0_ffn_in['ln1_g'], 'L0_ffn_ln1_b': _L0_ffn_in['ln1_b'], 'L0_ffn_ln2_g': _L0_ffn_in['ln2_g'], 'L0_ffn_ln2_b': _L0_ffn_in['ln2_b'], 'L0_ffn_mha_wq': _L0_ffn_in['mha_wq'], 'L0_ffn_mha_bq': _L0_ffn_in['mha_bq'], 'L0_ffn_mha_wk': _L0_ffn_in['mha_wk'], 'L0_ffn_mha_bk': _L0_ffn_in['mha_bk'], 'L0_ffn_mha_wv': _L0_ffn_in['mha_wv'], 'L0_ffn_mha_bv': _L0_ffn_in['mha_bv'], 'L0_ffn_mha_wo': _L0_ffn_in['mha_wo'], 'L0_ffn_mha_bo': _L0_ffn_in['mha_bo'], 'L0_ffn_mha_rw': _L0_ffn_in['mha_rw'], 'L0_ffn_mha_rb': _L0_ffn_in['mha_rb'], 'L0_ffn_ffn_rw': _L0_ffn_in['ffn_rw'], 'L0_ffn_ffn_rb': _L0_ffn_in['ffn_rb'], 'L0_ffn_fw1': _L0_ffn_in['fw1'], 'L0_ffn_fw2': _L0_ffn_in['fw2']}
    _x0 = _d['L0_attn_x']
    _d['L0_attn_x'] = jax.random.normal(jax.random.fold_in(jax.random.key(seed), 1), (8, 512, 128), dtype=_x0.dtype)
    del _x0
    return _d

def reference(L0_attn_x, L0_attn_w_in, L0_attn_conv_w, L0_attn_conv_b, L0_attn_dt_bias, L0_attn_a_log, L0_attn_d_skip, L0_attn_norm_w, L0_attn_w_out, L0_attn_w_fc, L0_attn_w_proj, L0_ffn_ln1_g, L0_ffn_ln1_b, L0_ffn_ln2_g, L0_ffn_ln2_b, L0_ffn_mha_wq, L0_ffn_mha_bq, L0_ffn_mha_wk, L0_ffn_mha_bk, L0_ffn_mha_wv, L0_ffn_mha_bv, L0_ffn_mha_wo, L0_ffn_mha_bo, L0_ffn_mha_rw, L0_ffn_mha_rb, L0_ffn_ffn_rw, L0_ffn_ffn_rb, L0_ffn_fw1, L0_ffn_fw2):

    def _L0_attn_ref(x, w_in, conv_w, conv_b, dt_bias, a_log, d_skip, norm_w, w_out, w_fc, w_proj):
        import jax, jax.numpy as jnp
        import numpy as np
        from jax import lax
        B, L, D = (4, 256, 128)
        DSTATE, DCONV, EXPAND, NGROUPS, CHUNK = (128, 4, 2, 1, 32)
        HEADDIM = 64
        DINNER = EXPAND * D
        NHEADS = DINNER // HEADDIM
        CONVDIM = DINNER + 2 * NGROUPS * DSTATE
        DINPROJ = 2 * DINNER + 2 * NGROUPS * DSTATE + NHEADS
        EPS_OUT = 1.1920929e-07
        EPS_GATE = 1e-05

        def rmsnorm(x, eps):
            return x * lax.rsqrt(jnp.mean(x * x, -1, keepdims=True) + eps)

        def segsum(x):
            c = x.shape[-1]
            xc = jnp.cumsum(x, -1)
            d = xc[..., :, None] - xc[..., None, :]
            mask = jnp.tril(jnp.ones((c, c), bool))
            return jnp.where(mask, d, -jnp.inf)

        def mamba2(xn, w_in, conv_w, conv_b, dt_bias, a_log, d_skip, norm_w, w_out):
            b, l, _ = xn.shape
            zxbcdt = xn @ w_in
            z = zxbcdt[..., :DINNER]
            xbc = zxbcdt[..., DINNER:DINNER + CONVDIM]
            dt_raw = zxbcdt[..., DINNER + CONVDIM:]
            xp = jnp.pad(xbc, ((0, 0), (DCONV - 1, 0), (0, 0)))
            xc = sum((xp[:, k:k + l, :] * conv_w[:, k] for k in range(DCONV))) + conv_b
            xc = jax.nn.silu(xc)
            xh = xc[..., :DINNER].reshape(b, l, NHEADS, HEADDIM)
            Bm = xc[..., DINNER:DINNER + NGROUPS * DSTATE].reshape(b, l, NGROUPS, DSTATE)
            Cm = xc[..., DINNER + NGROUPS * DSTATE:].reshape(b, l, NGROUPS, DSTATE)
            hpg = NHEADS // NGROUPS
            Bh = jnp.repeat(Bm, hpg, 2)
            Ch = jnp.repeat(Cm, hpg, 2)
            dt = jax.nn.softplus(dt_raw + dt_bias)
            a = dt * -jnp.exp(a_log)
            u = dt[..., None] * xh
            nc = l // CHUNK
            uc = u.reshape(b, nc, CHUNK, NHEADS, HEADDIM)
            Bc = Bh.reshape(b, nc, CHUNK, NHEADS, DSTATE)
            Cc = Ch.reshape(b, nc, CHUNK, NHEADS, DSTATE)
            ac = a.reshape(b, nc, CHUNK, NHEADS).transpose(0, 3, 1, 2)
            a_cum = jnp.cumsum(ac, -1)
            Lmat = jnp.exp(segsum(ac))
            y_diag = jnp.einsum('bclhn,bcshn,bhcls,bcshp->bclhp', Cc, Bc, Lmat, uc)
            decay_states = jnp.exp(a_cum[..., -1:] - a_cum)
            states = jnp.einsum('bclhn,bhcl,bclhp->bchpn', Bc, decay_states, uc)
            chunk_decay = jnp.exp(a_cum[..., -1])

            def step(s, inp):
                dec, st = inp
                return (s * dec[..., None, None] + st, s)
            xs = (jnp.moveaxis(chunk_decay, -1, 0), jnp.moveaxis(states, 1, 0))
            s0 = jnp.zeros((b, NHEADS, HEADDIM, DSTATE), xn.dtype)
            _, prev = lax.scan(step, s0, xs)
            prev = jnp.moveaxis(prev, 0, 1)
            y_off = jnp.einsum('bclhn,bchpn,bhcl->bclhp', Cc, prev, jnp.exp(a_cum))
            y = (y_diag + y_off).reshape(b, l, NHEADS, HEADDIM) + d_skip[:, None] * xh
            y = y.reshape(b, l, DINNER)
            g = rmsnorm(y * jax.nn.silu(z), EPS_GATE) * norm_w
            return g @ w_out
        h = x + mamba2(rmsnorm(x, EPS_OUT), w_in, conv_w, conv_b, dt_bias, a_log, d_skip, norm_w, w_out)
        m = rmsnorm(h, EPS_OUT) @ w_fc
        m = jnp.square(jax.nn.relu(m)) @ w_proj
        return h + m

    def _L0_ffn_ref(x, ln1_g, ln1_b, ln2_g, ln2_b, mha_wq, mha_bq, mha_wk, mha_bk, mha_wv, mha_bv, mha_wo, mha_bo, mha_rw, mha_rb, ffn_rw, ffn_rb, fw1, fw2):
        import jax, jax.numpy as jnp
        import numpy as np
        B, S, D, H, M, E, K = (4, 128, 128, 16, 2, 8, 2)
        KD = D // H
        F = 2 * D
        EPS = 1e-06

        def _ln(x, g, b):
            m = jnp.mean(x, axis=-1, keepdims=True)
            v = jnp.mean(jnp.square(x - m), axis=-1, keepdims=True)
            return (x - m) * jax.lax.rsqrt(v + EPS) * g + b
        n1 = _ln(x, ln1_g, ln1_b)
        mha_probs = jax.nn.softmax(jnp.mean(n1, axis=1) @ mha_rw + mha_rb, axis=-1)
        q = jnp.einsum('btd,mdhk->mbhtk', n1, mha_wq) + mha_bq[:, None, :, None, :]
        kk = jnp.einsum('btd,mdhk->mbhtk', n1, mha_wk) + mha_bk[:, None, :, None, :]
        v = jnp.einsum('btd,mdhk->mbhtk', n1, mha_wv) + mha_bv[:, None, :, None, :]
        scores = jnp.einsum('mbhtk,mbhsk->mbhts', q, kk) / jnp.sqrt(jnp.float32(KD))
        attn = jax.nn.softmax(scores, axis=-1)
        ctx = jnp.einsum('mbhts,mbhsk->mbthk', attn, v)
        mha_out = jnp.einsum('mbthk,mhkd->mbtd', ctx, mha_wo) + mha_bo[:, None, None, :]
        x = x + jnp.einsum('mbtd,bm->btd', mha_out, mha_probs)
        n2 = _ln(x, ln2_g, ln2_b)
        ffn_probs = jax.nn.softmax(jnp.mean(n2, axis=1) @ ffn_rw + ffn_rb, axis=-1)
        topk_p, topk_i = jax.lax.top_k(ffn_probs, K)
        topk_p = topk_p / jnp.sum(topk_p, axis=-1, keepdims=True)
        sw1 = fw1[topk_i]
        sw2 = fw2[topk_i]
        h = jax.nn.gelu(jnp.einsum('btd,bkdf->bktf', n2, sw1), approximate=False)
        eo = jnp.einsum('bktf,bkfd->bktd', h, sw2)
        return x + jnp.einsum('bktd,bk->btd', eo, topk_p)
    x = L0_attn_x
    x = _layernorm(x + _L0_attn_ref(x, L0_attn_w_in, L0_attn_conv_w, L0_attn_conv_b, L0_attn_dt_bias, L0_attn_a_log, L0_attn_d_skip, L0_attn_norm_w, L0_attn_w_out, L0_attn_w_fc, L0_attn_w_proj), axis=-1)
    x = _layernorm(x + _L0_ffn_ref(x, L0_ffn_ln1_g, L0_ffn_ln1_b, L0_ffn_ln2_g, L0_ffn_ln2_b, L0_ffn_mha_wq, L0_ffn_mha_bq, L0_ffn_mha_wk, L0_ffn_mha_bk, L0_ffn_mha_wv, L0_ffn_mha_bv, L0_ffn_mha_wo, L0_ffn_mha_bo, L0_ffn_mha_rw, L0_ffn_mha_rb, L0_ffn_ffn_rw, L0_ffn_ffn_rb, L0_ffn_fw1, L0_ffn_fw2), axis=-1)
    return x

_drawn_inputs = setup_inputs


def setup_inputs(seed=0):
    import zlib

    import numpy as np

    out = dict(_drawn_inputs(seed))
    spreads = {'L0_attn_conv_b': (0.0, 0.1),
     'L0_attn_d_skip': (1.0, 0.2),
     'L0_attn_norm_w': (1.0, 0.2),
     'L0_ffn_ln1_g': (1.0, 0.6),
     'L0_ffn_ln1_b': (0.0, 0.8),
     'L0_ffn_ln2_g': (1.0, 0.6),
     'L0_ffn_ln2_b': (0.0, 0.8),
     'L0_ffn_mha_bq': (0.0, 0.8),
     'L0_ffn_mha_bk': (0.0, 0.8),
     'L0_ffn_mha_bv': (0.0, 0.8),
     'L0_ffn_mha_bo': (0.0, 0.1),
     'L0_ffn_mha_rb': (0.0, 0.8),
     'L0_ffn_ffn_rb': (0.0, 0.54)}
    factors = {'L0_ffn_mha_wq': 8.0,
     'L0_ffn_mha_wk': 8.0,
     'L0_ffn_mha_wv': 8.0,
     'L0_ffn_mha_wo': 5.411,
     'L0_ffn_mha_rw': 8.0,
     'L0_ffn_ffn_rw': 6.024,
     'L0_ffn_fw1': 4.239,
     'L0_ffn_fw2': 4.193}
    for name, (base, spread) in spreads.items():
        noise = np.random.default_rng([zlib.crc32(name.encode()), seed]).standard_normal(out[name].shape)
        drawn = base * np.exp(spread * noise) if base else spread * noise
        out[name] = jnp.asarray(drawn.astype(out[name].dtype))
    for name, factor in factors.items():
        out[name] = (out[name] * factor).astype(out[name].dtype)
    return out
```

```python
import concourse.bass as bass
from concourse import mybir
from contextlib import ExitStack

FP32 = mybir.dt.float32
BF16 = mybir.dt.bfloat16
ALU = mybir.AluOpType
ACT = mybir.ActivationFunctionType
AX = mybir.AxisListType

P = 128
B, L, D = 8, 512, 128
TT = L // P
NH, HD = 4, 64
DI = NH * HD
CB = 4
KC = 4
FF = 4
EPS_RMS, EPS_GATE, EPS_LN, EPS_LN2 = 1.1920929e-07, 1e-05, 1e-05, 1e-06


class Count:

    def __init__(self, n, per):
        self.base, self.per, self.n = n * per + 1, per, 0

    def up(self):
        self.n += 1
        return 1

    def now(self):
        return self.base + self.n

    def end(self):
        assert self.n == self.per, (self.n, self.per)


def in_register(engine, count):
    return count if isinstance(count, int) else engine.to_reg(count)


def spread(ap, n):
    return ap.unsqueeze(len(ap.shape)).to_broadcast(list(ap.shape) + [n])


def build_mamba(nc, ctx, T, dram):
    def sb(name, shape, dt=FP32):
        return ctx.enter_context(nc.sbuf_tensor(name, shape, dt))

    def sem(name):
        return ctx.enter_context(nc.semaphore(name))

    X, X1, bank = T["X"], T["X1"], T["bank"]
    ident, tri, above, ones = T["ident"], T["tri"], T["above"], T["ones"]

    w_in = sb("w_in", [P, 2 * DI + 2 * P + NH])
    conv_w = sb("conv_w", [P, CB, KC])
    conv_b = sb("conv_b", [P, CB])
    dtb = sb("dtb", [P, NH]); neg_a = sb("neg_a", [P, NH]); dskip = sb("dskip", [P, NH])
    norm_w = sb("norm_w", [P, 2]); w_out = sb("w_out", [P, 2, D])
    w_fc = sb("w_fc", [P, FF * P]); w_proj = sb("w_proj", [P, FF, D])

    sq = sb("sq", [P, TT, D]); xn = sb("xn", [P, TT, D]); ms = sb("ms", [P, TT]); rstd = sb("rstd", [P, TT])
    xnT = sb("xnT", [P, L])
    conv = sb("conv", [P, CB, L]); xbcT = sb("xbcT", [P, CB, L])
    sz = sb("sz", [P, TT, DI])
    dtv = sb("dtv", [P, TT, NH]); dta = sb("dta", [P, TT, NH]); dte = sb("dte", [P, TT, NH])
    dt = sb("dt", [P, TT, NH]); a = sb("a", [P, TT, NH]); dec = sb("dec", [P, 2, TT, NH])
    aut = sb("aut", [P, 2, NH, P]); Lm = sb("Lm", [P, 2, NH, P]); Gm = sb("Gm", [P, 2, P]); M = sb("M", [P, 2, NH, P])
    xB = sb("xB", [P, 2, 3, P]); u = sb("u", [P, 2, DI]); du = sb("du", [P, 2, DI]); xd = sb("xd", [P, 2, DI])
    S = sb("S", [P, DI]); Sd = sb("Sd", [P, DI])
    yo = sb("yo", [P, DI]); yd = sb("yd", [P, DI]); ya = sb("ya", [P, DI]); g = sb("g", [P, TT, DI])
    gsq = sb("gsq", [P, DI]); gss = sb("gss", [P, TT]); gms = sb("gms", [P, TT]); grs = sb("grs", [P, TT])
    gT = sb("gT", [P, 2, 2, P]); h = sb("h", [P, TT, D])
    hms = sb("hms", [P, TT]); hrs = sb("hrs", [P, TT]); hnT = sb("hnT", [P, L])
    rl = sb("rl", [P, FF, L]); mT = sb("mT", [P, FF, L])
    r1 = sb("r1", [P, TT, D]); bst = sb("bst", [P, TT, 6]); mean = sb("mean", [P, TT]); dmean = sb("dmean", [P, TT]); vs = sb("vs", [P, TT]); lrs = sb("lrs", [P, TT])
    mhalf = T["mhalf"]

    names = ["weights", "prep", "sq_a", "ms_a", "rs_a", "xn_a", "pe_xnT", "act_xnT", "pe_conv", "act_tap", "conv_done",
             "silu_done", "pe_z", "z_read", "dt_read", "dve_dt", "act_dt", "a_ready", "pe_cum", "dec_ready", "aut_ready",
             "pe_seg", "L_ready", "pe_G", "Gm_ready", "M_ready", "pe_tok", "xB_ready", "u_ready", "pe_y", "y_read",
             "pe_st", "S_ready", "g_ready", "gss_ready", "gms_ready", "grs_ready", "pe_gT", "gT_ready", "pe_out", "h_ready",
             "sq_h", "ms_h", "rs_h", "hn_ready", "pe_hnT", "hnT_ready", "pe_fc", "relu_ready", "m_ready",
             "pe_proj", "var_ready", "lrs_ready", "x1_done", "m_dve", "m_pool", "m_prep"]
    static = ("weights", "prep", "m_prep")
    once = {n: sem("s_" + n) for n in static}
    s = {n: ctx.enter_context(nc.semaphore("s_" + n)) for n in [n for n in names if n not in static]}
    met = (T["masks"], 8)

    DVE_STEPS = 44

    with nc.Block() as block:
        @block.gpsimd
        def _(pool):
            for started in s.values():
                pool.sem_inc(started, 1)

    with nc.Block() as block:
        @block.sync
        def _(sp):
            loads = [
                (w_in[:, 0:DI], dram["w_in"][:, 0:DI]),
                (w_in[:, DI:DI + NH], dram["w_in"][:, 2 * DI + 2 * P:]),
                (w_in[:, DI + NH:], dram["w_in"][:, DI:2 * DI + 2 * P]),
                (conv_w[:, :, :], dram["conv_w"].rearrange("(j p) k -> p j k", p=P)),
                (conv_b[:, :], dram["conv_b"].rearrange("(j p) -> p j", p=P)),
                (dtb[:, :], dram["dt_bias"].partition_broadcast(P)),
                (neg_a[:, :], dram["a_log"].partition_broadcast(P)),
                (dskip[:, :], dram["d_skip"].partition_broadcast(P)),
                (norm_w[:, :], dram["norm_w"].rearrange("(j p) -> p j", p=P)),
                (w_out[:, :, :], dram["w_out"].rearrange("(j p) d -> p j d", p=P)),
                (w_fc[:, :], dram["w_fc"]),
                (w_proj[:, :, :], dram["w_proj"].rearrange("(j p) d -> p j d", p=P)),
            ]
            with nc.allow_non_contiguous_dma(reason="per-feature columns of a few bytes"):
              for dst, src in loads:
                  sp.dma_start(dst, src).then_inc(once["weights"], 16)
            T["mamba_loads"] = len(loads)

        @block.gpsimd
        def _(pool):
            def batch(b):
                pool.wait_ge(s["ms_a"], b + 1 + 1)
                pool.tensor_tensor(rstd[:, :], ms[:, :], mhalf[:, 0:TT], ALU.pow).then_inc(s["rs_a"], 1)
                for c in range(TT):
                    if c == 0:
                        pool.wait_ge(s["a_ready"], b + 1 + 1)
                    if c >= 2:
                        pool.wait_ge(s["pe_seg"], b * TT + c - 1 + 1)
                    else:
                        pool.wait_ge(s["pe_seg"], b * TT + 1)
                    pool.tensor_tensor(aut[:, c % 2], spread(a[:, c, :], P),
                                       tri[:, :].unsqueeze(1).to_broadcast([P, NH, P]), ALU.mult).then_inc(s["aut_ready"], 1)
                    pool.wait_ge(s["xB_ready"], b * TT + c + 1 + 1)
                    pool.wait_ge(s["pe_y"], (b * TT + (c - 1 if c >= 2 else 0)) + 1)
                    pool.wait_ge(s["pe_st"], (b * TT + (c - 1 if c >= 2 else 0)) + 1)
                    pool.wait_ge(s["y_read"], (b * TT + (c - 1 if c >= 2 else 0)) + 1)
                    xt = xB[:, c % 2, 0:2, :].rearrange("p a (h e) -> p (a h) e", e=HD)
                    pool.tensor_tensor(u[:, c % 2].rearrange("p (h e) -> p h e", e=HD), xt, spread(dt[:, c, :], HD), ALU.mult).then_inc(s["u_ready"], 1)
                    pool.tensor_tensor(xd[:, c % 2].rearrange("p (h e) -> p h e", e=HD), xt, spread(dskip[:, :], HD), ALU.mult).then_inc(s["u_ready"], 1)
                    pool.wait_ge(s["L_ready"], b * TT + c + 1 + 1)
                    pool.wait_ge(s["u_ready"], (b * TT + c) * 3 + 2 + 1)
                    pool.tensor_tensor(du[:, c % 2].rearrange("p (h e) -> p h e", e=HD), u[:, c % 2].rearrange("p (h e) -> p h e", e=HD),
                                       Lm[:, c % 2, :, P - 1:P].to_broadcast([P, NH, HD]), ALU.mult).then_inc(s["u_ready"], 1)
                    pool.wait_ge(s["Gm_ready"], b * TT + c + 1 + 1)
                    pool.tensor_tensor(M[:, c % 2], Lm[:, c % 2], Gm[:, c % 2, :].unsqueeze(1).to_broadcast([P, NH, P]), ALU.mult).then_inc(s["M_ready"], 1)
                pool.wait_ge(s["gms_ready"], b + 1 + 1)
                pool.tensor_tensor(grs[:, :], gms[:, :], mhalf[:, 0:TT], ALU.pow).then_inc(s["grs_ready"], 1)
                pool.wait_ge(s["ms_h"], b + 1 + 1)
                pool.tensor_tensor(hrs[:, :], hms[:, :], mhalf[:, 0:TT], ALU.pow).then_inc(s["rs_h"], 1)
                pool.wait_ge(s["var_ready"], b + 1 + 1)
                pool.tensor_tensor(lrs[:, :], vs[:, :], mhalf[:, 0:TT], ALU.pow).then_inc(s["lrs_ready"], 1)
            with pool.Fori(0, B) as b:
                batch(b)

        @block.scalar
        def _(act):
            act.wait_ge(once["weights"], 16 * 12)
            act.activation(neg_a[:, :], neg_a[:, :], ACT.Exp).then_inc(once["m_prep"], 1)

            def batch(b):
                act.wait_ge(s["sq_h"], b + 1)
                act.wait_ge(s["ms_h"], b + 1)
                act.activation(sq[:, :, :], X[:, bass.ds(b * TT, TT), :], ACT.Square).then_inc(s["sq_a"], 1)
                act.wait_ge(s["pe_xnT"], b + 1 + 1)
                act.wait_ge(s["pe_z"], b * TT + 1)
                act.activation(xnT[:, :], bank[0][:, :], ACT.Copy).then_inc(s["act_xnT"], 1)
                for j in range(CB):
                    act.wait_ge(s["pe_conv"], b * CB + j + 1 + 1)
                    act.wait_ge(s["silu_done"], b * CB + 1)
                    act.activation(conv[:, j, :], bank[1 + j][:, :], ACT.Identity, scale=conv_w[:, j, KC - 1:KC],
                                   bias=conv_b[:, j:j + 1]).then_inc(s["act_tap"], 1)
                for t in range(TT):
                    act.wait_ge(s["pe_z"], b * TT + t + 1 + 1)
                    act.wait_ge(s["g_ready"], b * TT + 1)
                    act.activation(sz[:, t, :], bank[5 + t % 2][:, 0:DI], ACT.Silu).then_inc(s["z_read"], 1)
                act.wait_ge(s["pe_y"], b * TT + 1)
                for j in range(CB):
                    act.wait_ge(s["conv_done"], b * CB + j + 1 + 1)
                    act.activation(xbcT[:, j, :], conv[:, j, :], ACT.Silu).then_inc(s["silu_done"], 1)
                act.wait_ge(s["dve_dt"], b + 1 + 1)
                act.activation(dte[:, :, :], dta[:, :, :], ACT.Exp, scale=-1.0).then_inc(s["act_dt"], 1)
                act.wait_ge(s["act_dt"], 2 * b + 1 + 1)
                act.activation(dta[:, :, :], dte[:, :, :], ACT.Ln, bias=1.0).then_inc(s["act_dt"], 1)
                act.wait_ge(s["pe_cum"], b + 1 + 1)
                act.wait_ge(s["y_read"], b * TT + 1)
                act.wait_ge(s["S_ready"], b * TT + 1)
                act.activation(dec[:, :, :, :], bank[2][:, 0:2 * TT * NH].rearrange("p (a t h) -> p a t h", a=2, h=NH), ACT.Exp).then_inc(s["dec_ready"], 1)
                for c in range(TT):
                    act.wait_ge(s["pe_tok"], b * TT + c + 1 + 1)
                    act.wait_ge(s["u_ready"], (b * TT + max(c - 1, 0)) * 3 + 1)
                    act.wait_ge(s["pe_st"], b * TT + max(c - 1, 0) + 1)
                    act.activation(xB[:, c % 2, :, :], bank[5][:, 0:3 * P].rearrange("p (a q) -> p a q", a=3), ACT.Copy).then_inc(s["xB_ready"], 1)
                    act.wait_ge(s["pe_seg"], b * TT + c + 1 + 1)
                    act.wait_ge(s["M_ready"], b * TT + max(c - 1, 0) + 1)
                    act.activation(Lm[:, c % 2], bank[7][:, :].rearrange("p (h q) -> p h q", h=NH), ACT.Exp).then_inc(s["L_ready"], 1)
                    act.wait_ge(s["g_ready"], b * TT + c + 1 + 1)
                    act.wait_ge(s["gss_ready"], b * TT + c + 1)
                    act.activation(gsq[:, :], g[:, c, :], ACT.Square, accum_out=gss[:, c:c + 1]).then_inc(s["gss_ready"], 1)
                for c in range(TT):
                    act.wait_ge(s["pe_gT"], b * TT + c + 1 + 1)
                    act.wait_ge(s["pe_out"], b * TT + max(c - 1, 0) + 1)
                    act.activation(gT[:, c % 2], bank[3][:, 0:DI].rearrange("p (a q) -> p a q", a=2), ACT.Copy).then_inc(s["gT_ready"], 1)
                act.wait_ge(s["h_ready"], b * TT + TT + 1)
                act.wait_ge(s["sq_a"], b + 1 + 1)
                act.wait_ge(s["xn_a"], b + 1 + 1)
                act.activation(sq[:, :, :], h[:, :, :], ACT.Square).then_inc(s["sq_h"], 1)
                act.wait_ge(s["pe_hnT"], b + 1 + 1)
                act.wait_ge(s["pe_fc"], b * FF + 1)
                act.activation(hnT[:, :], bank[0][:, :], ACT.Copy).then_inc(s["hnT_ready"], 1)
                for j in range(FF):
                    act.wait_ge(s["pe_fc"], b * FF + j + 1 + 1)
                    act.wait_ge(s["m_ready"], b * FF + 1)
                    act.activation(rl[:, j, :], bank[1 + j][:, :], ACT.Relu).then_inc(s["relu_ready"], 1)
            with act.Fori(0, B) as b:
                batch(b)

        @block.vector
        def _(dve):
            dve.wait_ge(once["weights"], 16 * 12)
            dve.wait_ge(once["m_prep"], 1)
            dve.tensor_scalar(neg_a[:, :], neg_a[:, :], -1.0, None, ALU.mult).then_inc(once["prep"], 1)
            for j in range(2):
                dve.tensor_scalar(w_out[:, j, :], w_out[:, j, :], norm_w[:, j:j + 1], None, ALU.mult).then_inc(once["prep"], 1)

            def batch(b):
                c_ = Count(b, DVE_STEPS)
                dve.wait_ge(s["sq_a"], b + 1 + 1)
                dve.tensor_reduce(ms[:, :], sq[:, :, :], AX.X, ALU.add).then_inc(s["m_dve"], c_.up())
                dve.wait_ge(s["m_dve"], c_.now())
                dve.tensor_scalar(ms[:, :], ms[:, :], 1.0 / D, EPS_RMS, ALU.mult, ALU.add).then_inc(s["ms_a"], 1)
                dve.wait_ge(s["rs_a"], b + 1 + 1)
                dve.wait_ge(s["pe_hnT"], b + 1)
                dve.tensor_tensor(xn[:, :, :], X[:, bass.ds(b * TT, TT), :], spread(rstd[:, :], D), ALU.mult).then_inc(s["xn_a"], 1)
                for j in range(CB):
                    for k in range(1, KC):
                        if k == 1:
                            dve.wait_ge(s["act_tap"], b * CB + j + 1 + 1)
                        else:
                            dve.wait_ge(s["m_dve"], c_.now())
                        i = dve.scalar_tensor_tensor(conv[:, j, k:L], bank[1 + j][:, 0:L - k], conv_w[:, j, KC - 1 - k:KC - k],
                                                     conv[:, j, k:L], ALU.mult, ALU.add)
                        if k == KC - 1:
                            i.then_inc(s["conv_done"], 1)
                        else:
                            i.then_inc(s["m_dve"], c_.up())
                for t in range(TT):
                    dve.wait_ge(s["z_read"], b * TT + t + 1 + 1)
                    if t == 0:
                        dve.wait_ge(s["a_ready"], b + 1)
                    dve.tensor_tensor(dtv[:, t, :], bank[5 + t % 2][:, DI:DI + NH], dtb[:, :], ALU.add).then_inc(s["m_dve"], c_.up())
                    dve.wait_ge(s["m_dve"], c_.now())
                    dve.scalar_tensor_tensor(dta[:, t, :], dtv[:, t, :], -1.0, dtv[:, t, :], ALU.mult, ALU.max).then_inc(s["m_dve"], c_.up())
                dve.wait_ge(s["m_dve"], c_.now())
                dve.tensor_scalar(dtv[:, :, :], dtv[:, :, :], 0.0, None, ALU.max).then_inc(s["dve_dt"], 1)
                dve.wait_ge(s["act_dt"], 2 * b + 2 + 1)
                dve.wait_ge(s["dve_dt"], b + 1 + 1)
                dve.tensor_tensor(dt[:, :, :], dtv[:, :, :], dta[:, :, :], ALU.add).then_inc(s["m_dve"], c_.up())
                dve.wait_ge(s["m_dve"], c_.now())
                dve.wait_ge(once["prep"], 3)
                dve.tensor_tensor(a[:, :, :], dt[:, :, :], neg_a[:, :].unsqueeze(1).to_broadcast([P, TT, NH]), ALU.mult).then_inc(s["a_ready"], 1)
                dve.wait_ge(s["pe_st"], b * TT + 1)
                dve.memset(S[:, :], 0.0).then_inc(s["m_dve"], c_.up())
                for c in range(TT):
                    def per_head(ap):
                        return ap.rearrange("p (h e) -> p h e", e=HD)
                    dve.wait_ge(s["pe_G"], b * TT + c + 1 + 1)
                    dve.wait_ge(s["M_ready"], b * TT + max(c - 1, 0) + 1)
                    dve.tensor_tensor(Gm[:, c % 2, :], bank[0][:, 0:P], tri[:, :], ALU.mult).then_inc(s["Gm_ready"], 1)
                    dve.wait_ge(s["pe_y"], b * TT + c + 1 + 1)
                    dve.wait_ge(s["dec_ready"], b + 1 + 1)
                    dve.tensor_tensor(per_head(yo[:, :]), per_head(bank[6][:, DI:2 * DI]), spread(dec[:, 0, c, :], HD), ALU.mult).then_inc(s["m_dve"], c_.up())
                    dve.wait_ge(s["u_ready"], (b * TT + c) * 3 + 2 + 1)
                    dve.tensor_tensor(yd[:, :], bank[6][:, 0:DI], xd[:, c % 2, :], ALU.add).then_inc(s["y_read"], 1)
                    dve.wait_ge(s["y_read"], b * TT + c + 1 + 1)
                    dve.wait_ge(s["m_dve"], c_.now())
                    dve.tensor_tensor(ya[:, :], yd[:, :], yo[:, :], ALU.add).then_inc(s["m_dve"], c_.up())
                    dve.wait_ge(s["S_ready"], b * TT + c + 1)
                    dve.tensor_tensor(per_head(Sd[:, :]), per_head(S[:, :]), spread(dec[:, 1, c, :], HD), ALU.mult).then_inc(s["m_dve"], c_.up())
                    dve.wait_ge(s["m_dve"], c_.now())
                    dve.wait_ge(s["pe_st"], b * TT + c + 1 + 1)
                    dve.tensor_tensor(S[:, :], bank[1][:, 0:DI], Sd[:, :], ALU.add).then_inc(s["S_ready"], 1)
                    dve.wait_ge(s["z_read"], b * TT + c + 1 + 1)
                    dve.wait_ge(s["pe_gT"], b * TT + 1)
                    dve.tensor_tensor(g[:, c, :], ya[:, :], sz[:, c, :], ALU.mult).then_inc(s["g_ready"], 1)
                    dve.wait_ge(s["g_ready"], b * TT + c + 1 + 1)
                dve.wait_ge(s["gss_ready"], b * TT + TT + 1)
                dve.tensor_scalar(gms[:, :], gss[:, :], 1.0 / DI, EPS_GATE, ALU.mult, ALU.add).then_inc(s["gms_ready"], 1)
                dve.wait_ge(s["grs_ready"], b + 1 + 1)
                for c in range(TT):
                    dve.wait_ge(s["pe_out"], b * TT + c + 1 + 1)
                    dve.scalar_tensor_tensor(h[:, c, :], bank[4][:, 0:D], grs[:, c:c + 1], X[:, bass.ds(b * TT + c, 1), :].rearrange("p o d -> p (o d)"), ALU.mult, ALU.add).then_inc(s["h_ready"], 1)
                dve.wait_ge(s["sq_h"], b + 1 + 1)
                dve.tensor_reduce(hms[:, :], sq[:, :, :], AX.X, ALU.add).then_inc(s["m_dve"], c_.up())
                dve.wait_ge(s["m_dve"], c_.now())
                dve.tensor_scalar(hms[:, :], hms[:, :], 1.0 / D, EPS_RMS, ALU.mult, ALU.add).then_inc(s["ms_h"], 1)
                dve.wait_ge(s["rs_h"], b + 1 + 1)
                dve.wait_ge(s["h_ready"], b * TT + TT + 1)
                dve.wait_ge(s["pe_xnT"], b + 1 + 1)
                dve.tensor_tensor(xn[:, :, :], h[:, :, :], spread(hrs[:, :], D), ALU.mult).then_inc(s["hn_ready"], 1)
                for j in range(FF):
                    dve.wait_ge(s["relu_ready"], b * FF + j + 1 + 1)
                    dve.wait_ge(s["pe_proj"], b + 1)
                    dve.scalar_tensor_tensor(mT[:, j, :], bank[1 + j][:, :], 0.0, rl[:, j, :], ALU.max, ALU.mult).then_inc(s["m_ready"], 1)
                dve.wait_ge(s["pe_proj"], b + 1 + 1)
                dve.tensor_tensor(r1[:, :, :], bank[5][:, :].rearrange("p (t d) -> p t d", t=TT), h[:, :, :], ALU.add).then_inc(s["m_dve"], c_.up())
                dve.wait_ge(s["m_dve"], c_.now())
                dve.tensor_tensor(r1[:, :, :], r1[:, :, :], X[:, bass.ds(b * TT, TT), :], ALU.add).then_inc(s["m_dve"], c_.up())
                dve.wait_ge(s["m_dve"], c_.now())
                for t in range(TT):
                    dve.bn_stats(bst[:, t, :], r1[:, t, :]).then_inc(s["m_dve"], c_.up())
                dve.wait_ge(s["m_dve"], c_.now())
                dve.tensor_tensor(mean[:, :], bst[:, :, 1], bst[:, :, 4], ALU.add).then_inc(s["m_dve"], c_.up())
                dve.tensor_tensor(dmean[:, :], bst[:, :, 1], bst[:, :, 4], ALU.subtract).then_inc(s["m_dve"], c_.up())
                dve.tensor_tensor(vs[:, :], bst[:, :, 2], bst[:, :, 5], ALU.add).then_inc(s["m_dve"], c_.up())
                dve.wait_ge(s["m_dve"], c_.now())
                dve.tensor_scalar(mean[:, :], mean[:, :], 0.5, None, ALU.mult).then_inc(s["m_dve"], c_.up())
                dve.tensor_tensor(dmean[:, :], dmean[:, :], dmean[:, :], ALU.mult).then_inc(s["m_dve"], c_.up())
                dve.tensor_scalar(vs[:, :], vs[:, :], 1.0 / D, EPS_LN, ALU.mult, ALU.add).then_inc(s["m_dve"], c_.up())
                dve.wait_ge(s["m_dve"], c_.now())
                dve.scalar_tensor_tensor(vs[:, :], dmean[:, :], 0.25, vs[:, :], ALU.mult, ALU.add).then_inc(s["var_ready"], 1)
                dve.wait_ge(s["lrs_ready"], b + 1 + 1)
                for t in range(TT):
                    dve.tensor_scalar(X1[:, bass.ds(b * TT + t, 1), :].rearrange("p o d -> p (o d)"), r1[:, t, :], mean[:, t:t + 1], lrs[:, t:t + 1], ALU.subtract, ALU.mult).then_inc(s["x1_done"], 1)
                dve.wait_ge(s["x1_done"], b * TT + TT + 1)
                c_.end()
            with dve.Fori(0, B) as b:
                batch(b)

        @block.tensor
        def _(pe):
            pe.wait_ge(once["weights"], 16 * 12)
            pe.wait_ge(once["prep"], 3)

            def mm(out, lhsT, rhs, first=True, last=True):
                return pe.matmul(out, lhsT, rhs, start=first, stop=last)

            def batch(b):
                pe.wait_ge(s["xn_a"], b + 1 + 1)
                pe.wait_ge(s["hnT_ready"], b + 1)
                for t in range(TT):
                    i = pe.transpose(bank[0][:, t * P:(t + 1) * P], xn[:, t, :], ident[:, :])
                i.then_inc(s["pe_xnT"], 1)
                pe.wait_ge(s["act_xnT"], b + 1 + 1)
                pe.wait_ge(s["m_ready"], b * FF + 1)
                pe.wait_ge(s["x1_done"], b * TT + 1)
                for j in range(CB):
                    mm(bank[1 + j][:, :], w_in[:, DI + NH + j * P:DI + NH + (j + 1) * P], xnT[:, :]).then_inc(s["pe_conv"], 1)
                for t in range(TT):
                    if t >= 2:
                        pe.wait_ge(s["z_read"], b * TT + t - 1 + 1)
                        pe.wait_ge(s["m_dve"], b * DVE_STEPS + 6 + 2 * t + 1)
                    mm(bank[5 + t % 2][:, 0:DI + NH], xnT[:, t * P:(t + 1) * P], w_in[:, 0:DI + NH]).then_inc(s["pe_z"], 1)
                pe.wait_ge(s["a_ready"], b + 1 + 1)
                pe.wait_ge(s["conv_done"], b * CB + CB + 1)
                n = TT * NH
                mm(bank[2][:, 0:n], tri[:, :], a[:, :, :].rearrange("p t h -> p (t h)"))
                mm(bank[2][:, n:2 * n], ones[:, :], a[:, :, :].rearrange("p t h -> p (t h)")).then_inc(s["pe_cum"], 1)
                pe.wait_ge(s["z_read"], b * TT + TT + 1)
                pe.wait_ge(s["dve_dt"], b + 1 + 1)
                pe.wait_ge(s["silu_done"], b * CB + CB + 1)
                for c in range(TT):
                    tok = slice(c * P, (c + 1) * P)
                    if c:
                        pe.wait_ge(s["xB_ready"], b * TT + c + 1)
                    for j in range(3):
                        i = pe.transpose(bank[5][:, j * P:(j + 1) * P], xbcT[:, j, tok], ident[:, :])
                    i.then_inc(s["pe_tok"], 1)
                    if c:
                        pe.wait_ge(s["Gm_ready"], b * TT + c + 1)
                    mm(bank[0][:, 0:P], xbcT[:, 2, tok], xbcT[:, 3, tok]).then_inc(s["pe_G"], 1)
                    pe.wait_ge(s["aut_ready"], b * TT + c + 1 + 1)
                    pe.wait_ge(s["L_ready"], b * TT + c + 1)
                    mm(bank[7][:, :], above[:, :], aut[:, c % 2].rearrange("p h q -> p (h q)")).then_inc(s["pe_seg"], 1)
                    pe.wait_ge(s["M_ready"], b * TT + c + 1 + 1)
                    pe.wait_ge(s["u_ready"], (b * TT + c + 1) * 3 + 1)
                    if c:
                        pe.wait_ge(s["S_ready"], b * TT + c + 1)
                        pe.wait_ge(s["y_read"], b * TT + c + 1)
                    else:
                        pe.wait_ge(s["m_dve"], b * DVE_STEPS + 19 + 1)
                    for hh in range(NH):
                        mm(bank[6][:, hh * HD:(hh + 1) * HD], M[:, c % 2, hh, :], u[:, c % 2, hh * HD:(hh + 1) * HD])
                    mm(bank[6][:, DI:2 * DI], xbcT[:, 3, tok], S[:, :]).then_inc(s["pe_y"], 1)
                    mm(bank[1][:, 0:DI], xB[:, c % 2, 2, :], du[:, c % 2, :]).then_inc(s["pe_st"], 1)
                for c in range(TT):
                    pe.wait_ge(s["g_ready"], b * TT + c + 1 + 1)
                    pe.wait_ge(s["gT_ready"], b * TT + c + 1)
                    for j in range(2):
                        i = pe.transpose(bank[3][:, j * P:(j + 1) * P], g[:, c, j * P:(j + 1) * P], ident[:, :])
                    i.then_inc(s["pe_gT"], 1)
                    pe.wait_ge(s["gT_ready"], b * TT + c + 1 + 1)
                    pe.wait_ge(s["h_ready"], b * TT + c + 1)
                    for j in range(2):
                        i = mm(bank[4][:, 0:D], gT[:, c % 2, j, :], w_out[:, j, :], j == 0, j == 1)
                    i.then_inc(s["pe_out"], 1)
                pe.wait_ge(s["hn_ready"], b + 1 + 1)
                for t in range(TT):
                    i = pe.transpose(bank[0][:, t * P:(t + 1) * P], xn[:, t, :], ident[:, :])
                i.then_inc(s["pe_hnT"], 1)
                pe.wait_ge(s["hnT_ready"], b + 1 + 1)
                for j in range(FF):
                    mm(bank[1 + j][:, :], w_fc[:, j * P:(j + 1) * P], hnT[:, :]).then_inc(s["pe_fc"], 1)
                pe.wait_ge(s["m_ready"], (b + 1) * FF + 1)
                for t in range(TT):
                    for j in range(FF):
                        i = mm(bank[5][:, t * P:(t + 1) * P], mT[:, j, t * P:(t + 1) * P], w_proj[:, j, :], j == 0, j == FF - 1)
                i.then_inc(s["pe_proj"], 1)
            with pe.Fori(0, B) as b:
                batch(b)


MX = 2
H, KD = 16, 8
GH = 4
NG = MX * H // GH
GM = NG // MX
SL = 4
PAIRS = [(0, 0), (1, 0), (2, 0), (0, 1), (1, 1), (0, 2)]
QROWS = len(PAIRS) * KD
MROWS = 3
RING, PRING = 3, 8
UNITS = NG * SL * GH
SCALE = float(KD) ** -0.5

SHARED = [(g, 1, "neg") for g in range(NG)] + [(g, 2, "ctx") for g in range(NG)] + [
    (0, 3, "ctxT1"), (1, 0, "wo"), (1, 3, "xT"), (2, 0, "q0"), (2, 3, "k0"), (3, 0, "v0"), (3, 3, "v1"),
    (4, 0, "v2"), (4, 3, "ctxT0"), (5, 0, "v3"), (5, 3, "q1"), (6, 0, "k1"), (6, 3, "logits")]
SHARED = sorted(SHARED)
PREP = ["xT", "q0", "k0", "v0", "v1", "v2", "v3", "q1", "k1", "logits"]
BEFORE = [(0, 2, "ctx"), (0, 3, "ctxT1"), (1, 0, "wo")]


class Phase:

    def __init__(self, kind, b):
        self.kind, self.b = kind, b
        self.first, self.last = kind == "first", kind == "last"
        prologue = [(0, 0, n) for n in PREP] + [(0, 1, "neg")]
        if kind == "prologue":
            self.uses, self.base = prologue, 0
        elif kind == "epilogue":
            before = Phase("last", b - 1)
            self.uses, self.base = BEFORE, before.base + len(before.uses)
        else:
            self.uses = [x for x in SHARED
                         if not (self.first and x in BEFORE)
                         and not (self.last and (x[2] in PREP or (x[2] == "neg" and x[0] >= NG - 1)))]
            self.base = len(prologue) + (0 if self.first else b * len(SHARED) - len(BEFORE))

    def has(self, use):
        return use in self.uses

    def number(self, use):
        return self.base + self.uses.index(use) + 1


def build_attention(nc, ctx, T, dram):
    def sb(name, shape, dt=FP32):
        return ctx.enter_context(nc.sbuf_tensor(name, shape, dt))

    X, X1, bank, ident = T["X"], T["X1"], T["bank"], T["ident"]
    MAXB, EXPB, PVB, SH = (0, 1), (2, 3, 4), (5, 6), bank[7]
    shb = SH[:, :].bitcast(BF16)

    identb = sb("identb", [P, P], BF16)
    Q = [sb(f"Q{m}", [QROWS + MROWS, H, L], BF16) for m in range(MX)]
    K = [sb(f"K{m}", [QROWS + MROWS, H, L], BF16) for m in range(MX)]
    parts = [[sb(f"parts{m}{i}", [P, 3, L], BF16) for i in range(2)] for m in range(MX)]
    full = [sb(f"full{i}", [P, L]) for i in range(2)]; rest = sb("rest", [P, L])
    V = sb("V", [P, SL, MX * H, 32]); vtmp = sb("vtmp", [P, SL, MX * H, KD])
    E = sb("E", [P, PRING, L])
    top = sb("top", [P, 2, GH * TT]); negr = sb("negr", [P, 2, GH * TT]); neg = sb("neg", [P, 2, 3, GH * TT], BF16)
    negT = sb("negT", [3 * GH * TT, 2, P], BF16)
    ctxu = sb("ctxu", [P, L]); rl_ = sb("rsum", [P, TT, GH]); ctxn = sb("ctxn", [P, MX, TT, H, KD]); ctxT = sb("ctxT", [P, MX, L])
    wq = sb("wq", [P, MX, H * KD]); wk = sb("wk", [P, MX, H * KD]); wv = sb("wv", [P, MX, H * KD]); wo = sb("wo", [P, MX, D]); wop = sb("wop", [P, MX, D])
    bq = sb("bq", [P, MX]); bk = sb("bk", [P, MX]); bv = sb("bv", [P, MX * H * KD]); bo = sb("bo", [P, MX, D]); bop = sb("bop", [P, D])
    raw = sb("raw", [P, 2, MX, H * KD])
    rw = sb("rw", [P, MX]); rb = sb("rb", [P, MX]); lg_ = sb("lng", [P, 2])
    n1T = sb("n1T", [P, L]); xh = sb("xh", [P, TT, D]); msum = sb("msum", [P, 1]); nmat = sb("nmat", [P, P])
    bst = sb("bst2", [P, TT, 6]); mean = sb("mean2", [P, TT]); dmean = sb("dmean2", [P, TT]); vs = sb("vs2", [P, TT]); lrs = sb("lrs2", [P, TT])
    lgt = sb("lgt", [P, MX]); lmx = sb("lmx", [P, 1]); pe_ = sb("pexp", [P, MX]); psm = sb("psm", [P, 1]); pr = sb("pr", [P, MX])
    t1 = sb("t1", [P, TT, D])

    primed = ["pe_max", "max_read", "pe_exp", "exp_done", "pv_done", "neg_ready", "negT_ready", "neg_rows", "evac", "pe_shared",
              "shared_free", "var", "lrs", "xh", "split", "stack0", "stack1", "v_filled", "nmat", "lmax", "pexp", "pr", "wop",
              "t1", "x2", "x1_sum", "c_dve_ln", "c_dve_ctx", "c_pool_neg", "c_pool_split", "c_dve_p"]
    loaded = ctx.enter_context(nc.semaphore("t_weights"))
    set_up = ctx.enter_context(nc.semaphore("t_set_up"))
    s = {n: ctx.enter_context(nc.semaphore("t_" + n)) for n in primed}
    met = (set_up, 6)

    loads = [(raw[:, 0, m, :], dram["wq"][m].rearrange("d h k -> d (h k)")) for m in range(MX)]
    loads += [(raw[:, 1, m, :], dram["wk"][m].rearrange("d h k -> d (h k)")) for m in range(MX)]
    loads += [(wv[:, m, :], dram["wv"][m].rearrange("d h k -> d (h k)")) for m in range(MX)]
    loads += [(wo[:, m, :], dram["wo"][m].rearrange("h k d -> (h k) d")) for m in range(MX)]
    for m in range(MX):
        loads += [(bq[:, m:m + 1], dram["bq"][m].rearrange("h k -> k h")), (bk[:, m:m + 1], dram["bk"][m].rearrange("h k -> k h"))]
    loads += [
              (bv[:, :], dram["bv"].rearrange("m h k -> (m h k)").partition_broadcast(P)),
              (bo[:, :, :], dram["bo"].rearrange("m d -> (m d)").partition_broadcast(P)),
              (rw[:, :], dram["rw"]), (rb[:, :], dram["rb"].partition_broadcast(P)),
              (lg_[:, 0:1], dram["ln1_g"].rearrange("(p o) -> p o", o=1)), (lg_[:, 1:2], dram["ln1_b"].rearrange("(p o) -> p o", o=1))]

    with nc.Block() as block:
        @block.sync
        def _(sp):
            with nc.allow_non_contiguous_dma(reason="per-feature columns of a few bytes"):
                for dst, src in loads:
                    if len(dst.shape) == 3:
                        src = src.rearrange("p (m d) -> p m d", m=MX)
                    sp.dma_start(dst, src).then_inc(loaded, 16)
            sp.wait_ge(loaded, 16 * len(loads))

        @block.gpsimd
        def _(pool):
            for started in s.values():
                pool.sem_inc(started, 1)
            pool.memset(V[:, :, :, :], 0.0).then_inc(set_up, 1)
            for m in range(MX):
                pool.memset(K[m][:, :, :], 1.0).then_inc(set_up, 1)
                pool.memset(Q[m][:, :, :], 0.0).then_inc(set_up, 1)
            pool.wait_ge(set_up, 1)
            pool.memset(V[:, :, :, KD:KD + 1], 1.0).then_inc(set_up, 1)
            pool.wait_ge(set_up, 6)

        @block.vector
        def _(dve):
            dve.tensor_copy(identb[:, :], ident[:, :])
            dve.wait_ge(loaded, 16 * len(loads))
            dve.tensor_scalar(bq[:, :], bq[:, :], SCALE, None, ALU.mult)
            for i, w in enumerate((wq, wk)):
                for m in range(MX):
                    dve.tensor_copy(w[:, m, :].rearrange("p (k h) -> p k h", h=H), raw[:, i, m, :].rearrange("p (h k) -> p k h", k=KD))

    LN_STEPS, CTX_STEPS, NEG_STEPS, SPLIT_STEPS, P_STEPS = 11, 1, 4, 3, 3

    def phases(engine, body):
        body(Phase("prologue", 0))
        body(Phase("first", 0))
        with engine.Fori(1, B - 1) as b:
            body(Phase("middle", b))
        body(Phase("last", B - 1))
        body(Phase("epilogue", B))

    with nc.Block() as block:
        @block.tensor
        def _(pe):
            def shared(ph, use, next_b):
                if not ph.has(use):
                    return
                what, b = use[2], ph.b
                if what == "neg":
                    count = in_register(pe, ph.number(use) - 1 + 1)
                    pe.wait_ge(*met)
                    pe.wait_ge(s["shared_free"], count)
                else:
                    pe.wait_ge(s["shared_free"], ph.number(use) - 1 + 1)
                if what == "neg":
                    n = b * NG + use[0] + 1 if ph.kind != "prologue" else 0
                    count = in_register(pe, n + 1 + 1)
                    pe.wait_ge(*met)
                    pe.wait_ge(s["neg_ready"], count)
                    par = (use[0] + 1) % 2 if ph.kind != "prologue" else 0
                    i = pe.transpose(shb[0:3 * GH * TT, 0:P], neg[:, par].rearrange("p a c -> p (a c)"), identb[:, :])
                elif what == "ctx":
                    n = b * NG + use[0]
                    pe.wait_ge(s["evac"], n + 1)
                    for t in range(TT):
                        i = pe.transpose(SH[:, t * P:(t + 1) * P], ctxu[:, t * P:(t + 1) * P], ident[:, :])
                elif what in ("ctxT0", "ctxT1"):
                    m = int(what[-1])
                    for t in range(TT):
                        i = pe.transpose(SH[:, t * P:(t + 1) * P], ctxn[:, m, t].rearrange("p h k -> p (h k)"), ident[:, :])
                elif what == "wo":
                    pe.wait_ge(s["wop"], b + 1)
                    for t in range(TT):
                        for m in range(MX):
                            i = pe.matmul(SH[:, t * P:(t + 1) * P], ctxT[:, m, t * P:(t + 1) * P], wop[:, m, :], start=m == 0, stop=m == MX - 1)
                elif what == "xT":
                    pe.wait_ge(s["xh"], next_b + 1 + 1)
                    for t in range(TT):
                        i = pe.transpose(SH[:, t * P:(t + 1) * P], xh[:, t, :], ident[:, :])
                elif what[0] in "qk":
                    w = {"q": wq, "k": wk}[what[0]]
                    i = pe.matmul(SH[:, :], w[:, int(what[1]), :], n1T[:, :], start=True, stop=True)
                elif what[0] == "v":
                    t = int(what[1])
                    i = pe.matmul(SH[:, 0:MX * H * KD], n1T[:, t * P:(t + 1) * P], wv[:, :, :].rearrange("p m c -> p (m c)"), start=True, stop=True)
                else:
                    pe.wait_ge(s["nmat"], next_b + 1 + 1)
                    i = pe.matmul(SH[:, 0:MX], nmat[:, :], rw[:, :], start=True, stop=True)
                i.then_inc(s["pe_shared"], 1)

            def max_unit(b, g, i, stacks_of):
                m, h, t = (g % NG) // GM, (g % GM) * GH + i // TT, i % TT
                u = b * UNITS + g * 16 + i
                if i == 0:
                    pe.wait_ge(s[f"stack{m}"], 16 * 2 * len(PAIRS) * (stacks_of + 1) + 1)
                pe.wait_ge(s["max_read"], (u - 1 if not (isinstance(b, int) and b == 0 and g == 0 and i == 0) else 0) + 1)
                pe.matmul(bank[MAXB[i % 2]][:, :], Q[m][0:QROWS, h, t * P:(t + 1) * P], K[m][0:QROWS, h, :], start=True, stop=True).then_inc(s["pe_max"], 1)

            def values(b, slot):
                g, st = slot // SL, slot % SL
                if st == 0:
                    pe.wait_ge(s["evac"], (b * NG + g - 1 if not (isinstance(b, int) and b * NG + g - 1 < 0) else 0) + 1)
                    if g % GM == 0:
                        pe.wait_ge(s["v_filled"], b * MX + g // GM + 1 + 1)
                pe.wait_ge(s["exp_done"], b * UNITS + (slot + 1) * GH + 1)
                for i in range(GH):
                    u = slot * GH + i
                    last = pe.matmul(bank[PVB[g % 2]][32 * i:32 * i + 32, :], V[:, st, g * GH + i, :], E[:, u % PRING, :],
                                     start=st == 0, stop=st == SL - 1)
                last.then_inc(s["pv_done"], 1)

            def body(ph):
                b = ph.b
                if ph.kind == "prologue":
                    for what in PREP:
                        shared(ph, (0, 0, what), 0)
                    for i in range(16):
                        max_unit(0, 0, i, 0)
                    shared(ph, (0, 1, "neg"), 0)
                    for i in range(16):
                        max_unit(0, 1, i, 0)
                    return
                if ph.kind == "epilogue":
                    values(b - 1, NG * SL - 1)
                    for use in BEFORE:
                        shared(ph, use, 0)
                    return
                for g in range(NG):
                    for st in range(SL):
                        for i in range(GH):
                            if not (ph.last and g + 2 >= NG):
                                max_unit(b, g + 2, st * GH + i, b + (g + 2) // NG)
                            m, u = g // GM, (g * SL + st) * GH + i
                            if st == 0 and i == 0:
                                pe.wait_ge(s["neg_rows"], 16 * (b * NG + g + 1) + 1)
                            pe.wait_ge(s["exp_done"], b * UNITS + max(u - RING + 1, 0) + 1)
                            pe.matmul(bank[EXPB[u % RING]][:, :], K[m][:, (g % GM) * GH + i, st * P:(st + 1) * P],
                                      Q[m][:, (g % GM) * GH + i, :], start=True, stop=True).then_inc(s["pe_exp"], 1)
                        slot = g * SL + st
                        if slot:
                            values(b, slot - 1)
                        elif not ph.first:
                            values(b - 1, NG * SL - 1)
                        for use in SHARED:
                            if use[:2] == (g, st):
                                shared(ph, use, b + 1)
            phases(pe, body)

        @block.scalar
        def _(act):
            def shared(ph, use, next_b):
                if not ph.has(use):
                    return
                what, b = use[2], ph.b
                if what in ("ctx", "wo", "logits") or what[0] == "v":
                    return
                act.wait_ge(s["pe_shared"], ph.number(use) + 1)
                if what == "neg":
                    n = b * NG + use[0] + 1 if ph.kind != "prologue" else 0
                    par = (use[0] + 1) % 2 if ph.kind != "prologue" else 0
                    act.wait_ge(s["neg_rows"], 16 * n + 1)
                    i = act.activation(negT[:, par, :], shb[0:3 * GH * TT, 0:P], ACT.Copy)
                elif what in ("ctxT0", "ctxT1"):
                    i = act.activation(ctxT[:, int(what[-1]), :], SH[:, :], ACT.Copy)
                elif what == "xT":
                    act.wait_ge(s["nmat"], next_b + 1)
                    i = act.activation(n1T[:, :], SH[:, :], ACT.Identity, scale=lg_[:, 0:1], bias=lg_[:, 1:2], accum_out=msum[:, :])
                else:
                    m, k = int(what[1]), what[0] == "k"
                    act.wait_ge(s["split"], next_b * 4 + max(2 * m + k - 1, 0) + 1)
                    if k:
                        i = act.activation(full[1][:, :], SH[:, :], ACT.Identity, bias=bk[:, m:m + 1])
                    else:
                        i = act.activation(full[0][:, :], SH[:, :], ACT.Identity, scale=SCALE, bias=bq[:, m:m + 1])
                i.then_inc(s["shared_free"], 1)

            def evacuate(ph, b, g):
                act.wait_ge(s["pv_done"], b * NG * SL + (g + 1) * SL + 1)
                if g < 0 or ph.kind == "epilogue":
                    act.wait_ge(s["pe_shared"], ph.base + 1)
                elif ph.has((g, 2, "ctx")):
                    act.wait_ge(s["pe_shared"], ph.number((g, 2, "ctx")) + 1)
                act.activation(ctxu[:, :], bank[PVB[g % 2]][:, :], ACT.Copy).then_inc(s["evac"], 1)

            def body(ph):
                b = ph.b
                if ph.kind == "prologue":
                    for what in PREP:
                        shared(ph, (0, 0, what), 0)
                    shared(ph, (0, 1, "neg"), 0)
                    return
                if ph.kind == "epilogue":
                    evacuate(ph, b - 1, NG - 1)
                    for use in BEFORE:
                        shared(ph, use, 0)
                    return
                for g in range(NG):
                    for st in range(SL):
                        for i in range(GH):
                            u = (g * SL + st) * GH + i
                            act.wait_ge(s["pe_exp"], b * UNITS + u + 1 + 1)
                            if i == 0:
                                act.wait_ge(s["pv_done"], (b * NG * SL + g * SL + st - 1 if not (ph.first and g * SL + st < 1) else 0) + 1)
                            act.activation(E[:, u % PRING, :], bank[EXPB[u % RING]][:, :], ACT.Exp).then_inc(s["exp_done"], 1)
                        if st == 1 and not (ph.first and g == 0):
                            evacuate(ph, b, g - 1)
                        for use in SHARED:
                            if use[:2] == (g, st):
                                shared(ph, use, b + 1)
                        if (g, st) == (2, 2):
                            act.wait_ge(s["lmax"], b + 1 + 1)
                            act.activation(pe_[:, :], lgt[:, :], ACT.Exp, bias=lmx[:, :], accum_out=psm[:, :]).then_inc(s["pexp"], 1)
            phases(act, body)

        @block.vector
        def _(dve):
            def normalize_1(n):
                c = Count(n, LN_STEPS)
                for t in range(TT):
                    dve.bn_stats(bst[:, t, :], X1[:, bass.ds(n * TT + t, 1), :].rearrange("p o d -> p (o d)")).then_inc(s["c_dve_ln"], c.up())
                dve.wait_ge(s["c_dve_ln"], c.now())
                dve.tensor_tensor(mean[:, :], bst[:, :, 1], bst[:, :, 4], ALU.add).then_inc(s["c_dve_ln"], c.up())
                dve.tensor_tensor(dmean[:, :], bst[:, :, 1], bst[:, :, 4], ALU.subtract).then_inc(s["c_dve_ln"], c.up())
                dve.tensor_tensor(vs[:, :], bst[:, :, 2], bst[:, :, 5], ALU.add).then_inc(s["c_dve_ln"], c.up())
                dve.wait_ge(s["c_dve_ln"], c.now())
                dve.tensor_scalar(mean[:, :], mean[:, :], 0.5, None, ALU.mult).then_inc(s["c_dve_ln"], c.up())
                dve.tensor_tensor(dmean[:, :], dmean[:, :], dmean[:, :], ALU.mult).then_inc(s["c_dve_ln"], c.up())
                dve.tensor_scalar(vs[:, :], vs[:, :], 1.0 / D, EPS_LN2, ALU.mult, ALU.add).then_inc(s["c_dve_ln"], c.up())
                dve.wait_ge(s["c_dve_ln"], c.now())
                dve.scalar_tensor_tensor(vs[:, :], dmean[:, :], 0.25, vs[:, :], ALU.mult, ALU.add).then_inc(s["c_dve_ln"], c.up())
                dve.wait_ge(s["c_dve_ln"], c.now())
                dve.tensor_scalar(mean[:, :], mean[:, :], 1.0, None, ALU.mult).then_inc(s["var"], 1)
                c.end()

            def normalize_2(n):
                dve.wait_ge(s["lrs"], n + 1 + 1)
                dve.wait_ge(s["var"], n + 1 + 1)
                for t in range(TT):
                    i = dve.tensor_scalar(xh[:, t, :], X1[:, bass.ds(n * TT + t, 1), :].rearrange("p o d -> p (o d)"),
                                          mean[:, t:t + 1], lrs[:, t:t + 1], ALU.subtract, ALU.mult)
                i.then_inc(s["xh"], 1)

            def shared(ph, use, next_b):
                if not ph.has(use):
                    return
                what, b = use[2], ph.b
                if what == "ctx":
                    dve.wait_ge(s["pe_shared"], ph.number(use) + 1)
                    n = b * NG + use[0] - 1
                    g = (use[0] - 1) % NG
                    c = Count(n, CTX_STEPS)
                    sh = SH[:, :].rearrange("p (t h c) -> p t h c", t=TT, h=GH)
                    dve.reciprocal(rl_[:, :, :], sh[:, :, :, KD]).then_inc(s["c_dve_ctx"], c.up())
                    dve.wait_ge(s["c_dve_ctx"], c.now())
                    hs = (g % GM) * GH
                    for h in range(GH):
                        i = dve.tensor_tensor(ctxn[:, g // GM, :, hs + h, :], sh[:, :, h, 0:KD], spread(rl_[:, :, h], KD), ALU.mult)
                    i.then_inc(s["shared_free"], 1)
                    c.end()
                elif what == "wo":
                    dve.wait_ge(s["pe_shared"], ph.number(use) + 1)
                    dve.wait_ge(s["x2"], (b - 1 if not isinstance(b, int) or b > 0 else 0) + 1)
                    dve.tensor_tensor(t1[:, :, :], SH[:, :].rearrange("p (t d) -> p t d", t=TT), X1[:, bass.ds((b - 1) * TT, TT), :], ALU.add).then_inc(s["shared_free"], 1)
                    dve.wait_ge(s["shared_free"], ph.number(use) + 1)
                    dve.tensor_tensor(X[:, bass.ds((b - 1) * TT, TT), :], t1[:, :, :], bop[:, :].unsqueeze(1).to_broadcast([P, TT, D]), ALU.add).then_inc(s["x2"], 1)
                elif what == "logits":
                    dve.wait_ge(s["pe_shared"], ph.number(use) + 1)
                    dve.tensor_tensor(lgt[:, :], SH[:, 0:MX], rb[:, :], ALU.add).then_inc(s["shared_free"], 1)
                elif what[0] == "v":
                    dve.wait_ge(s["pe_shared"], ph.number(use) + 1)
                    dve.wait_ge(s["v_filled"], MX * next_b + 1)
                    dve.tensor_tensor(vtmp[:, int(what[1])].rearrange("p h k -> p (h k)"), SH[:, 0:MX * H * KD], bv[:, :], ALU.add).then_inc(s["shared_free"], 1)

            def max_unit(b, g, i):
                u = b * UNITS + g * 16 + i
                if i == 0:
                    n = b * NG + g
                    dve.wait_ge(s["neg_ready"], (n - 1 if not (isinstance(b, int) and n < 1) else 0) + 1)
                dve.wait_ge(s["pe_max"], u + 1 + 1)
                dve.tensor_reduce(top[:, g % 2, i:i + 1], bank[MAXB[i % 2]][:, :], AX.X, ALU.max).then_inc(s["max_read"], 1)

            def body(ph):
                b = ph.b
                if ph.kind == "prologue":
                    normalize_1(0)
                    normalize_2(0)
                    for what in PREP:
                        shared(ph, (0, 0, what), 0)
                    for g in range(2):
                        for i in range(16):
                            max_unit(0, g, i)
                    return
                if ph.kind == "epilogue":
                    for use in BEFORE:
                        shared(ph, use, 0)
                    return
                for g in range(NG):
                    for st in range(SL):
                        for i in range(GH):
                            if not (ph.last and g + 2 >= NG):
                                max_unit(b, g + 2, st * GH + i)
                        if not ph.last:
                            if (g, st) == (0, 0):
                                normalize_1(b + 1)
                            if (g, st) == (0, 3):
                                normalize_2(b + 1)
                        for use in SHARED:
                            if use[:2] == (g, st):
                                shared(ph, use, b + 1)
                        c = Count(b, P_STEPS)
                        if (g, st) == (2, 1):
                            dve.tensor_reduce(lmx[:, :], lgt[:, :], AX.X, ALU.max, negate=True).then_inc(s["lmax"], 1)
                        if (g, st) == (2, 3):
                            dve.wait_ge(s["pexp"], b + 1 + 1)
                            dve.reciprocal(psm[:, :], psm[:, :]).then_inc(s["c_dve_p"], c.up())
                            dve.wait_ge(s["c_dve_p"], c.now())
                            dve.tensor_scalar(pr[:, :], pe_[:, :], psm[:, :], None, ALU.mult).then_inc(s["c_dve_p"], c.up())
                            dve.wait_ge(s["c_dve_p"], c.now())
                            dve.tensor_scalar(bop[:, :], bo[:, 0, :], pr[:, 0:1], None, ALU.mult).then_inc(s["c_dve_p"], c.up())
                            dve.wait_ge(s["c_dve_p"], c.now())
                            dve.scalar_tensor_tensor(bop[:, :], bo[:, 1, :], pr[:, 1:2], bop[:, :], ALU.mult, ALU.add).then_inc(s["pr"], 1)
                            c.end()
            phases(dve, body)

        @block.gpsimd
        def _(pool):
            def negate(n, par):
                c = Count(n, NEG_STEPS)
                count = in_register(pool, 16 * (n + 1) + 1)
                pool.wait_ge(*met)
                pool.wait_ge(s["max_read"], count)
                pool.tensor_scalar(negr[:, par, :], top[:, par, :], -1.0, 0.0, ALU.mult, ALU.add).then_inc(s["c_pool_neg"], c.up())
                pool.tensor_scalar(neg[:, par, 0, :], top[:, par, :], -1.0, 0.0, ALU.mult, ALU.add).then_inc(s["c_pool_neg"], c.up())
                count = in_register(pool, c.now())
                pool.wait_ge(*met)
                pool.wait_ge(s["c_pool_neg"], count)
                pool.tensor_tensor(negr[:, par, :], negr[:, par, :], neg[:, par, 0, :], ALU.subtract).then_inc(s["c_pool_neg"], c.up())
                count = in_register(pool, c.now())
                pool.wait_ge(*met)
                pool.wait_ge(s["c_pool_neg"], count)
                pool.tensor_scalar(neg[:, par, 1, :], negr[:, par, :], 1.0, 0.0, ALU.mult, ALU.add).then_inc(s["c_pool_neg"], c.up())
                count = in_register(pool, c.now())
                pool.wait_ge(*met)
                pool.wait_ge(s["c_pool_neg"], count)
                pool.tensor_tensor(neg[:, par, 2, :], negr[:, par, :], neg[:, par, 1, :], ALU.subtract).then_inc(s["neg_ready"], 1)
                c.end()

            def split(ph, use, n):
                m, k = int(use[2][1]), int(use[2][0] == "k")
                c = Count(n * 4 + 2 * m + k, SPLIT_STEPS)
                count = in_register(pool, ph.number(use) + 1)
                pool.wait_ge(*met)
                pool.wait_ge(s["shared_free"], count)
                count = in_register(pool, 16 * 2 * len(PAIRS) * n + 1)
                pool.wait_ge(*met)
                pool.wait_ge(s[f"stack{m}"], count)
                a, f = parts[m][k], full[k]
                pool.tensor_scalar(a[:, 0, :], f[:, :], 1.0, 0.0, ALU.mult, ALU.add).then_inc(s["c_pool_split"], c.up())
                count = in_register(pool, c.now())
                pool.wait_ge(*met)
                pool.wait_ge(s["c_pool_split"], count)
                pool.tensor_tensor(rest[:, :], f[:, :], a[:, 0, :], ALU.subtract).then_inc(s["c_pool_split"], c.up())
                count = in_register(pool, c.now())
                pool.wait_ge(*met)
                pool.wait_ge(s["c_pool_split"], count)
                pool.tensor_scalar(a[:, 1, :], rest[:, :], 1.0, 0.0, ALU.mult, ALU.add).then_inc(s["c_pool_split"], c.up())
                count = in_register(pool, c.now())
                pool.wait_ge(*met)
                pool.wait_ge(s["c_pool_split"], count)
                pool.tensor_tensor(a[:, 2, :], rest[:, :], a[:, 1, :], ALU.subtract).then_inc(s["split"], 1)
                c.end()

            def fill_v(m, n, used):
                if used is not None:
                    count = in_register(pool, used + 1)
                    pool.wait_ge(*met)
                    pool.wait_ge(s["pv_done"], count)
                hs = slice(m * H, (m + 1) * H)
                pool.tensor_scalar(V[:, :, hs, 0:KD], vtmp[:, :, hs, :], 1.0, 0.0, ALU.mult, ALU.add).then_inc(s["v_filled"], 1)

            def rsqrt(n):
                count = in_register(pool, n + 1 + 1)
                pool.wait_ge(*met)
                pool.wait_ge(s["var"], count)
                pool.tensor_tensor(lrs[:, :], vs[:, :], T["mhalf"][:, 0:TT], ALU.pow).then_inc(s["lrs"], 1)

            def mean_tokens(ph, use, n):
                count = in_register(pool, ph.number(use) + 1)
                pool.wait_ge(*met)
                pool.wait_ge(s["shared_free"], count)
                pool.tensor_scalar(nmat[:, :], T["ones"][:, :], msum[:, :], 1.0 / L, ALU.mult, ALU.mult).then_inc(s["nmat"], 1)

            def x1_sum(n):
                count = in_register(pool, n + 1 + 1)
                pool.wait_ge(*met)
                pool.wait_ge(s["x2"], count)
                xs = bass.ds(n * TT, TT)
                pool.tensor_tensor(X1[:, xs, :], X1[:, xs, :], X[:, xs, :], ALU.add).then_inc(s["x1_sum"], 1)

            def body(ph):
                b = ph.b
                if ph.kind == "prologue":
                    rsqrt(0)
                    mean_tokens(ph, (0, 0, "xT"), 0)
                    for what in ("q0", "k0"):
                        split(ph, (0, 0, what), 0)
                    count = in_register(pool, ph.number((0, 0, "v3")) + 1)
                    pool.wait_ge(*met)
                    pool.wait_ge(s["shared_free"], count)
                    for m in range(MX):
                        fill_v(m, 0, None)
                    for what in ("q1", "k1"):
                        split(ph, (0, 0, what), 0)
                    negate(0, 0)
                    return
                if ph.kind == "epilogue":
                    x1_sum(b - 1)
                    return
                for g in range(NG):
                    if not (ph.last and g == NG - 1):
                        negate(b * NG + g + 1, (g + 1) % 2)
                    if g == 0 and not ph.last:
                        rsqrt(b + 1)
                    if g == 1 and not ph.first:
                        fill_v(1, b, b * NG * SL)
                        x1_sum(b - 1)
                    if g == 2 and not ph.last:
                        mean_tokens(ph, (1, 3, "xT"), b + 1)
                        split(ph, (2, 0, "q0"), b + 1)
                    if g == 3:
                        if not ph.last:
                            split(ph, (2, 3, "k0"), b + 1)
                        count = in_register(pool, b + 1 + 1)
                        pool.wait_ge(*met)
                        pool.wait_ge(s["pr"], count)
                        if not ph.first:
                            count = in_register(pool, ph.number((1, 0, "wo")) + 1)
                            pool.wait_ge(*met)
                            pool.wait_ge(s["shared_free"], count)
                        for m in range(MX):
                            i = pool.tensor_scalar(wop[:, m, :], wo[:, m, :], pr[:, m:m + 1], 0.0, ALU.mult, ALU.add)
                        i.then_inc(s["wop"], 1)
                    if g == 5 and not ph.last:
                        count = in_register(pool, ph.number((5, 0, "v3")) + 1)
                        pool.wait_ge(*met)
                        pool.wait_ge(s["shared_free"], count)
                        fill_v(0, b + 1, b * NG * SL + GM * SL)
                        split(ph, (5, 3, "q1"), b + 1)
                    if g == 6 and not ph.last:
                        split(ph, (6, 0, "k1"), b + 1)
            phases(pool, body)

        @block.sync
        def _(sp):
            def fill(m, n, used):
                count = in_register(sp, 4 * n + 2 * m + 2 + 1)
                sp.wait_ge(*met)
                sp.wait_ge(s["split"], count)
                if used is not None:
                    count = in_register(sp, used + 1)
                    sp.wait_ge(*met)
                    sp.wait_ge(s["pv_done"], count)
                for i, stack in enumerate((Q[m], K[m])):
                    for j, pair in enumerate(PAIRS):
                        src = parts[m][i][:, pair[i], :]
                        sp.dma_start(stack[j * KD:(j + 1) * KD, :, :], src).then_inc(s[f"stack{m}"], 16)

            def send(ph, use, n, g):
                count = in_register(sp, ph.number(use) + 1)
                sp.wait_ge(*met)
                sp.wait_ge(s["shared_free"], count)
                count = in_register(sp, 16 * n + 1)
                sp.wait_ge(*met)
                sp.wait_ge(s["neg_rows"], count)
                m, h = (g % NG) // GM, (g % GM) * GH
                dst = Q[m][QROWS:QROWS + MROWS, h:h + GH, :].rearrange("a h (t p) -> a (h t) p", p=P)
                sp.dma_start(dst, negT[:, g % 2, :]).then_inc(s["neg_rows"], 16)

            def body(ph):
                b = ph.b
                if ph.kind == "prologue":
                    for m in range(MX):
                        fill(m, 0, None)
                    send(ph, (0, 1, "neg"), 0, 0)
                    return
                if ph.kind == "epilogue":
                    return
                for g in range(NG):
                    if ph.has((g, 1, "neg")):
                        send(ph, (g, 1, "neg"), b * NG + g + 1, g + 1)
                    if g == 0 and not ph.first:
                        fill(1, b, b * NG * SL)
                    if g == 4 and not ph.last:
                        fill(0, b + 1, b * NG * SL + GM * SL)
            phases(sp, body)


NE, TOP = 8, 2
FE = 2


def build_experts(nc, ctx, T, dram, out):
    def sb(name, shape, dt=FP32):
        return ctx.enter_context(nc.sbuf_tensor(name, shape, dt))

    X, X1, bank, ident = T["X"], T["X1"], T["bank"], T["ident"]
    rw = sb("f_rw", [P, NE]); rb = sb("f_rb", [P, NE]); ln = sb("f_ln", [P, 2])
    bst = sb("f_bst", [P, 2, TT, 6]); mean = sb("f_mean", [P, 2, TT]); dmean = sb("f_dmean", [P, 2, TT]); vs = sb("f_vs", [P, 2, TT]); rs = sb("f_rs", [P, 2, TT])
    xh = sb("f_xh", [P, TT, D]); n2T = sb("f_n2T", [P, 2, L]); msum = sb("f_msum", [P, 1]); nmat = sb("f_nmat", [P, P])
    lg = sb("f_lg", [P, NE]); lmx = sb("f_lmx", [P, 1]); pe_ = sb("f_pe", [P, NE]); psm = sb("f_psm", [P, 1]); pr = sb("f_pr", [P, NE])
    best = sb("f_best", [P, 8]); which = sb("f_which", [P, 2, 8], mybir.dt.uint32); bs = sb("f_bs", [P, 1]); wgt = sb("f_wgt", [P, 2, TOP])
    w1 = sb("f_w1", [P, 2, TOP, FE * P]); w2 = sb("f_w2", [P, 2, TOP, FE, D]); w2p = sb("f_w2p", [P, TOP * FE, D])
    hid = sb("f_hid", [P, TOP * FE, L]); y = sb("f_y", [P, TT, D]); res = sb("f_res", [P, 2, TT, D])

    names = ["var", "rs", "xh", "pe_T", "n2T", "nmat", "pe_lg", "lmx", "pexp", "picked", "w1_in0", "w1_in1", "w2_in0", "w2_in1", "w2p", "pe_up", "gelu",
             "pe_down", "y", "yvar", "yrs", "res", "stored", "c_ln", "c_ln2", "c_pick", "c_y"]
    loaded = ctx.enter_context(nc.semaphore("f_loaded"))
    s = {n: ctx.enter_context(nc.semaphore("f_" + n)) for n in names}
    met = (T["masks"], 8)

    with nc.Block() as block:
        @block.gpsimd
        def _(pool):
            for started in s.values():
                pool.sem_inc(started, 1)

        @block.sync
        def _(sp):
            with nc.allow_non_contiguous_dma(reason="per-feature columns of a few bytes"):
                for dst, src in [(rw[:, :], dram["f_rw"]), (rb[:, :], dram["f_rb"].partition_broadcast(P)),
                                 (ln[:, 0:1], dram["ln2_g"].rearrange("(p o) -> p o", o=1)), (ln[:, 1:2], dram["ln2_b"].rearrange("(p o) -> p o", o=1))]:
                    sp.dma_start(dst, src).then_inc(loaded, 16)
            sp.wait_ge(loaded, 64)

    def rounds(engine, choose, run):
        def pair(q, last):
            choose(2 * q + 1, 1, q)
            run(2 * q, 0, q)
            if not last:
                choose(2 * q + 2, 0, q + 1)
            run(2 * q + 1, 1, q)
        choose(0, 0, 0)
        with engine.Fori(0, B // 2 - 1) as q:
            pair(q, False)
        pair(B // 2 - 1, True)

    def rows(ap, n):
        return ap[:, bass.ds(n, 1), :].rearrange("p o d -> p (o d)")

    def layer_norm(dve, chain, steps, which_one, source, eps, name):
        b_, m_, d_, v_ = bst[:, which_one], mean[:, which_one], dmean[:, which_one], vs[:, which_one]
        for t in range(TT):
            dve.bn_stats(b_[:, t, :], source(t)).then_inc(s[steps], chain.up())
        dve.wait_ge(s[steps], chain.now())
        dve.tensor_tensor(m_, b_[:, :, 1], b_[:, :, 4], ALU.add).then_inc(s[steps], chain.up())
        dve.tensor_tensor(d_, b_[:, :, 1], b_[:, :, 4], ALU.subtract).then_inc(s[steps], chain.up())
        dve.tensor_tensor(v_, b_[:, :, 2], b_[:, :, 5], ALU.add).then_inc(s[steps], chain.up())
        dve.wait_ge(s[steps], chain.now())
        dve.tensor_scalar(m_, m_, 0.5, None, ALU.mult).then_inc(s[steps], chain.up())
        dve.tensor_tensor(d_, d_, d_, ALU.mult).then_inc(s[steps], chain.up())
        dve.tensor_scalar(v_, v_, 1.0 / D, eps, ALU.mult, ALU.add).then_inc(s[steps], chain.up())
        dve.wait_ge(s[steps], chain.now())
        dve.scalar_tensor_tensor(v_, d_, 0.25, v_, ALU.mult, ALU.add).then_inc(s[name], 1)

    with nc.Block() as block:
        @block.vector
        def _(dve):
            def choose(b, par, q):
                c = Count(b, 10)
                layer_norm(dve, c, "c_ln", 0, lambda t: rows(X, b * TT + t), EPS_LN2, "var")
                c.end()
                dve.wait_ge(s["rs"], b + 1 + 1)
                dve.wait_ge(s["pe_T"], b + 1)
                for t in range(TT):
                    i = dve.tensor_scalar(xh[:, t, :], rows(X, b * TT + t), mean[:, 0, t:t + 1], rs[:, 0, t:t + 1], ALU.subtract, ALU.mult)
                i.then_inc(s["xh"], 1)
                c = Count(b, 8)
                dve.wait_ge(s["pe_lg"], b + 1 + 1)
                dve.tensor_tensor(lg[:, :], bank[2][:, 0:NE], rb[:, :], ALU.add).then_inc(s["c_pick"], c.up())
                count = in_register(dve, c.now())
                dve.wait_ge(*met)
                dve.wait_ge(s["c_pick"], count)
                dve.tensor_reduce(lmx[:, :], lg[:, :], AX.X, ALU.max, negate=True).then_inc(s["lmx"], 1)
                dve.wait_ge(s["pexp"], b + 1 + 1)
                dve.reciprocal(psm[:, :], psm[:, :]).then_inc(s["c_pick"], c.up())
                count = in_register(dve, c.now())
                dve.wait_ge(*met)
                dve.wait_ge(s["c_pick"], count)
                dve.tensor_scalar(pr[:, :], pe_[:, :], psm[:, :], None, ALU.mult).then_inc(s["c_pick"], c.up())
                count = in_register(dve, c.now())
                dve.wait_ge(*met)
                dve.wait_ge(s["c_pick"], count)
                dve.max(best[:, :], pr[:, :]).then_inc(s["c_pick"], c.up())
                count = in_register(dve, c.now())
                dve.wait_ge(*met)
                dve.wait_ge(s["c_pick"], count)
                dve.max_index(which[:, par, :], best[:, :], pr[:, :]).then_inc(s["c_pick"], c.up())
                dve.tensor_tensor(bs[:, :], best[:, 0:1], best[:, 1:2], ALU.add).then_inc(s["c_pick"], c.up())
                count = in_register(dve, c.now())
                dve.wait_ge(*met)
                dve.wait_ge(s["c_pick"], count)
                dve.reciprocal(bs[:, :], bs[:, :]).then_inc(s["c_pick"], c.up())
                dve.memset(dmean[:, 0, 0:1], 0.0).then_inc(s["c_pick"], c.up())
                count = in_register(dve, c.now())
                dve.wait_ge(*met)
                dve.wait_ge(s["c_pick"], count)
                dve.tensor_scalar(wgt[:, par, :], best[:, 0:TOP], bs[:, :], None, ALU.mult).then_inc(s["picked"], 1)
                c.end()

            def run(b, par, q):
                c = Count(b, 10)
                dve.wait_ge(s["pe_down"], b + 1 + 1)
                dve.wait_ge(s["res"], b + 1)
                dve.tensor_tensor(y[:, :, :], bank[6][:, :].rearrange("p (t d) -> p t d", t=TT), X1[:, bass.ds(b * TT, TT), :], ALU.add).then_inc(s["y"], 1)
                dve.wait_ge(s["y"], b + 1 + 1)
                layer_norm(dve, c, "c_y", 1, lambda t: y[:, t, :], EPS_LN, "yvar")
                c.end()
                dve.wait_ge(s["yrs"], b + 1 + 1)
                dve.wait_ge(s["stored"], 16 * b + 1)
                for t in range(TT):
                    i = dve.tensor_scalar(res[:, par, t, :], y[:, t, :], mean[:, 1, t:t + 1], rs[:, 1, t:t + 1], ALU.subtract, ALU.mult)
                i.then_inc(s["res"], 1)
            rounds(dve, choose, run)

        @block.gpsimd
        def _(pool):
            def choose(b, par, q):
                count = in_register(pool, b + 1 + 1)
                pool.wait_ge(*met)
                pool.wait_ge(s["var"], count)
                pool.tensor_tensor(rs[:, 0], vs[:, 0], T["mhalf"][:, 0:TT], ALU.pow).then_inc(s["rs"], 1)
                count = in_register(pool, b + 1 + 1)
                pool.wait_ge(*met)
                pool.wait_ge(s["n2T"], count)
                pool.tensor_scalar(nmat[:, :], T["ones"][:, :], msum[:, :], 1.0 / L, ALU.mult, ALU.mult).then_inc(s["nmat"], 1)

            def run(b, par, q):
                count = in_register(pool, b + 1 + 1)
                pool.wait_ge(*met)
                pool.wait_ge(s["picked"], count)
                count = in_register(pool, 32 * (q + 1) + 1)
                pool.wait_ge(*met)
                pool.wait_ge(s[f"w2_in{par}"], count)
                count = in_register(pool, b + 1)
                pool.wait_ge(*met)
                pool.wait_ge(s["pe_down"], count)
                for e in range(TOP):
                    i = pool.tensor_scalar(w2p[:, e * FE:(e + 1) * FE, :], w2[:, par, e], wgt[:, par, e:e + 1], 0.0, ALU.mult, ALU.add)
                i.then_inc(s["w2p"], 1)
                count = in_register(pool, b + 1 + 1)
                pool.wait_ge(*met)
                pool.wait_ge(s["yvar"], count)
                pool.tensor_tensor(rs[:, 1], vs[:, 1], T["mhalf"][:, 0:TT], ALU.pow).then_inc(s["yrs"], 1)
            rounds(pool, choose, run)

        @block.scalar
        def _(act):
            def choose(b, par, q):
                act.wait_ge(s["pe_T"], b + 1 + 1)
                act.wait_ge(s["nmat"], b + 1)
                act.activation(n2T[:, par, :], bank[0][:, :], ACT.Identity, scale=ln[:, 0:1], bias=ln[:, 1:2], accum_out=msum[:, :]).then_inc(s["n2T"], 1)
                act.wait_ge(s["lmx"], b + 1 + 1)
                act.activation(pe_[:, :], lg[:, :], ACT.Exp, bias=lmx[:, :], accum_out=psm[:, :]).then_inc(s["pexp"], 1)

            def run(b, par, q):
                act.wait_ge(s["pe_down"], b + 1)
                for j in range(TOP * FE):
                    act.wait_ge(s["pe_up"], b * TOP * FE + j + 1 + 1)
                    act.activation(hid[:, j, :], bank[4 + j % 2][:, :], ACT.Gelu).then_inc(s["gelu"], 1)
            rounds(act, choose, run)

        @block.tensor
        def _(pe):
            def choose(b, par, q):
                pe.wait_ge(s["xh"], b + 1 + 1)
                pe.wait_ge(s["n2T"], b + 1)
                for t in range(TT):
                    i = pe.transpose(bank[0][:, t * P:(t + 1) * P], xh[:, t, :], ident[:, :])
                i.then_inc(s["pe_T"], 1)
                pe.wait_ge(s["nmat"], b + 1 + 1)
                pe.wait_ge(s["picked"], b + 1)
                pe.matmul(bank[2][:, 0:NE], nmat[:, :], rw[:, :], start=True, stop=True).then_inc(s["pe_lg"], 1)

            def run(b, par, q):
                pe.wait_ge(s[f"w1_in{par}"], 32 * (q + 1) + 1)
                for j in range(TOP * FE):
                    pe.wait_ge(s["gelu"], b * TOP * FE + max(j - 1, 0) + 1)
                    pe.matmul(bank[4 + j % 2][:, :], w1[:, par, j // FE, (j % FE) * P:(j % FE + 1) * P], n2T[:, par, :], start=True, stop=True).then_inc(s["pe_up"], 1)
                pe.wait_ge(s["gelu"], (b + 1) * TOP * FE + 1)
                pe.wait_ge(s["w2p"], b + 1 + 1)
                pe.wait_ge(s["y"], b + 1)
                for t in range(TT):
                    for j in range(TOP * FE):
                        i = pe.matmul(bank[6][:, t * P:(t + 1) * P], hid[:, j, t * P:(t + 1) * P], w2p[:, j, :], start=j == 0, stop=j == TOP * FE - 1)
                i.then_inc(s["pe_down"], 1)
            rounds(pe, choose, run)

        @block.sync
        def _(sp):
            def choose(b, par, q):
                count = in_register(sp, b + 1 + 1)
                sp.wait_ge(*met)
                sp.wait_ge(s["picked"], count)
                count = in_register(sp, (b - 1 if isinstance(b, int) and b > 0 or not isinstance(b, int) else 0) + 1)
                sp.wait_ge(*met)
                sp.wait_ge(s["w2p"], count)
                count = in_register(sp, (b - 1 if isinstance(b, int) and b > 0 or not isinstance(b, int) else 0) + 1)
                sp.wait_ge(*met)
                sp.wait_ge(s["pe_down"], count)
                for e in range(TOP):
                    x = sp.value_load(which[0:1, par, e:e + 1], min_val=0, max_val=NE - 1)
                    sp.dma_start(w1[:, par, e, :], dram["fw1"][bass.ds(x, 1), :, :].rearrange("o d f -> d (o f)")).then_inc(s[f"w1_in{par}"], 16)
                    sp.dma_start(w2[:, par, e], dram["fw2"][bass.ds(x, 1), :, :].rearrange("o (j p) d -> p (o j) d", p=P)).then_inc(s[f"w2_in{par}"], 16)

            def run(b, par, q):
                count = in_register(sp, b + 1 + 1)
                sp.wait_ge(*met)
                sp.wait_ge(s["res"], count)
                count = in_register(sp, 16 * b + 1)
                sp.wait_ge(*met)
                sp.wait_ge(s["stored"], count)
                sp.dma_start(out[bass.ds(b, 1), :, :].rearrange("o (t p) d -> p (o t) d", p=P), res[:, par]).then_inc(s["stored"], 16)
            rounds(sp, choose, run)
            sp.wait_ge(s["stored"], 16 * B + 1)


def build(nc, dram, out):
    with ExitStack() as ctx:
        def sb(name, shape, dt=FP32):
            return ctx.enter_context(nc.sbuf_tensor(name, shape, dt))
        T = {"X": sb("X", [P, B * TT, D]), "X1": sb("X1", [P, B * TT, D]),
             "ident": sb("ident", [P, P]), "tri": sb("tri", [P, P]), "above": sb("above", [P, P]),
             "ones": sb("ones", [P, P]), "mhalf": sb("mhalf", [P, 16])}
        T["bank"] = [ctx.enter_context(nc.psum_tensor(f"bank{i}", [P, 512], FP32)) for i in range(8)]
        x_loaded = ctx.enter_context(nc.semaphore("x_loaded"))
        masks = ctx.enter_context(nc.semaphore("masks"))
        T["masks"] = masks
        with nc.Block() as block:
            @block.sync
            def _(sp):
                for q in range(B):
                    sp.dma_start(T["X"][:, q * TT:(q + 1) * TT, :], dram["x"][q].rearrange("(t p) d -> p t d", p=P)).then_inc(x_loaded, 16)
                sp.wait_ge(x_loaded, 16 * B)

            @block.gpsimd
            def _(pool):
                pool.memset(T["ident"][:, :], 0.0).then_inc(masks, 1)
                for n in ("tri", "above", "ones"):
                    pool.memset(T[n][:, :], 1.0).then_inc(masks, 1)
                pool.memset(T["mhalf"][:, :], -0.5).then_inc(masks, 1)
                pool.wait_ge(masks, 5)
                pool.affine_select(out=T["ident"][:, :], in_=T["ident"][:, :], compare_op=ALU.not_equal, fill=1.0,
                                   base=0, pattern=[[-1, P]], channel_multiplier=1).then_inc(masks, 1)
                pool.affine_select(out=T["tri"][:, :], in_=T["tri"][:, :], compare_op=ALU.is_ge, fill=0.0,
                                   base=0, pattern=[[1, P]], channel_multiplier=-1).then_inc(masks, 1)
                pool.affine_select(out=T["above"][:, :], in_=T["above"][:, :], compare_op=ALU.is_ge, fill=0.0,
                                   base=-1, pattern=[[-1, P]], channel_multiplier=1).then_inc(masks, 1)
                pool.wait_ge(masks, 8)
        with ExitStack() as inner:
            build_mamba(nc, inner, T, dram)
        with ExitStack() as inner:
            build_attention(nc, inner, T, dram)
        with ExitStack() as inner:
            build_experts(nc, inner, T, dram, out)


_INS = {'x': 'L0_attn_x', 'w_in': 'L0_attn_w_in', 'conv_w': 'L0_attn_conv_w', 'conv_b': 'L0_attn_conv_b', 'dt_bias': 'L0_attn_dt_bias',
        'a_log': 'L0_attn_a_log', 'd_skip': 'L0_attn_d_skip', 'norm_w': 'L0_attn_norm_w', 'w_out': 'L0_attn_w_out', 'w_fc': 'L0_attn_w_fc', 'w_proj': 'L0_attn_w_proj',
        'ln1_g': 'L0_ffn_ln1_g', 'ln1_b': 'L0_ffn_ln1_b', 'wq': 'L0_ffn_mha_wq', 'wk': 'L0_ffn_mha_wk', 'wv': 'L0_ffn_mha_wv', 'wo': 'L0_ffn_mha_wo',
        'bq': 'L0_ffn_mha_bq', 'bk': 'L0_ffn_mha_bk', 'bv': 'L0_ffn_mha_bv', 'bo': 'L0_ffn_mha_bo', 'rw': 'L0_ffn_mha_rw', 'rb': 'L0_ffn_mha_rb',
        'ln2_g': 'L0_ffn_ln2_g', 'ln2_b': 'L0_ffn_ln2_b', 'f_rw': 'L0_ffn_ffn_rw', 'f_rb': 'L0_ffn_ffn_rb', 'fw1': 'L0_ffn_fw1', 'fw2': 'L0_ffn_fw2'}


def kernel(**inputs):
    import numpy as _np
    import concourse.bacc as _bacc
    from concourse import mybir as _mybir
    from concourse.bass_utils import run_bass_kernel_spmd as _run

    nc = _bacc.Bacc("TRN2", target_bir_lowering=False, num_devices=1)
    arrays, dram = {}, {}
    for short, name in _INS.items():
        a = _np.ascontiguousarray(inputs[name])
        arrays["in_" + short] = a
        dram[short] = nc.dram_tensor("in_" + short, a.shape, _mybir.dt.from_np(a.dtype), kind="ExternalInput").ap()
    out = nc.dram_tensor("out_0", (8, 512, 128), _mybir.dt.float32, kind="ExternalOutput").ap()
    build(nc, dram, out)
    r = _run(nc, [arrays], core_ids=[0])
    return r.results[0]["out_0"]
```

```python
import concourse.bass as bass
from concourse import mybir
from contextlib import ExitStack

FP32 = mybir.dt.float32
BF16 = mybir.dt.bfloat16
ALU = mybir.AluOpType
ACT = mybir.ActivationFunctionType
AX = mybir.AxisListType

P = 128
B, L, D = 8, 512, 128
TT = L // P
NH, HD = 4, 64
DI = NH * HD
CB = 4
KC = 4
FF = 4
EPS_RMS, EPS_GATE, EPS_LN, EPS_LN2 = 1.1920929e-07, 1e-05, 1e-05, 1e-06


class Count:

    def __init__(self, n, per):
        self.base, self.per, self.n = n * per + 1, per, 0

    def up(self):
        self.n += 1
        return 1

    def now(self):
        return self.base + self.n

    def end(self):
        assert self.n == self.per, (self.n, self.per)


def in_register(engine, count):
    return count if isinstance(count, int) else engine.to_reg(count)


def spread(ap, n):
    return ap.unsqueeze(len(ap.shape)).to_broadcast(list(ap.shape) + [n])


def build_mamba(nc, ctx, T, dram, later_loads):
    def sb(name, shape, dt=FP32):
        return ctx.enter_context(nc.sbuf_tensor(name, shape, dt))

    def two(name, shape, dt=FP32):
        return [sb(name + half, shape, dt) for half in ("_even", "_odd")]

    X, ident, tri, above, ones, mhalf = T["X"], T["ident"], T["tri"], T["above"], T["ones"], T["mhalf"]
    R = [T["bank"][0:4], T["bank"][4:8]]

    w_in = sb("w_in", [P, 2 * DI + 2 * P + NH])
    conv_w = sb("conv_w", [P, CB, KC])
    conv_b = sb("conv_b", [P, CB])
    dtb = sb("dtb", [P, NH])
    neg_a = sb("neg_a", [P, NH])
    dskip = sb("dskip", [P, NH])
    norm_w = sb("norm_w", [P, 2])
    w_out = sb("w_out", [P, 2, D])
    w_fc = sb("w_fc", [P, FF * P])
    w_proj = sb("w_proj", [P, FF, D])

    sq = two("sq", [P, TT, D])
    xn = two("xn", [P, TT, D])
    ms = two("ms", [P, TT])
    rstd = two("rstd", [P, TT])
    xnT = two("xnT", [P, L])
    xbcT = two("xbcT", [P, CB, L])
    sz = two("sz", [P, TT, DI])
    dtv = two("dtv", [P, TT, NH])
    dta = two("dta", [P, TT, NH])
    dte = two("dte", [P, TT, NH])
    dt = two("dt", [P, TT, NH])
    a = two("a", [P, TT, NH])
    dec = two("dec", [P, 2, TT, NH])
    aut = two("aut", [P, 2, NH, P])
    Lm = two("Lm", [P, 2, NH, P])
    Gm = two("Gm", [P, 2, P])
    M = two("M", [P, 2, NH, P])
    xB = two("xB", [P, 2, 4, P])
    u = two("u", [P, 2, DI])
    du = two("du", [P, 2, DI])
    xd = two("xd", [P, 2, DI])
    S = two("S", [P, DI])
    Sd = two("Sd", [P, DI])
    yo = two("yo", [P, DI])
    yd = two("yd", [P, DI])
    g = two("g", [P, TT, DI])
    gsq = two("gsq", [P, DI])
    gss = two("gss", [P, TT])
    gms = two("gms", [P, TT])
    grs = two("grs", [P, TT])
    gT = two("gT", [P, 2, 2, P])
    h = two("h", [P, TT, D])
    hms = two("hms", [P, TT])
    hrs = two("hrs", [P, TT])
    hnT = two("hnT", [P, L])
    rl = two("rl", [P, 2, L])
    mT = two("mT", [P, FF, L])
    r1 = two("r1", [P, TT, D])
    bst = two("bst", [P, TT, 6])
    mean = two("mean", [P, TT])
    dmean = two("dmean", [P, TT])
    vs = two("vs", [P, TT])
    lrs = two("lrs", [P, TT])

    names = ["sq_x", "ms_x", "rs_x", "xn", "pe_xnT", "xnT", "pe_conv", "tap", "conv", "silu", "pe_z", "sz", "dt_read", "dt_abs",
             "dt_exp", "dt_ln", "a", "pe_cum", "dec", "aut", "pe_seg", "Lm", "Gm", "M", "pe_tok", "xB", "u", "xd", "du", "pe_y",
             "y_read", "pe_st", "S", "g", "gss", "gms", "grs", "pe_gT", "gT", "pe_out", "h", "sq_h", "ms_h", "rs_h", "hn",
             "pe_hnT", "hnT", "pe_fc", "relu", "mT", "pe_proj", "proj_read", "var", "lrs", "x1", "step"]
    sems = [{n: ctx.enter_context(nc.semaphore(f"{half}_{n}")) for n in names} for half in ("even", "odd")]
    weights = ctx.enter_context(nc.semaphore("weights"))
    neg_exp = ctx.enter_context(nc.semaphore("neg_exp"))
    folded = ctx.enter_context(nc.semaphore("folded"))
    STEPS = 31
    T["used"] = [weights, neg_exp, folded] + [used for half in sems for used in half.values()]

    def heads(ap):
        return ap.rearrange("p (h e) -> p h e", e=HD)

    with nc.Block() as block:
        @block.scalar
        def _(act):
            loads = [
                (w_in[:, 0:NH], dram["w_in"][:, 2 * DI + 2 * P:]),
                (w_in[:, NH:], dram["w_in"][:, 0:2 * DI + 2 * P]),
                (conv_w[:, :, :], dram["conv_w"].rearrange("(j p) k -> p j k", p=P)),
                (conv_b[:, :], dram["conv_b"].rearrange("(j p) -> p j", p=P)),
                (dtb[:, :], dram["dt_bias"].partition_broadcast(P)),
                (neg_a[:, :], dram["a_log"].partition_broadcast(P)),
                (dskip[:, :], dram["d_skip"].partition_broadcast(P)),
                (norm_w[:, :], dram["norm_w"].rearrange("(j p) -> p j", p=P)),
                (w_out[:, :, :], dram["w_out"].rearrange("(j p) d -> p j d", p=P)),
                (w_fc[:, :], dram["w_fc"]),
                (w_proj[:, :, :], dram["w_proj"].rearrange("(j p) d -> p j d", p=P)),
            ]
            with nc.allow_non_contiguous_dma(reason="per-feature columns of a few bytes"):
                for dst, src in loads:
                    act.dma_start(dst, src).then_inc(weights, 16)
            act.wait_ge(weights, 16 * len(loads))
            act.activation(neg_a[:, :], neg_a[:, :], ACT.Exp).then_inc(neg_exp, 1)

        @block.vector
        def _(dve):
            dve.wait_ge(neg_exp, 1)
            dve.tensor_scalar(neg_a[:, :], neg_a[:, :], -1.0, None, ALU.mult)
            for j in range(2):
                dve.tensor_scalar(w_out[:, j, :], w_out[:, j, :], norm_w[:, j:j + 1], None, ALU.mult)

        @block.sync
        def _(sp):
            for lo, hi in ((0, 2), (2, B)):
                sp.dma_start(X[:, lo * TT:hi * TT, :], dram["x"][lo:hi].rearrange("b (t p) d -> p (b t) d", p=P)).then_inc(T["x_loaded"], 16)
            sp.wait_ge(T["x_loaded"], 32)

        @block.gpsimd
        def _(pool):
            pool.memset(ident[:, :], 0.0).then_inc(T["masks"], 1)
            for mask in (tri, above, ones):
                pool.memset(mask[:, :], 1.0).then_inc(T["masks"], 1)
            pool.memset(mhalf[:, :], -0.5).then_inc(T["masks"], 1)
            pool.wait_ge(T["masks"], 5)
            pool.affine_select(out=ident[:, :], in_=ident[:, :], compare_op=ALU.not_equal, fill=1.0,
                               base=0, pattern=[[-1, P]], channel_multiplier=1).then_inc(T["masks"], 1)
            pool.affine_select(out=tri[:, :], in_=tri[:, :], compare_op=ALU.is_ge, fill=0.0,
                               base=0, pattern=[[1, P]], channel_multiplier=-1).then_inc(T["masks"], 1)
            pool.affine_select(out=above[:, :], in_=above[:, :], compare_op=ALU.is_ge, fill=0.0,
                               base=-1, pattern=[[-1, P]], channel_multiplier=1).then_inc(T["masks"], 1)
            for half in sems:
                for started in half.values():
                    pool.sem_inc(started, 1)
            pool.wait_ge(T["masks"], 8)

    def back(q, c, per=TT):
        return q * per + max(c - 1, 0) + 1

    with nc.Block() as block:
        @block.sync
        def _(sp):
            with nc.allow_non_contiguous_dma(reason="per-feature columns of a few bytes"):
                for dst, src in later_loads:
                    sp.dma_start(dst, src).then_inc(T["later"], 16)

        @block.gpsimd
        def _(pool):
            def power(e, out, in_, name):
                pool.tensor_tensor(out[e][:, :], in_[e][:, :], mhalf[:, 0:TT], ALU.pow).then_inc(sems[e][name], 1)

            def segment_operand(q, e, c):
                s = sems[e]
                pool.wait_ge(s["a"], q + 2)
                pool.wait_ge(s["pe_seg"], back(q, c))
                pool.tensor_tensor(aut[e][:, c % 2], spread(a[e][:, c, :], P),
                                   tri[:, :].unsqueeze(1).to_broadcast([P, NH, P]), ALU.mult).then_inc(s["aut"], 1)

            def chunk_inputs(q, e, c):
                s = sems[e]
                pool.wait_ge(s["xB"], q * TT + c + 2)
                pool.wait_ge(s["pe_y"], back(q, c))
                pool.wait_ge(s["y_read"], back(q, c))
                xt = xB[e][:, c % 2, 0:2, :].rearrange("p a (h e) -> p (a h) e", e=HD)
                pool.tensor_tensor(heads(u[e][:, c % 2]), xt, spread(dt[e][:, c, :], HD), ALU.mult).then_inc(s["u"], 1)
                pool.tensor_tensor(heads(xd[e][:, c % 2]), xt, spread(dskip[:, :], HD), ALU.mult).then_inc(s["xd"], 1)

            def chunk_weights(q, e, c):
                s = sems[e]
                pool.wait_ge(s["Lm"], q * TT + c + 2)
                pool.wait_ge(s["Gm"], q * TT + c + 2)
                pool.tensor_tensor(M[e][:, c % 2], Lm[e][:, c % 2], Gm[e][:, c % 2, :].unsqueeze(1).to_broadcast([P, NH, P]),
                                   ALU.mult).then_inc(s["M"], 1)
                if c < TT - 1:
                    pool.wait_ge(s["pe_st"], q * (TT - 1) + max(c - 1, 0) + 1)
                    pool.wait_ge(s["u"], q * TT + c + 2)
                    pool.tensor_tensor(heads(du[e][:, c % 2]), heads(u[e][:, c % 2]),
                                       Lm[e][:, c % 2, :, P - 1:P].to_broadcast([P, NH, HD]), ALU.mult).then_inc(s["du"], 1)

            def pair(q):
                for e in range(2):
                    pool.wait_ge(sems[e]["ms_x"], q + 2)
                    power(e, rstd, ms, "rs_x")
                for c in range(TT):
                    for e in range(2):
                        segment_operand(q, e, c)
                    for e in range(2):
                        chunk_inputs(q, e, c)
                    for e in range(2):
                        chunk_weights(q, e, c)
                for e in range(2):
                    pool.wait_ge(sems[e]["gms"], q + 2)
                    power(e, grs, gms, "grs")
                for e in range(2):
                    pool.wait_ge(sems[e]["ms_h"], q + 2)
                    power(e, hrs, hms, "rs_h")
                for e in range(2):
                    pool.wait_ge(sems[e]["var"], q + 2)
                    power(e, lrs, vs, "lrs")
            with pool.Fori(0, B // 2) as q:
                pair(q)

        @block.scalar
        def _(act):
            def square_x(q, e):
                s = sems[e]
                act.wait_ge(s["ms_h"], q + 1)
                act.activation(sq[e][:, :, :], X[:, bass.ds((2 * q + e) * TT, TT), :], ACT.Square).then_inc(s["sq_x"], 1)

            def copy_xnT(q, e):
                s = sems[e]
                act.wait_ge(s["pe_xnT"], q + 2)
                act.wait_ge(s["pe_z"], q * TT + 1)
                act.activation(xnT[e][:, :], R[e][0][:, :], ACT.Copy).then_inc(s["xnT"], 1)

            def newest_tap(q, e, j):
                s = sems[e]
                act.wait_ge(s["pe_conv"], q * CB + j + 2)
                act.wait_ge(s["pe_y"], q * TT + 1)
                act.activation(xbcT[e][:, j, :], R[e][(1 + j) % 4][:, :], ACT.Identity, scale=conv_w[:, j, KC - 1:KC],
                               bias=conv_b[:, j:j + 1]).then_inc(s["tap"], 1)

            def gate(q, e, t):
                s = sems[e]
                act.wait_ge(s["pe_z"], q * TT + t + 2)
                act.wait_ge(s["g"], q * TT + 1)
                act.activation(sz[e][:, t, :], R[e][(1 + t) % 4][:, NH:NH + DI], ACT.Silu).then_inc(s["sz"], 1)

            def silu(q, e, j):
                s = sems[e]
                act.wait_ge(s["conv"], q * CB + j + 2)
                act.activation(xbcT[e][:, j, :], xbcT[e][:, j, :], ACT.Silu).then_inc(s["silu"], 1)

            def chunk_copies(q, e, c):
                s = sems[e]
                act.wait_ge(s["pe_tok"], q * TT + c + 2)
                act.wait_ge(s["xd"], back(q, c))
                act.wait_ge(s["Gm"], back(q, c))
                act.wait_ge(s["pe_st"], q * (TT - 1) + max(c - 1, 0) + 1)
                act.activation(xB[e][:, c % 2, :, :], R[e][0][:, :].rearrange("p (a q) -> p a q", a=4), ACT.Copy).then_inc(s["xB"], 1)

            def chunk_decays(q, e, c):
                s = sems[e]
                act.wait_ge(s["pe_seg"], q * TT + c + 2)
                act.wait_ge(s["M"], back(q, c))
                act.wait_ge(s["du"], q * (TT - 1) + max(c - 1, 0) + 1)
                act.activation(Lm[e][:, c % 2], R[e][1][:, :].rearrange("p (h q) -> p h q", h=NH), ACT.Exp).then_inc(s["Lm"], 1)

            def square_g(q, e, c):
                s = sems[e]
                act.wait_ge(s["g"], q * TT + c + 2)
                act.wait_ge(s["gss"], q * TT + c + 1)
                if c == 0:
                    act.wait_ge(s["gms"], q + 1)
                act.activation(gsq[e][:, :], g[e][:, c, :], ACT.Square, accum_out=gss[e][:, c:c + 1]).then_inc(s["gss"], 1)

            def copy_gT(q, e, c):
                s = sems[e]
                act.wait_ge(s["pe_gT"], q * TT + c + 2)
                act.wait_ge(s["pe_out"], back(q, c))
                act.activation(gT[e][:, c % 2], R[e][c % 2][:, 0:DI].rearrange("p (a q) -> p a q", a=2), ACT.Copy).then_inc(s["gT"], 1)

            def relu(q, e, j):
                s = sems[e]
                act.wait_ge(s["pe_fc"], q * FF + j + 2)
                act.wait_ge(s["mT"], back(q, j, FF))
                act.activation(rl[e][:, j % 2, :], R[e][(1 + j) % 4][:, :], ACT.Relu).then_inc(s["relu"], 1)

            def pair(q):
                for e in range(2):
                    square_x(q, e)
                for e in range(2):
                    copy_xnT(q, e)
                for j in range(CB):
                    for e in range(2):
                        newest_tap(q, e, j)
                for t in range(TT):
                    for e in range(2):
                        gate(q, e, t)
                for j in range(CB):
                    for e in range(2):
                        silu(q, e, j)
                for e in range(2):
                    act.wait_ge(sems[e]["dt_abs"], q + 2)
                    act.activation(dte[e][:, :, :], dta[e][:, :, :], ACT.Exp, scale=-1.0).then_inc(sems[e]["dt_exp"], 1)
                for e in range(2):
                    act.wait_ge(sems[e]["dt_exp"], q + 2)
                    act.activation(dta[e][:, :, :], dte[e][:, :, :], ACT.Ln, bias=1.0).then_inc(sems[e]["dt_ln"], 1)
                for e in range(2):
                    act.wait_ge(sems[e]["pe_cum"], q + 2)
                    act.wait_ge(sems[e]["y_read"], q * TT + 1)
                    act.wait_ge(sems[e]["S"], q * (TT - 1) + 1)
                    act.activation(dec[e][:, :, :, :], R[e][3][:, 0:2 * TT * NH].rearrange("p (a t h) -> p a t h", a=2, h=NH),
                                   ACT.Exp).then_inc(sems[e]["dec"], 1)
                for c in range(TT):
                    for e in range(2):
                        chunk_copies(q, e, c)
                    for e in range(2):
                        chunk_decays(q, e, c)
                    for e in range(2):
                        if c:
                            square_g(q, e, c - 1)
                for e in range(2):
                    square_g(q, e, TT - 1)
                for c in range(TT):
                    for e in range(2):
                        copy_gT(q, e, c)
                for e in range(2):
                    act.wait_ge(sems[e]["h"], q * TT + TT + 1)
                    act.wait_ge(sems[e]["ms_x"], q + 2)
                    act.activation(sq[e][:, :, :], h[e][:, :, :], ACT.Square).then_inc(sems[e]["sq_h"], 1)
                for e in range(2):
                    act.wait_ge(sems[e]["pe_hnT"], q + 2)
                    act.wait_ge(sems[e]["pe_fc"], q * FF + 1)
                    act.activation(hnT[e][:, :], R[e][0][:, :], ACT.Copy).then_inc(sems[e]["hnT"], 1)
                for j in range(FF):
                    for e in range(2):
                        relu(q, e, j)
            with act.Fori(0, B // 2) as q:
                pair(q)

        @block.vector
        def _(dve):
            def mean_squares(q, e, c_, out, name, source):
                s = sems[e]
                dve.wait_ge(s[source], q + 2)
                dve.tensor_reduce(out[e][:, :], sq[e][:, :, :], AX.X, ALU.add).then_inc(s["step"], c_.up())
                dve.wait_ge(s["step"], c_.now())
                dve.tensor_scalar(out[e][:, :], out[e][:, :], 1.0 / D, EPS_RMS, ALU.mult, ALU.add).then_inc(s[name], 1)

            def scale_x(q, e):
                s = sems[e]
                dve.wait_ge(s["rs_x"], q + 2)
                dve.wait_ge(s["pe_hnT"], q + 1)
                dve.tensor_tensor(xn[e][:, :, :], X[:, bass.ds((2 * q + e) * TT, TT), :], spread(rstd[e][:, :], D), ALU.mult).then_inc(s["xn"], 1)

            def older_taps(q, e, c_, j):
                s = sems[e]
                for k in range(1, KC):
                    if k == 1:
                        dve.wait_ge(s["tap"], q * CB + j + 2)
                    else:
                        dve.wait_ge(s["step"], c_.now())
                    tap = dve.scalar_tensor_tensor(xbcT[e][:, j, k:L], R[e][(1 + j) % 4][:, 0:L - k], conv_w[:, j, KC - 1 - k:KC - k],
                                                   xbcT[e][:, j, k:L], ALU.mult, ALU.add)
                    if k < KC - 1:
                        tap.then_inc(s["step"], c_.up())
                tap.then_inc(s["conv"], 1)

            def read_dt(q, e, t):
                s = sems[e]
                dve.wait_ge(s["sz"], q * TT + t + 2)
                if t == 0:
                    dve.wait_ge(s["a"], q + 1)
                dve.tensor_tensor(dtv[e][:, t, :], R[e][(1 + t) % 4][:, 0:NH], dtb[:, :], ALU.add).then_inc(s["dt_read"], 1)

            def softplus_in(q, e, c_):
                s = sems[e]
                dve.wait_ge(s["dt_read"], q * TT + TT + 1)
                dve.scalar_tensor_tensor(dta[e][:, :, :], dtv[e][:, :, :], -1.0, dtv[e][:, :, :], ALU.mult, ALU.max).then_inc(s["step"], c_.up())
                dve.wait_ge(s["step"], c_.now())
                dve.tensor_scalar(dtv[e][:, :, :], dtv[e][:, :, :], 0.0, None, ALU.max).then_inc(s["dt_abs"], 1)

            def softplus_out(q, e, c_):
                s = sems[e]
                dve.wait_ge(s["dt_ln"], q + 2)
                dve.wait_ge(s["xd"], q * TT + 1)
                dve.tensor_tensor(dt[e][:, :, :], dtv[e][:, :, :], dta[e][:, :, :], ALU.add).then_inc(s["step"], c_.up())
                dve.wait_ge(s["step"], c_.now())
                dve.tensor_tensor(a[e][:, :, :], dt[e][:, :, :], neg_a[:, :].unsqueeze(1).to_broadcast([P, TT, NH]), ALU.mult).then_inc(s["a"], 1)

            def mask_scores(q, e, c):
                s = sems[e]
                dve.wait_ge(s["xB"], q * TT + c + 2)
                dve.wait_ge(s["M"], back(q, c))
                dve.tensor_tensor(Gm[e][:, c % 2, :], xB[e][:, c % 2, 3, :], tri[:, :], ALU.mult).then_inc(s["Gm"], 1)

            def state(q, e, c_, c):
                s = sems[e]
                if c == TT - 1:
                    return
                if c:
                    dve.wait_ge(s["S"], q * (TT - 1) + c + 1)
                    dve.wait_ge(s["dec"], q + 2)
                    dve.tensor_tensor(heads(Sd[e][:, :]), heads(S[e][:, :]), spread(dec[e][:, 1, c, :], HD), ALU.mult).then_inc(s["step"], c_.up())
                    dve.wait_ge(s["step"], c_.now())
                dve.wait_ge(s["pe_st"], q * (TT - 1) + c + 2)
                if c:
                    dve.tensor_tensor(S[e][:, :], R[e][3][:, 0:DI], Sd[e][:, :], ALU.add).then_inc(s["S"], 1)
                else:
                    dve.tensor_copy(S[e][:, :], R[e][3][:, 0:DI]).then_inc(s["S"], 1)

            def output(q, e, c_, c):
                s = sems[e]
                dve.wait_ge(s["pe_y"], q * TT + c + 2)
                dve.wait_ge(s["xd"], q * TT + c + 2)
                if c == 0:
                    dve.wait_ge(s["g"], q * TT + 1)
                    dve.tensor_tensor(yd[e][:, :], R[e][2][:, 0:DI], xd[e][:, 0, :], ALU.add).then_inc(s["y_read"], 1)
                else:
                    dve.wait_ge(s["dec"], q + 2)
                    dve.wait_ge(s["g"], q * TT + c + 1)
                    dve.tensor_tensor(heads(yo[e][:, :]), heads(R[e][2][:, DI:2 * DI]), spread(dec[e][:, 0, c, :], HD), ALU.mult).then_inc(s["step"], c_.up())
                    dve.tensor_tensor(yd[e][:, :], R[e][2][:, 0:DI], xd[e][:, c % 2, :], ALU.add).then_inc(s["y_read"], 1)
                    dve.wait_ge(s["step"], c_.now())
                    dve.wait_ge(s["y_read"], q * TT + c + 2)
                    dve.tensor_tensor(yd[e][:, :], yd[e][:, :], yo[e][:, :], ALU.add).then_inc(s["step"], c_.up())
                    dve.wait_ge(s["step"], c_.now())
                dve.wait_ge(s["sz"], q * TT + c + 2)
                dve.wait_ge(s["y_read"], q * TT + c + 2)
                dve.wait_ge(s["pe_gT"], q * TT + 1)
                dve.tensor_tensor(g[e][:, c, :], yd[e][:, :], sz[e][:, c, :], ALU.mult).then_inc(s["g"], 1)

            def residual(q, e, c):
                s = sems[e]
                dve.wait_ge(s["pe_out"], q * TT + c + 2)
                if c == 0:
                    dve.wait_ge(s["grs"], q + 2)
                dve.scalar_tensor_tensor(h[e][:, c, :], R[e][2 + c % 2][:, 0:D], grs[e][:, c:c + 1],
                                         X[:, bass.ds((2 * q + e) * TT + c, 1), :].rearrange("p o d -> p (o d)"), ALU.mult, ALU.add).then_inc(s["h"], 1)

            def scale_h(q, e):
                s = sems[e]
                dve.wait_ge(s["rs_h"], q + 2)
                dve.wait_ge(s["pe_xnT"], q + 2)
                dve.tensor_tensor(xn[e][:, :, :], h[e][:, :, :], spread(hrs[e][:, :], D), ALU.mult).then_inc(s["hn"], 1)

            def square_relu(q, e, j):
                s = sems[e]
                dve.wait_ge(s["relu"], q * FF + j + 2)
                dve.wait_ge(s["pe_proj"], q + 1)
                dve.scalar_tensor_tensor(mT[e][:, j, :], R[e][(1 + j) % 4][:, :], 0.0, rl[e][:, j % 2, :], ALU.max, ALU.mult).then_inc(s["mT"], 1)

            def sum_and_stats(q, e, c_):
                s = sems[e]
                dve.wait_ge(s["pe_proj"], q + 2)
                dve.wait_ge(s["x1"], q + 1)
                dve.tensor_tensor(r1[e][:, :, :], R[e][1][:, :].rearrange("p (t d) -> p t d", t=TT), h[e][:, :, :], ALU.add).then_inc(s["proj_read"], 1)
                dve.wait_ge(s["proj_read"], q + 2)
                dve.tensor_tensor(r1[e][:, :, :], r1[e][:, :, :], X[:, bass.ds((2 * q + e) * TT, TT), :], ALU.add).then_inc(s["step"], c_.up())
                dve.wait_ge(s["step"], c_.now())
                for t in range(TT):
                    dve.bn_stats(bst[e][:, t, :], r1[e][:, t, :]).then_inc(s["step"], c_.up())
                dve.wait_ge(s["step"], c_.now())
                dve.tensor_tensor(mean[e][:, :], bst[e][:, :, 1], bst[e][:, :, 4], ALU.add).then_inc(s["step"], c_.up())
                dve.tensor_tensor(dmean[e][:, :], bst[e][:, :, 1], bst[e][:, :, 4], ALU.subtract).then_inc(s["step"], c_.up())
                dve.tensor_tensor(vs[e][:, :], bst[e][:, :, 2], bst[e][:, :, 5], ALU.add).then_inc(s["step"], c_.up())
                dve.wait_ge(s["step"], c_.now())
                dve.tensor_scalar(mean[e][:, :], mean[e][:, :], 0.5, None, ALU.mult).then_inc(s["step"], c_.up())
                dve.tensor_tensor(dmean[e][:, :], dmean[e][:, :], dmean[e][:, :], ALU.mult).then_inc(s["step"], c_.up())
                dve.tensor_scalar(vs[e][:, :], vs[e][:, :], 1.0 / D, EPS_LN, ALU.mult, ALU.add).then_inc(s["step"], c_.up())
                dve.wait_ge(s["step"], c_.now())
                dve.scalar_tensor_tensor(vs[e][:, :], dmean[e][:, :], 0.25, vs[e][:, :], ALU.mult, ALU.add).then_inc(s["var"], 1)

            def normalize(q, e):
                s = sems[e]
                dve.wait_ge(s["lrs"], q + 2)
                for t in range(TT):
                    last = dve.tensor_scalar(X[:, bass.ds((2 * q + e) * TT + t, 1), :].rearrange("p o d -> p (o d)"), r1[e][:, t, :],
                                             mean[e][:, t:t + 1], lrs[e][:, t:t + 1], ALU.subtract, ALU.mult)
                last.then_inc(s["x1"], 1)

            def pair(q):
                steps = [Count(q, STEPS), Count(q, STEPS)]
                for e in range(2):
                    mean_squares(q, e, steps[e], ms, "ms_x", "sq_x")
                for e in range(2):
                    scale_x(q, e)
                for j in range(CB):
                    for e in range(2):
                        older_taps(q, e, steps[e], j)
                for t in range(TT):
                    for e in range(2):
                        read_dt(q, e, t)
                for e in range(2):
                    softplus_in(q, e, steps[e])
                for e in range(2):
                    softplus_out(q, e, steps[e])
                for c in range(TT):
                    for e in range(2):
                        mask_scores(q, e, c)
                    for e in range(2):
                        output(q, e, steps[e], c)
                        state(q, e, steps[e], c)
                for e in range(2):
                    dve.wait_ge(sems[e]["gss"], q * TT + TT + 1)
                    dve.tensor_scalar(gms[e][:, :], gss[e][:, :], 1.0 / DI, EPS_GATE, ALU.mult, ALU.add).then_inc(sems[e]["gms"], 1)
                for c in range(TT):
                    for e in range(2):
                        residual(q, e, c)
                for e in range(2):
                    mean_squares(q, e, steps[e], hms, "ms_h", "sq_h")
                for e in range(2):
                    scale_h(q, e)
                for j in range(FF):
                    for e in range(2):
                        square_relu(q, e, j)
                for e in range(2):
                    sum_and_stats(q, e, steps[e])
                for e in range(2):
                    normalize(q, e)
                    steps[e].end()
            with dve.Fori(0, B // 2) as q:
                pair(q)

        @block.tensor
        def _(pe):
            def mm(out, lhsT, rhs, first=True, last=True):
                return pe.matmul(out, lhsT, rhs, start=first, stop=last)

            def transpose_xn(q, e, ready, name):
                pe.wait_ge(sems[e][ready], q + 2)
                for t in range(TT):
                    last = pe.transpose(R[e][0][:, t * P:(t + 1) * P], xn[e][:, t, :], ident[:, :])
                last.then_inc(sems[e][name], 1)

            def convolved(q, e, j):
                s = sems[e]
                if j == 0:
                    pe.wait_ge(s["xnT"], q + 2)
                    pe.wait_ge(s["proj_read"], q + 1)
                mm(R[e][(1 + j) % 4][:, :], w_in[:, DI + NH + j * P:DI + NH + (j + 1) * P], xnT[e][:, :]).then_inc(s["pe_conv"], 1)

            def gates(q, e, t):
                s = sems[e]
                pe.wait_ge(s["conv"], q * CB + t + 2)
                mm(R[e][(1 + t) % 4][:, 0:DI + NH], xnT[e][:, t * P:(t + 1) * P], w_in[:, 0:DI + NH]).then_inc(s["pe_z"], 1)

            def cumulate(q, e):
                s, n = sems[e], TT * NH
                pe.wait_ge(s["a"], q + 2)
                mm(R[e][3][:, 0:n], tri[:, :], a[e][:, :, :].rearrange("p t h -> p (t h)"))
                mm(R[e][3][:, n:2 * n], ones[:, :], a[e][:, :, :].rearrange("p t h -> p (t h)")).then_inc(s["pe_cum"], 1)

            def tokens_and_scores(q, e, c):
                s, tok = sems[e], slice(c * P, (c + 1) * P)
                if c == 0:
                    pe.wait_ge(s["silu"], q * CB + CB + 1)
                    pe.wait_ge(s["dt_abs"], q + 2)
                pe.wait_ge(s["xB"], q * TT + c + 1)
                for j in range(3):
                    pe.transpose(R[e][0][:, j * P:(j + 1) * P], xbcT[e][:, j, tok], ident[:, :])
                mm(R[e][0][:, 3 * P:4 * P], xbcT[e][:, 2, tok], xbcT[e][:, 3, tok]).then_inc(s["pe_tok"], 1)

            def segments(q, e, c):
                s = sems[e]
                pe.wait_ge(s["aut"], q * TT + c + 2)
                pe.wait_ge(s["Lm"], q * TT + c + 1)
                mm(R[e][1][:, :], above[:, :], aut[e][:, c % 2].rearrange("p h q -> p (h q)")).then_inc(s["pe_seg"], 1)

            def outputs(q, e, c):
                s, tok = sems[e], slice(c * P, (c + 1) * P)
                pe.wait_ge(s["y_read"], q * TT + c + 1)
                if c:
                    pe.wait_ge(s["S"], q * (TT - 1) + c + 1)
                    mm(R[e][2][:, DI:2 * DI], xbcT[e][:, 3, tok], S[e][:, :])
                pe.wait_ge(s["M"], q * TT + c + 2)
                pe.wait_ge(s["u"], q * TT + c + 2)
                for hh in range(NH):
                    last = mm(R[e][2][:, hh * HD:(hh + 1) * HD], M[e][:, c % 2, hh, :], u[e][:, c % 2, hh * HD:(hh + 1) * HD])
                last.then_inc(s["pe_y"], 1)
                if c < TT - 1:
                    pe.wait_ge(s["du"], q * (TT - 1) + c + 2)
                    if c == 0:
                        pe.wait_ge(s["dec"], q + 2)
                    mm(R[e][3][:, 0:DI], xB[e][:, c % 2, 2, :], du[e][:, c % 2, :]).then_inc(s["pe_st"], 1)

            def transpose_g(q, e, c):
                s = sems[e]
                pe.wait_ge(s["g"], q * TT + c + 2)
                pe.wait_ge(s["gT"], back(q, c))
                for j in range(2):
                    last = pe.transpose(R[e][c % 2][:, j * P:(j + 1) * P], g[e][:, c, j * P:(j + 1) * P], ident[:, :])
                last.then_inc(s["pe_gT"], 1)

            def project_out(q, e, c):
                s = sems[e]
                pe.wait_ge(s["gT"], q * TT + c + 2)
                pe.wait_ge(s["h"], back(q, c))
                if c == 1:
                    pe.wait_ge(s["S"], (q + 1) * (TT - 1) + 1)
                for j in range(2):
                    last = mm(R[e][2 + c % 2][:, 0:D], gT[e][:, c % 2, j, :], w_out[:, j, :], j == 0, j == 1)
                last.then_inc(s["pe_out"], 1)

            def pair(q):
                for e in range(2):
                    transpose_xn(q, e, "xn", "pe_xnT")
                for j in range(CB):
                    for e in range(2):
                        convolved(q, e, j)
                for t in range(TT):
                    for e in range(2):
                        gates(q, e, t)
                for e in range(2):
                    cumulate(q, e)
                for c in range(TT):
                    for e in range(2):
                        tokens_and_scores(q, e, c)
                        segments(q, e, c)
                    for e in range(2):
                        outputs(q, e, c)
                for c in range(TT):
                    for e in range(2):
                        transpose_g(q, e, c)
                    for e in range(2):
                        project_out(q, e, c)
                for e in range(2):
                    transpose_xn(q, e, "hn", "pe_hnT")
                for j in range(FF):
                    for e in range(2):
                        if j == 0:
                            pe.wait_ge(sems[e]["hnT"], q + 2)
                        mm(R[e][(1 + j) % 4][:, :], w_fc[:, j * P:(j + 1) * P], hnT[e][:, :]).then_inc(sems[e]["pe_fc"], 1)
                for e in range(2):
                    pe.wait_ge(sems[e]["mT"], (q + 1) * FF + 1)
                    for t in range(TT):
                        for j in range(FF):
                            last = mm(R[e][1][:, t * P:(t + 1) * P], mT[e][:, j, t * P:(t + 1) * P], w_proj[:, j, :], j == 0, j == FF - 1)
                    last.then_inc(sems[e]["pe_proj"], 1)
            with pe.Fori(0, B // 2) as q:
                pair(q)


MX = 2
H, KD = 16, 8
GH = 4
NG = MX * H // GH
GM = NG // MX
SL = 4
PAIRS = [(0, 0), (1, 0), (2, 0), (0, 1), (1, 1), (0, 2)]
QROWS = len(PAIRS) * KD
MROWS = 3
RING, PRING = 3, 8
UNITS = NG * SL * GH
SCALE = float(KD) ** -0.5
TWO_ONES = 1 + 16256 * 2.0 ** -23

SHARED = [(g, 1, "neg") for g in range(NG)] + [(g, 2, "ctx") for g in range(NG)] + [
    (0, 3, "ctxT1"), (1, 0, "wo"), (1, 3, "xT"), (2, 0, "q0"), (2, 3, "k0"), (3, 0, "v0"), (3, 3, "v1"),
    (4, 0, "v2"), (4, 3, "ctxT0"), (5, 0, "v3"), (5, 3, "q1"), (6, 0, "k1"), (6, 3, "logits")]
SHARED = sorted(SHARED)
READ_AT = {}
for use in SHARED:
    g, st = divmod(use[0] * SL + use[1] + 1, SL)
    READ_AT.setdefault((g, st, 1), []).append(use)
PREP = ["xT", "q0", "k0", "v0", "v1", "v2", "v3", "q1", "k1", "logits"]
BEFORE = [(0, 2, "ctx"), (0, 3, "ctxT1"), (1, 0, "wo")]


class Phase:

    def __init__(self, kind, b):
        self.kind, self.b = kind, b
        self.first, self.last = kind == "first", kind == "last"
        prologue = [(0, 0, n) for n in PREP] + [(0, 1, "neg")]
        if kind == "prologue":
            self.uses, self.base = prologue, 0
        elif kind == "epilogue":
            before = Phase("last", b - 1)
            self.uses, self.base = BEFORE, before.base + len(before.uses)
        else:
            self.uses = [x for x in SHARED
                         if not (self.first and x in BEFORE)
                         and not (self.last and (x[2] in PREP or (x[2] == "neg" and x[0] >= NG - 1)))]
            self.base = len(prologue) + (0 if self.first else b * len(SHARED) - len(BEFORE))

    def has(self, use):
        return use in self.uses

    def number(self, use):
        return self.base + self.uses.index(use) + 1


def build_attention(nc, ctx, T):
    def sb(name, shape, dt=FP32):
        return ctx.enter_context(nc.sbuf_tensor(name, shape, dt))

    X, X1, bank, ident = T["X"], T["X1"], T["bank"], T["ident"]
    MAXB, EXPB, PVB, SH = (0, 1, 5), (2, 3, 4), 6, bank[7]
    shb = SH[:, :].bitcast(BF16)

    identb = sb("identb", [P, P], BF16)
    Q = [sb(f"Q{m}", [QROWS + MROWS, H, L], BF16) for m in range(MX)]
    K = [sb(f"K{m}", [QROWS + MROWS, H, L], BF16) for m in range(MX)]
    parts = [[sb(f"parts{m}{i}", [P, 3, L], BF16) for i in range(2)] for m in range(MX)]
    full = [sb(f"full{i}", [P, L]) for i in range(2)]; rest = sb("rest", [P, L])
    V = sb("V", [P, SL, MX * H, 32]); vtmp = sb("vtmp", [P, SL, MX * H, KD])
    E = sb("E", [P, PRING, L])
    top = sb("top", [P, 2, GH * TT]); negr = sb("negr", [P, 2, GH * TT]); neg = sb("neg", [P, 2, 3, GH * TT], BF16)
    negT = sb("negT", [3 * GH * TT, 2, P], BF16)
    ctxu = sb("ctxu", [P, L]); rl_ = sb("rsum", [P, TT, GH]); ctxn = sb("ctxn", [P, MX, TT, H, KD]); ctxT = sb("ctxT", [P, MX, L])
    wq = sb("wq", [P, MX, H * KD]); wk = sb("wk", [P, MX, H * KD]); wop = sb("wop", [P, MX, D]); bop = sb("bop", [P, D])
    wv, wo, bq, bk, bv, bo, rw, rb, lg_ = T["wv"], T["wo"], T["bq"], T["bk"], T["bv"], T["bo"], T["rw"], T["rb"], T["ln1"]
    n1T = sb("n1T", [P, L]); xh = sb("xh", [P, TT, D]); msum = sb("msum", [P, 1]); nmat = sb("nmat", [P, P])
    bst = sb("bst2", [P, TT, 6]); mean = sb("mean2", [P, TT]); dmean = sb("dmean2", [P, TT]); vs = sb("vs2", [P, TT]); lrs = sb("lrs2", [P, TT])
    lgt = sb("lgt", [P, MX]); lmx = sb("lmx", [P, 1]); pe_ = sb("pexp", [P, MX]); psm = sb("psm", [P, 1]); pr = sb("pr", [P, MX])
    t1 = sb("t1", [P, TT, D])

    primed = ["pe_max", "max_read", "pe_exp", "exp_done", "pv_done", "neg_ready", "negT_ready", "neg_rows", "evac", "pe_shared",
              "shared_free", "var", "lrs", "xh", "split", "stack0", "stack1", "v_filled", "nmat", "lmax", "pexp", "pr", "wop",
              "t1", "x2", "x1_sum", "c_dve_ln", "c_dve_ctx", "c_pool_neg", "c_pool_split", "c_dve_p"]
    set_up = ctx.enter_context(nc.semaphore("t_set_up"))
    s = {n: ctx.enter_context(nc.semaphore("t_" + n)) for n in primed}
    met = (T["masks"], 8)

    with nc.Block() as block:
        @block.gpsimd
        def _(pool):
            for used in T["used"]:
                pool.sem_clear(used)
            for started in s.values():
                pool.sem_inc(started, 1)
            pool.memset(K[1][32:, :, :].bitcast(FP32), TWO_ONES).then_inc(set_up, 1)
            pool.wait_ge(set_up, 1)
            pool.memset(V[:, :, :, KD + 1:], 0.0)
            pool.memset(V[:, :, :, KD:KD + 1], 1.0)

        @block.vector
        def _(dve):
            dve.memset(K[0][32:, :, :].bitcast(FP32), TWO_ONES)
            dve.tensor_copy(identb[:, :], ident[:, :])
            dve.wait_ge(T["later"], 16 * T["later_loads"])
            dve.tensor_scalar(bq[:, :], bq[:, :], SCALE, None, ALU.mult)
            for i, w in enumerate((wq, wk)):
                for m in range(MX):
                    dve.tensor_copy(w[:, m, :].rearrange("p (k h) -> p k h", h=H), T["raw"][:, i, m, :].rearrange("p (h k) -> p k h", k=KD))

    LN_STEPS, CTX_STEPS, NEG_STEPS, SPLIT_STEPS, P_STEPS = 10, 1, 4, 3, 3

    def phases(engine, body):
        body(Phase("prologue", 0))
        body(Phase("first", 0))
        with engine.Fori(1, B - 1) as b:
            body(Phase("middle", b))
        body(Phase("last", B - 1))
        body(Phase("epilogue", B))

    with nc.Block() as block:
        @block.tensor
        def _(pe):
            def shared(ph, use, next_b):
                if not ph.has(use):
                    return
                what, b = use[2], ph.b
                if what == "neg":
                    count = in_register(pe, ph.number(use) - 1 + 1)
                    pe.wait_ge(*met)
                    pe.wait_ge(s["shared_free"], count)
                else:
                    pe.wait_ge(s["shared_free"], ph.number(use) - 1 + 1)
                if what == "neg":
                    n = b * NG + use[0] + 1 if ph.kind != "prologue" else 0
                    count = in_register(pe, n + 1 + 1)
                    pe.wait_ge(*met)
                    pe.wait_ge(s["neg_ready"], count)
                    par = (use[0] + 1) % 2 if ph.kind != "prologue" else 0
                    i = pe.transpose(shb[0:3 * GH * TT, 0:P], neg[:, par].rearrange("p a c -> p (a c)"), identb[:, :])
                elif what == "ctx":
                    n = b * NG + use[0]
                    pe.wait_ge(s["evac"], n + 1)
                    for t in range(TT):
                        i = pe.transpose(SH[:, t * P:(t + 1) * P], ctxu[:, t * P:(t + 1) * P], ident[:, :])
                elif what in ("ctxT0", "ctxT1"):
                    m = int(what[-1])
                    for t in range(TT):
                        i = pe.transpose(SH[:, t * P:(t + 1) * P], ctxn[:, m, t].rearrange("p h k -> p (h k)"), ident[:, :])
                elif what == "wo":
                    pe.wait_ge(s["wop"], b + 1)
                    for t in range(TT):
                        for m in range(MX):
                            i = pe.matmul(SH[:, t * P:(t + 1) * P], ctxT[:, m, t * P:(t + 1) * P], wop[:, m, :], start=m == 0, stop=m == MX - 1)
                elif what == "xT":
                    pe.wait_ge(s["xh"], (next_b + 1) * TT + 1)
                    for t in range(TT):
                        i = pe.transpose(SH[:, t * P:(t + 1) * P], xh[:, t, :], ident[:, :])
                elif what[0] in "qk":
                    w = {"q": wq, "k": wk}[what[0]]
                    i = pe.matmul(SH[:, :], w[:, int(what[1]), :], n1T[:, :], start=True, stop=True)
                elif what[0] == "v":
                    t = int(what[1])
                    i = pe.matmul(SH[:, 0:MX * H * KD], n1T[:, t * P:(t + 1) * P], wv[:, :, :].rearrange("p m c -> p (m c)"), start=True, stop=True)
                else:
                    pe.wait_ge(s["nmat"], next_b + 1 + 1)
                    i = pe.matmul(SH[:, 0:MX], nmat[:, :], rw[:, :], start=True, stop=True)
                i.then_inc(s["pe_shared"], 1)

            def max_unit(b, g, i, stacks_of, at):
                m, h, t = (g % NG) // GM, (g % GM) * GH + i // TT, i % TT
                u = b * UNITS + g * 16 + i
                if i == 0:
                    pe.wait_ge(s[f"stack{m}"], 16 * 2 * len(PAIRS) * (stacks_of + 1) + 1)
                before = at if isinstance(b, int) and b == 0 and g < 2 else None
                if before is None or before >= len(MAXB):
                    pe.wait_ge(s["max_read"], (u - 1 if at < 2 else u - 2) + 1)
                pe.matmul(bank[MAXB[at % len(MAXB)]][:, :], Q[m][0:QROWS, h, t * P:(t + 1) * P], K[m][0:QROWS, h, :], start=True, stop=True).then_inc(s["pe_max"], 1)

            def values(b, slot):
                g, st = slot // SL, slot % SL
                if st == 0:
                    pe.wait_ge(s["evac"], b * NG + g + 1)
                    if g % GM == 0:
                        pe.wait_ge(s["v_filled"], b * MX + g // GM + 1 + 1)
                pe.wait_ge(s["exp_done"], b * UNITS + (slot + 1) * GH + 1)
                for i in range(GH):
                    u = slot * GH + i
                    last = pe.matmul(bank[PVB][32 * i:32 * i + 32, :], V[:, st, g * GH + i, :], E[:, u % PRING, :],
                                     start=st == 0, stop=st == SL - 1)
                last.then_inc(s["pv_done"], 1)

            def body(ph):
                b = ph.b
                if ph.kind == "prologue":
                    for what in PREP:
                        shared(ph, (0, 0, what), 0)
                    for i in range(16):
                        max_unit(0, 0, i, 0, i)
                    shared(ph, (0, 1, "neg"), 0)
                    for i in range(16):
                        max_unit(0, 1, i, 0, 16 + i)
                    return
                if ph.kind == "epilogue":
                    values(b - 1, NG * SL - 1)
                    for use in BEFORE:
                        shared(ph, use, 0)
                    return
                for g in range(NG):
                    for st in range(SL):
                        slot = g * SL + st
                        for i in range(GH):
                            if not (ph.last and g + 2 >= NG):
                                max_unit(b, g + 2, st * GH + i, b + (g + 2) // NG, g * 16 + st * GH + i)
                            m, u = g // GM, (g * SL + st) * GH + i
                            if st == 0 and i == 0:
                                pe.wait_ge(s["neg_rows"], 16 * (b * NG + g + 1) + 1)
                            pe.wait_ge(s["exp_done"], b * UNITS + max(u - RING + 1, 0) + 1)
                            pe.matmul(bank[EXPB[u % RING]][:, :], K[m][:, (g % GM) * GH + i, st * P:(st + 1) * P],
                                      Q[m][:, (g % GM) * GH + i, :], start=True, stop=True).then_inc(s["pe_exp"], 1)
                        if slot:
                            values(b, slot - 1)
                        elif not ph.first:
                            values(b - 1, NG * SL - 1)
                        for use in SHARED:
                            if use[:2] == (g, st):
                                shared(ph, use, b + 1)
            phases(pe, body)

        @block.scalar
        def _(act):
            def shared(ph, use, next_b):
                if not ph.has(use):
                    return
                what, b = use[2], ph.b
                if what in ("ctx", "wo", "logits") or what[0] == "v":
                    return
                act.wait_ge(s["pe_shared"], ph.number(use) + 1)
                if what == "neg":
                    n = b * NG + use[0] + 1 if ph.kind != "prologue" else 0
                    par = (use[0] + 1) % 2 if ph.kind != "prologue" else 0
                    act.wait_ge(s["neg_rows"], 16 * n + 1)
                    i = act.activation(negT[:, par, :], shb[0:3 * GH * TT, 0:P], ACT.Copy)
                elif what in ("ctxT0", "ctxT1"):
                    i = act.activation(ctxT[:, int(what[-1]), :], SH[:, :], ACT.Copy)
                elif what == "xT":
                    act.wait_ge(s["nmat"], next_b + 1)
                    i = act.activation(n1T[:, :], SH[:, :], ACT.Identity, scale=lg_[:, 0:1], bias=lg_[:, 1:2], accum_out=msum[:, :])
                else:
                    m, k = int(what[1]), what[0] == "k"
                    act.wait_ge(s["split"], next_b * 4 + max(2 * m + k - 1, 0) + 1)
                    if k:
                        i = act.activation(full[1][:, :], SH[:, :], ACT.Identity, bias=bk[:, m:m + 1])
                    else:
                        i = act.activation(full[0][:, :], SH[:, :], ACT.Identity, scale=SCALE, bias=bq[:, m:m + 1])
                i.then_inc(s["shared_free"], 1)

            def evacuate(ph, b, g):
                act.wait_ge(s["pv_done"], b * NG * SL + (g + 1) * SL + 1)
                if g < 0 or ph.kind == "epilogue":
                    act.wait_ge(s["pe_shared"], ph.base + 1)
                elif ph.has((g, 2, "ctx")):
                    act.wait_ge(s["pe_shared"], ph.number((g, 2, "ctx")) + 1)
                act.activation(ctxu[:, :], bank[PVB][:, :], ACT.Copy).then_inc(s["evac"], 1)

            def body(ph):
                b = ph.b
                if ph.kind == "prologue":
                    for what in PREP:
                        shared(ph, (0, 0, what), 0)
                    shared(ph, (0, 1, "neg"), 0)
                    return
                if ph.kind == "epilogue":
                    evacuate(ph, b - 1, NG - 1)
                    for use in BEFORE:
                        shared(ph, use, 0)
                    return
                for g in range(NG):
                    for st in range(SL):
                        for i in range(GH):
                            u = (g * SL + st) * GH + i
                            act.wait_ge(s["pe_exp"], b * UNITS + u + 1 + 1)
                            if i == 0:
                                act.wait_ge(s["pv_done"], (b * NG * SL + g * SL + st - 1 if not (ph.first and g * SL + st < 1) else 0) + 1)
                            act.activation(E[:, u % PRING, :], bank[EXPB[u % RING]][:, :], ACT.Exp).then_inc(s["exp_done"], 1)
                            if st == 1 and i == 0 and not (ph.first and g == 0):
                                evacuate(ph, b, g - 1)
                            for use in READ_AT.get((g, st, i), ()):
                                shared(ph, use, b + 1)
                        if (g, st) == (2, 2):
                            act.wait_ge(s["lmax"], b + 1 + 1)
                            act.activation(pe_[:, :], lgt[:, :], ACT.Exp, bias=lmx[:, :], accum_out=psm[:, :]).then_inc(s["pexp"], 1)
            phases(act, body)

        @block.vector
        def _(dve):
            def statistics(n, t, c):
                dve.bn_stats(bst[:, t, :], X1[:, bass.ds(n * TT + t, 1), :].rearrange("p o d -> p (o d)")).then_inc(s["c_dve_ln"], c.up())

            def variance(n, c):
                dve.wait_ge(s["c_dve_ln"], c.now())
                dve.tensor_tensor(mean[:, :], bst[:, :, 1], bst[:, :, 4], ALU.add).then_inc(s["c_dve_ln"], c.up())
                dve.tensor_tensor(dmean[:, :], bst[:, :, 1], bst[:, :, 4], ALU.subtract).then_inc(s["c_dve_ln"], c.up())
                dve.tensor_tensor(vs[:, :], bst[:, :, 2], bst[:, :, 5], ALU.add).then_inc(s["c_dve_ln"], c.up())
                dve.wait_ge(s["c_dve_ln"], c.now())
                dve.tensor_scalar(mean[:, :], mean[:, :], 0.5, None, ALU.mult).then_inc(s["c_dve_ln"], c.up())
                dve.tensor_tensor(dmean[:, :], dmean[:, :], dmean[:, :], ALU.mult).then_inc(s["c_dve_ln"], c.up())
                dve.tensor_scalar(vs[:, :], vs[:, :], 1.0 / D, EPS_LN2, ALU.mult, ALU.add).then_inc(s["c_dve_ln"], c.up())
                dve.wait_ge(s["c_dve_ln"], c.now())
                dve.scalar_tensor_tensor(vs[:, :], dmean[:, :], 0.25, vs[:, :], ALU.mult, ALU.add).then_inc(s["var"], 1)
                c.end()

            def normalize(n, t):
                if t == 0:
                    dve.wait_ge(s["lrs"], n + 1 + 1)
                dve.tensor_scalar(xh[:, t, :], X1[:, bass.ds(n * TT + t, 1), :].rearrange("p o d -> p (o d)"),
                                  mean[:, t:t + 1], lrs[:, t:t + 1], ALU.subtract, ALU.mult).then_inc(s["xh"], 1)

            def shared(ph, use, next_b):
                if not ph.has(use):
                    return
                what, b = use[2], ph.b
                if what == "ctx":
                    dve.wait_ge(s["pe_shared"], ph.number(use) + 1)
                    n = b * NG + use[0] - 1
                    g = (use[0] - 1) % NG
                    c = Count(n, CTX_STEPS)
                    sh = SH[:, :].rearrange("p (t h c) -> p t h c", t=TT, h=GH)
                    dve.reciprocal(rl_[:, :, :], sh[:, :, :, KD]).then_inc(s["c_dve_ctx"], c.up())
                    dve.wait_ge(s["c_dve_ctx"], c.now())
                    hs = (g % GM) * GH
                    dve.tensor_tensor(ctxn[:, g // GM, :, hs:hs + GH, :], sh[:, :, :, 0:KD], spread(rl_[:, :, :], KD), ALU.mult).then_inc(s["shared_free"], 1)
                    c.end()
                elif what == "wo":
                    dve.wait_ge(s["pe_shared"], ph.number(use) + 1)
                    dve.wait_ge(s["x2"], (b - 1 if not isinstance(b, int) or b > 0 else 0) + 1)
                    dve.tensor_tensor(t1[:, :, :], SH[:, :].rearrange("p (t d) -> p t d", t=TT), X1[:, bass.ds((b - 1) * TT, TT), :], ALU.add).then_inc(s["shared_free"], 1)
                    dve.wait_ge(s["shared_free"], ph.number(use) + 1)
                    dve.tensor_tensor(X[:, bass.ds((b - 1) * TT, TT), :], t1[:, :, :], bop[:, :].unsqueeze(1).to_broadcast([P, TT, D]), ALU.add).then_inc(s["x2"], 1)
                elif what == "logits":
                    dve.wait_ge(s["pe_shared"], ph.number(use) + 1)
                    dve.tensor_tensor(lgt[:, :], SH[:, 0:MX], rb[:, :], ALU.add).then_inc(s["shared_free"], 1)
                elif what[0] == "v":
                    dve.wait_ge(s["pe_shared"], ph.number(use) + 1)
                    dve.wait_ge(s["v_filled"], MX * next_b + 1)
                    dve.tensor_tensor(vtmp[:, int(what[1])].rearrange("p h k -> p (h k)"), SH[:, 0:MX * H * KD], bv[:, :], ALU.add).then_inc(s["shared_free"], 1)

            def max_unit(b, g, i, at):
                u = b * UNITS + g * 16 + i
                if i == 0:
                    n = b * NG + g
                    dve.wait_ge(s["neg_ready"], (n - 1 if not (isinstance(b, int) and n < 1) else 0) + 1)
                dve.wait_ge(s["pe_max"], u + 1 + 1)
                dve.tensor_reduce(top[:, g % 2, i:i + 1], bank[MAXB[at % len(MAXB)]][:, :], AX.X, ALU.max).then_inc(s["max_read"], 1)

            def body(ph):
                b = ph.b
                if ph.kind == "prologue":
                    ln_steps = Count(0, LN_STEPS)
                    for t in range(TT):
                        statistics(0, t, ln_steps)
                    variance(0, ln_steps)
                    for t in range(TT):
                        normalize(0, t)
                    for what in PREP:
                        shared(ph, (0, 0, what), 0)
                    for g in range(2):
                        for i in range(16):
                            max_unit(0, g, i, g * 16 + i)
                    return
                if ph.kind == "epilogue":
                    for use in BEFORE:
                        shared(ph, use, 0)
                    return
                ln_steps = Count(b + 1, LN_STEPS)
                for g in range(NG):
                    for st in range(SL):
                        for i in range(GH):
                            if not (ph.last and g + 2 >= NG):
                                max_unit(b, g + 2, st * GH + i, g * 16 + st * GH + i)
                            for use in READ_AT.get((g, st, i), ()):
                                shared(ph, use, b + 1)
                            if not ph.last and i == GH - 1:
                                if g == 0:
                                    statistics(b + 1, st, ln_steps)
                                if (g, st) == (1, 0):
                                    variance(b + 1, ln_steps)
                            if not ph.last and (g, st) == (1, 2):
                                normalize(b + 1, i)
                        c = Count(b, P_STEPS)
                        if (g, st) == (2, 1):
                            dve.tensor_reduce(lmx[:, :], lgt[:, :], AX.X, ALU.max, negate=True).then_inc(s["lmax"], 1)
                        if (g, st) == (2, 3):
                            dve.wait_ge(s["pexp"], b + 1 + 1)
                            dve.reciprocal(psm[:, :], psm[:, :]).then_inc(s["c_dve_p"], c.up())
                            dve.wait_ge(s["c_dve_p"], c.now())
                            dve.tensor_scalar(pr[:, :], pe_[:, :], psm[:, :], None, ALU.mult).then_inc(s["c_dve_p"], c.up())
                            dve.wait_ge(s["c_dve_p"], c.now())
                            dve.tensor_scalar(bop[:, :], bo[:, 0, :], pr[:, 0:1], None, ALU.mult).then_inc(s["c_dve_p"], c.up())
                            dve.wait_ge(s["c_dve_p"], c.now())
                            dve.scalar_tensor_tensor(bop[:, :], bo[:, 1, :], pr[:, 1:2], bop[:, :], ALU.mult, ALU.add).then_inc(s["pr"], 1)
                            c.end()
            phases(dve, body)

        @block.gpsimd
        def _(pool):
            def negate(n, par):
                c = Count(n, NEG_STEPS)
                count = in_register(pool, 16 * (n + 1) + 1)
                pool.wait_ge(*met)
                pool.wait_ge(s["max_read"], count)
                pool.tensor_scalar(negr[:, par, :], top[:, par, :], -1.0, 0.0, ALU.mult, ALU.add).then_inc(s["c_pool_neg"], c.up())
                pool.tensor_scalar(neg[:, par, 0, :], top[:, par, :], -1.0, 0.0, ALU.mult, ALU.add).then_inc(s["c_pool_neg"], c.up())
                count = in_register(pool, c.now())
                pool.wait_ge(*met)
                pool.wait_ge(s["c_pool_neg"], count)
                pool.tensor_tensor(negr[:, par, :], negr[:, par, :], neg[:, par, 0, :], ALU.subtract).then_inc(s["c_pool_neg"], c.up())
                count = in_register(pool, c.now())
                pool.wait_ge(*met)
                pool.wait_ge(s["c_pool_neg"], count)
                pool.tensor_scalar(neg[:, par, 1, :], negr[:, par, :], 1.0, 0.0, ALU.mult, ALU.add).then_inc(s["c_pool_neg"], c.up())
                count = in_register(pool, c.now())
                pool.wait_ge(*met)
                pool.wait_ge(s["c_pool_neg"], count)
                pool.tensor_tensor(neg[:, par, 2, :], negr[:, par, :], neg[:, par, 1, :], ALU.subtract).then_inc(s["neg_ready"], 1)
                c.end()

            def split(ph, use, n):
                m, k = int(use[2][1]), int(use[2][0] == "k")
                c = Count(n * 4 + 2 * m + k, SPLIT_STEPS)
                count = in_register(pool, ph.number(use) + 1)
                pool.wait_ge(*met)
                pool.wait_ge(s["shared_free"], count)
                count = in_register(pool, 16 * 2 * len(PAIRS) * n + 1)
                pool.wait_ge(*met)
                pool.wait_ge(s[f"stack{m}"], count)
                a, f = parts[m][k], full[k]
                pool.tensor_scalar(a[:, 0, :], f[:, :], 1.0, 0.0, ALU.mult, ALU.add).then_inc(s["c_pool_split"], c.up())
                count = in_register(pool, c.now())
                pool.wait_ge(*met)
                pool.wait_ge(s["c_pool_split"], count)
                pool.tensor_tensor(rest[:, :], f[:, :], a[:, 0, :], ALU.subtract).then_inc(s["c_pool_split"], c.up())
                count = in_register(pool, c.now())
                pool.wait_ge(*met)
                pool.wait_ge(s["c_pool_split"], count)
                pool.tensor_scalar(a[:, 1, :], rest[:, :], 1.0, 0.0, ALU.mult, ALU.add).then_inc(s["c_pool_split"], c.up())
                count = in_register(pool, c.now())
                pool.wait_ge(*met)
                pool.wait_ge(s["c_pool_split"], count)
                pool.tensor_tensor(a[:, 2, :], rest[:, :], a[:, 1, :], ALU.subtract).then_inc(s["split"], 1)
                c.end()

            def fill_v(m, n, used):
                if used is not None:
                    count = in_register(pool, used + 1)
                    pool.wait_ge(*met)
                    pool.wait_ge(s["pv_done"], count)
                hs = slice(m * H, (m + 1) * H)
                pool.tensor_scalar(V[:, :, hs, 0:KD], vtmp[:, :, hs, :], 1.0, 0.0, ALU.mult, ALU.add).then_inc(s["v_filled"], 1)

            def rsqrt(n):
                count = in_register(pool, n + 1 + 1)
                pool.wait_ge(*met)
                pool.wait_ge(s["var"], count)
                pool.tensor_tensor(lrs[:, :], vs[:, :], T["mhalf"][:, 0:TT], ALU.pow).then_inc(s["lrs"], 1)

            def mean_tokens(ph, use, n):
                count = in_register(pool, ph.number(use) + 1)
                pool.wait_ge(*met)
                pool.wait_ge(s["shared_free"], count)
                pool.tensor_scalar(nmat[:, :], T["ones"][:, :], msum[:, :], 1.0 / L, ALU.mult, ALU.mult).then_inc(s["nmat"], 1)

            def x1_sum(n):
                count = in_register(pool, n + 1 + 1)
                pool.wait_ge(*met)
                pool.wait_ge(s["x2"], count)
                xs = bass.ds(n * TT, TT)
                pool.tensor_tensor(X1[:, xs, :], X1[:, xs, :], X[:, xs, :], ALU.add).then_inc(s["x1_sum"], 1)

            def body(ph):
                b = ph.b
                if ph.kind == "prologue":
                    rsqrt(0)
                    mean_tokens(ph, (0, 0, "xT"), 0)
                    for what in ("q0", "k0"):
                        split(ph, (0, 0, what), 0)
                    count = in_register(pool, ph.number((0, 0, "v3")) + 1)
                    pool.wait_ge(*met)
                    pool.wait_ge(s["shared_free"], count)
                    for m in range(MX):
                        fill_v(m, 0, None)
                    for what in ("q1", "k1"):
                        split(ph, (0, 0, what), 0)
                    negate(0, 0)
                    return
                if ph.kind == "epilogue":
                    x1_sum(b - 1)
                    return
                for g in range(NG):
                    if not (ph.last and g == NG - 1):
                        negate(b * NG + g + 1, (g + 1) % 2)
                    if g == 1 and not ph.last:
                        rsqrt(b + 1)
                    if g == 1 and not ph.first:
                        fill_v(1, b, b * NG * SL)
                        x1_sum(b - 1)
                    if g == 2 and not ph.last:
                        mean_tokens(ph, (1, 3, "xT"), b + 1)
                        split(ph, (2, 0, "q0"), b + 1)
                    if g == 3:
                        if not ph.last:
                            split(ph, (2, 3, "k0"), b + 1)
                        count = in_register(pool, b + 1 + 1)
                        pool.wait_ge(*met)
                        pool.wait_ge(s["pr"], count)
                        if not ph.first:
                            count = in_register(pool, ph.number((1, 0, "wo")) + 1)
                            pool.wait_ge(*met)
                            pool.wait_ge(s["shared_free"], count)
                        for m in range(MX):
                            i = pool.tensor_scalar(wop[:, m, :], wo[:, m, :], pr[:, m:m + 1], 0.0, ALU.mult, ALU.add)
                        i.then_inc(s["wop"], 1)
                    if g == 5 and not ph.last:
                        count = in_register(pool, ph.number((5, 0, "v3")) + 1)
                        pool.wait_ge(*met)
                        pool.wait_ge(s["shared_free"], count)
                        fill_v(0, b + 1, b * NG * SL + GM * SL)
                    if g == 6 and not ph.last:
                        split(ph, (5, 3, "q1"), b + 1)
                        split(ph, (6, 0, "k1"), b + 1)
            phases(pool, body)

        @block.sync
        def _(sp):
            def fill(m, n, used):
                count = in_register(sp, 4 * n + 2 * m + 2 + 1)
                sp.wait_ge(*met)
                sp.wait_ge(s["split"], count)
                if used is not None:
                    count = in_register(sp, used + 1)
                    sp.wait_ge(*met)
                    sp.wait_ge(s["pv_done"], count)
                for i, stack in enumerate((Q[m], K[m])):
                    for j, pair in enumerate(PAIRS):
                        src = parts[m][i][:, pair[i], :]
                        sp.dma_start(stack[j * KD:(j + 1) * KD, :, :], src).then_inc(s[f"stack{m}"], 16)

            def send(ph, use, n, g):
                count = in_register(sp, ph.number(use) + 1)
                sp.wait_ge(*met)
                sp.wait_ge(s["shared_free"], count)
                count = in_register(sp, 16 * n + 1)
                sp.wait_ge(*met)
                sp.wait_ge(s["neg_rows"], count)
                m, h = (g % NG) // GM, (g % GM) * GH
                dst = Q[m][QROWS:QROWS + MROWS, h:h + GH, :].rearrange("a h (t p) -> a (h t) p", p=P)
                sp.dma_start(dst, negT[:, g % 2, :]).then_inc(s["neg_rows"], 16)

            def body(ph):
                b = ph.b
                if ph.kind == "prologue":
                    for m in range(MX):
                        fill(m, 0, None)
                    send(ph, (0, 1, "neg"), 0, 0)
                    return
                if ph.kind == "epilogue":
                    return
                for g in range(NG):
                    if ph.has((g, 1, "neg")):
                        send(ph, (g, 1, "neg"), b * NG + g + 1, g + 1)
                    if g == 0 and not ph.first:
                        fill(1, b, b * NG * SL)
                    if g == 4 and not ph.last:
                        fill(0, b + 1, b * NG * SL + GM * SL)
            phases(sp, body)


NE, TOP = 8, 2
FE = 2
HB = TOP * FE


def build_experts(nc, ctx, T, dram, out):
    def sb(name, shape, dt=FP32):
        return ctx.enter_context(nc.sbuf_tensor(name, shape, dt))

    X, X1, bank, ident, ones = T["X"], T["X1"], T["bank"], T["ident"], T["ones"]
    rw, rb, ln = T["f_rw"], T["f_rb"], T["f_ln"]
    bst = sb("f_bst", [P, B * TT, 6]); mean = sb("f_mean", [P, B * TT]); dmean = sb("f_dmean", [P, B * TT])
    vs = sb("f_vs", [P, B * TT]); rs = sb("f_rs", [P, B * TT])
    xh = sb("f_xh", [P, 2, TT, D]); n2T = sb("f_n2T", [P, B, L]); msum = sb("f_msum", [P, B]); mtok = sb("f_mtok", [P, B])
    lg = sb("f_lg", [B, NE]); lmx = sb("f_lmx", [B, 1]); pexp = sb("f_pexp", [B, NE]); psm = sb("f_psm", [B, 1]); pr = sb("f_pr", [B, NE])
    best = sb("f_best", [B, 8]); which = sb("f_which", [B, 8], mybir.dt.uint32); bsum = sb("f_bsum", [B, 1]); share = sb("f_share", [B, TOP])
    diag = sb("f_diag", [B, B, TOP]); weight = sb("f_weight", [P, B * TOP]); chosen = sb("f_chosen", [1, B * TOP], mybir.dt.uint32)
    w1 = sb("f_w1", [P, 2, TOP, FE * P]); w2 = sb("f_w2", [P, 2, TOP, FE, D]); w2p = sb("f_w2p", [P, 2, HB, D])
    hid = sb("f_hid", [P, 2, HB, L]); y = sb("f_y", [P, TT, D]); res = sb("f_res", [P, 2, TT, D])
    bst_y = sb("f_bst_y", [P, TT, 6]); mean_y = sb("f_mean_y", [P, TT]); dmean_y = sb("f_dmean_y", [P, TT])
    vs_y = sb("f_vs_y", [P, TT]); rs_y = sb("f_rs_y", [P, TT])

    names = ["stats", "var", "rs", "xh", "pe_T", "n2T", "mtok", "pe_lg", "lmx", "pexp", "which", "chosen", "diag", "pe_weight", "weight",
             "w1_in0", "w1_in1", "w2_in0", "w2_in1", "w2p", "pe_up", "gelu", "pe_down", "y", "yvar", "yrs", "res",
             "stored0", "stored1", "c_var", "c_pick", "c_y"]
    s = {n: ctx.enter_context(nc.semaphore("f_" + n)) for n in names}
    met = (T["masks"], 8)

    with nc.Block() as block:
        @block.gpsimd
        def _(pool):
            for started in s.values():
                pool.sem_inc(started, 1)
            pool.wait_ge(T["later"], 16 * T["later_loads"])

    def rows(ap, n):
        return ap[:, bass.ds(n, 1), :].rearrange("p o d -> p (o d)")

    def combine(dve, b_, m_, d_, v_, eps, counted, chain, name):
        dve.tensor_tensor(m_, b_[:, :, 1], b_[:, :, 4], ALU.add).then_inc(s[counted], chain.up())
        dve.tensor_tensor(d_, b_[:, :, 1], b_[:, :, 4], ALU.subtract).then_inc(s[counted], chain.up())
        dve.tensor_tensor(v_, b_[:, :, 2], b_[:, :, 5], ALU.add).then_inc(s[counted], chain.up())
        dve.wait_ge(s[counted], chain.now())
        dve.tensor_scalar(m_, m_, 0.5, None, ALU.mult).then_inc(s[counted], chain.up())
        dve.tensor_tensor(d_, d_, d_, ALU.mult).then_inc(s[counted], chain.up())
        dve.tensor_scalar(v_, v_, 1.0 / D, eps, ALU.mult, ALU.add).then_inc(s[counted], chain.up())
        dve.wait_ge(s[counted], chain.now())
        dve.scalar_tensor_tensor(v_, d_, 0.25, v_, ALU.mult, ALU.add).then_inc(s[name], 1)

    def used(b):
        return 1 if isinstance(b, int) and b < 2 else b

    with nc.Block() as block:
        @block.vector
        def _(dve):
            with dve.Fori(0, B) as b:
                for t in range(TT):
                    dve.bn_stats(bst[:, bass.ds(b * TT + t, 1), :].rearrange("p o c -> p (o c)"), rows(X, b * TT + t)).then_inc(s["stats"], 1)
            c = Count(0, 6)
            dve.wait_ge(s["stats"], B * TT + 1)
            combine(dve, bst, mean[:, :], dmean[:, :], vs[:, :], EPS_LN2, "c_var", c, "var")
            c.end()
            dve.wait_ge(s["rs"], 2)

            def normalize(b, par):
                dve.wait_ge(s["pe_T"], used(b))
                for t in range(TT):
                    n = bass.ds(b * TT + t, 1)
                    last = dve.tensor_scalar(xh[:, par, t, :], rows(X, b * TT + t), mean[:, n], rs[:, n], ALU.subtract, ALU.mult)
                last.then_inc(s["xh"], 1)
            normalize(0, 0)
            normalize(1, 1)
            with dve.Fori(1, B // 2) as q:
                normalize(2 * q, 0)
                normalize(2 * q + 1, 1)

            c = Count(0, 9)
            dve.wait_ge(s["n2T"], B + 1)
            dve.tensor_scalar(mtok[:, :], msum[:, :], 1.0 / L, None, ALU.mult).then_inc(s["mtok"], 1)
            dve.wait_ge(s["pe_lg"], 2)
            dve.tensor_tensor(lg[:, :], bank[2][0:B, 0:NE], rb[0:B, :], ALU.add).then_inc(s["c_pick"], c.up())
            dve.wait_ge(s["c_pick"], c.now())
            dve.tensor_reduce(lmx[:, :], lg[:, :], AX.X, ALU.max, negate=True).then_inc(s["lmx"], 1)
            dve.wait_ge(s["pexp"], 2)
            dve.reciprocal(psm[:, :], psm[:, :]).then_inc(s["c_pick"], c.up())
            dve.wait_ge(s["c_pick"], c.now())
            dve.tensor_scalar(pr[:, :], pexp[:, :], psm[:, :], None, ALU.mult).then_inc(s["c_pick"], c.up())
            dve.wait_ge(s["c_pick"], c.now())
            dve.max(best[:, :], pr[:, :]).then_inc(s["c_pick"], c.up())
            dve.wait_ge(s["c_pick"], c.now())
            dve.max_index(which[:, :], best[:, :], pr[:, :]).then_inc(s["which"], 1)
            dve.tensor_tensor(bsum[:, :], best[:, 0:1], best[:, 1:2], ALU.add).then_inc(s["c_pick"], c.up())
            dve.wait_ge(s["c_pick"], c.now())
            dve.reciprocal(bsum[:, :], bsum[:, :]).then_inc(s["c_pick"], c.up())
            dve.wait_ge(s["c_pick"], c.now())
            dve.tensor_scalar(share[:, :], best[:, 0:TOP], bsum[:, :], None, ALU.mult).then_inc(s["c_pick"], c.up())
            dve.wait_ge(s["c_pick"], c.now())
            dve.tensor_tensor(diag[:, :, :], share[:, :].unsqueeze(1).to_broadcast([B, B, TOP]), spread(ident[0:B, 0:B], TOP), ALU.mult).then_inc(s["diag"], 1)
            dve.wait_ge(s["pe_weight"], 2)
            dve.tensor_copy(weight[:, :], bank[3][:, 0:B * TOP]).then_inc(s["weight"], 1)

            def sum_and_normalize(b, par, q):
                c = Count(b, 10)
                dve.wait_ge(s["pe_down"], b + 2)
                dve.wait_ge(s["res"], b + 1)
                dve.tensor_tensor(y[:, :, :], bank[4 + par][:, :].rearrange("p (t d) -> p t d", t=TT), X1[:, bass.ds(b * TT, TT), :], ALU.add).then_inc(s["y"], 1)
                dve.wait_ge(s["y"], b + 2)
                for t in range(TT):
                    dve.bn_stats(bst_y[:, t, :], y[:, t, :]).then_inc(s["c_y"], c.up())
                dve.wait_ge(s["c_y"], c.now())
                combine(dve, bst_y, mean_y[:, :], dmean_y[:, :], vs_y[:, :], EPS_LN, "c_y", c, "yvar")
                c.end()
                dve.wait_ge(s["yrs"], b + 2)
                dve.wait_ge(s[f"stored{par}"], 16 * q + 1)
                for t in range(TT):
                    last = dve.tensor_scalar(res[:, par, t, :], y[:, t, :], mean_y[:, t:t + 1], rs_y[:, t:t + 1], ALU.subtract, ALU.mult)
                last.then_inc(s["res"], 1)
            with dve.Fori(0, B // 2) as q:
                sum_and_normalize(2 * q, 0, q)
                sum_and_normalize(2 * q + 1, 1, q)

        @block.gpsimd
        def _(pool):
            def weigh(b, par, q):
                count = in_register(pool, 32 * (q + 1) + 1)
                pool.wait_ge(*met)
                pool.wait_ge(s[f"w2_in{par}"], count)
                count = in_register(pool, used(b))
                pool.wait_ge(*met)
                pool.wait_ge(s["pe_down"], count)
                for e in range(TOP):
                    share_of_e = weight[:, bass.ds(b * TOP + e, 1)].unsqueeze(2).to_broadcast([P, FE, D])
                    last = pool.tensor_tensor(w2p[:, par, e * FE:(e + 1) * FE, :], w2[:, par, e], share_of_e, ALU.mult)
                last.then_inc(s["w2p"], 1)

            def scale(b):
                count = in_register(pool, b + 2)
                pool.wait_ge(*met)
                pool.wait_ge(s["yvar"], count)
                pool.tensor_tensor(rs_y[:, :], vs_y[:, :], T["mhalf"][:, 0:TT], ALU.pow).then_inc(s["yrs"], 1)

            pool.wait_ge(s["var"], 2)
            pool.tensor_tensor(rs[:, :], vs[:, :], T["mhalf"][:, 0:1].to_broadcast([P, B * TT]), ALU.pow).then_inc(s["rs"], 1)
            pool.wait_ge(s["weight"], 2)
            weigh(0, 0, 0)
            weigh(1, 1, 0)
            with pool.Fori(1, B // 2) as q:
                for par in range(2):
                    scale(2 * q + par - 2)
                    weigh(2 * q + par, par, q)
            for b in range(B - 2, B):
                scale(b)

        @block.scalar
        def _(act):
            def transposed(b, par, q):
                act.wait_ge(s["pe_T"], b + 2)
                act.activation(rows(n2T, b), bank[par][:, :], ACT.Identity, scale=ln[:, 0:1], bias=ln[:, 1:2], accum_out=msum[:, bass.ds(b, 1)]).then_inc(s["n2T"], 1)
            with act.Fori(0, B // 2) as q:
                transposed(2 * q, 0, q)
                transposed(2 * q + 1, 1, q)
            act.wait_ge(s["lmx"], 2)
            act.activation(pexp[:, :], lg[:, :], ACT.Exp, bias=lmx[:, :], accum_out=psm[:, :]).then_inc(s["pexp"], 1)

            def gelu(b, par, q):
                act.wait_ge(s["pe_down"], used(b))
                for j in range(HB):
                    act.wait_ge(s["pe_up"], b * HB + j + 2)
                    act.activation(hid[:, par, j, :], bank[j][:, :], ACT.Gelu).then_inc(s["gelu"], 1)
            gelu(0, 0, 0)
            gelu(1, 1, 0)
            with act.Fori(1, B // 2) as q:
                gelu(2 * q, 0, q)
                gelu(2 * q + 1, 1, q)

        @block.tensor
        def _(pe):
            def transpose_tokens(b, par, q):
                pe.wait_ge(s["xh"], b + 2)
                pe.wait_ge(s["n2T"], used(b))
                for t in range(TT):
                    last = pe.transpose(bank[par][:, t * P:(t + 1) * P], xh[:, par, t, :], ident[:, :])
                last.then_inc(s["pe_T"], 1)
            transpose_tokens(0, 0, 0)
            transpose_tokens(1, 1, 0)
            with pe.Fori(1, B // 2) as q:
                transpose_tokens(2 * q, 0, q)
                transpose_tokens(2 * q + 1, 1, q)
            pe.wait_ge(s["mtok"], 2)
            pe.matmul(bank[2][0:B, 0:NE], mtok[:, :], rw[:, :], start=True, stop=True).then_inc(s["pe_lg"], 1)
            pe.wait_ge(s["diag"], 2)
            pe.matmul(bank[3][:, 0:B * TOP], ones[0:B, :], diag[:, :, :].rearrange("s b e -> s (b e)"), start=True, stop=True).then_inc(s["pe_weight"], 1)
            pe.wait_ge(s["weight"], 2)

            def up(b, par, q):
                pe.wait_ge(s[f"w1_in{par}"], 32 * (q + 1) + 1)
                for j in range(HB):
                    if not (isinstance(b, int) and b == 0):
                        pe.wait_ge(s["gelu"], (b - 1) * HB + j + 2)
                    pe.matmul(bank[j][:, :], w1[:, par, j // FE, (j % FE) * P:(j % FE + 1) * P], rows(n2T, b), start=True, stop=True).then_inc(s["pe_up"], 1)

            def down(b, par):
                pe.wait_ge(s["gelu"], (b + 1) * HB + 1)
                pe.wait_ge(s["w2p"], b + 2)
                pe.wait_ge(s["y"], used(b))
                for t in range(TT):
                    for j in range(HB):
                        last = pe.matmul(bank[4 + par][:, t * P:(t + 1) * P], hid[:, par, j, t * P:(t + 1) * P], w2p[:, par, j, :], start=j == 0, stop=j == HB - 1)
                last.then_inc(s["pe_down"], 1)
            up(0, 0, 0)
            up(1, 1, 0)
            down(0, 0)
            with pe.Fori(1, B // 2) as q:
                up(2 * q, 0, q)
                down(2 * q - 1, 1)
                up(2 * q + 1, 1, q)
                down(2 * q, 0)
            down(B - 1, 1)

        @block.sync
        def _(sp):
            sp.wait_ge(s["which"], 2)
            sp.dma_start(chosen[:, :], which[:, 0:TOP]).then_inc(s["chosen"], 16)
            sp.wait_ge(s["chosen"], 17)

            def load(b, par, q):
                if not isinstance(b, int):
                    count = in_register(sp, (b - 1) * HB + 1)
                    sp.wait_ge(*met)
                    sp.wait_ge(s["pe_up"], count)
                    count = in_register(sp, b)
                    sp.wait_ge(*met)
                    sp.wait_ge(s["w2p"], count)
                for e in range(TOP):
                    at = chosen[0:1, b * TOP + e:b * TOP + e + 1] if isinstance(b, int) else chosen[0:1, bass.ds(b * TOP + e, 1)]
                    x = sp.value_load(at, min_val=0, max_val=NE - 1)
                    sp.dma_start(w1[:, par, e, :], dram["fw1"][bass.ds(x, 1), :, :].rearrange("o d f -> d (o f)")).then_inc(s[f"w1_in{par}"], 16)
                    sp.dma_start(w2[:, par, e], dram["fw2"][bass.ds(x, 1), :, :].rearrange("o (j p) d -> p (o j) d", p=P)).then_inc(s[f"w2_in{par}"], 16)

            def store(b, par, q):
                count = in_register(sp, b + 2)
                sp.wait_ge(*met)
                sp.wait_ge(s["res"], count)
                sp.dma_start(out[bass.ds(b, 1), :, :].rearrange("o (t p) d -> p (o t) d", p=P), res[:, par]).then_inc(s[f"stored{par}"], 16)
            load(0, 0, 0)
            load(1, 1, 0)
            with sp.Fori(1, B // 2) as q:
                for par in range(2):
                    load(2 * q + par, par, q)
                    store(2 * q + par - 2, par, q - 1)
            for par in range(2):
                store(B - 2 + par, par, B // 2 - 1)
            for par in range(2):
                sp.wait_ge(s[f"stored{par}"], 16 * (B // 2) + 1)


def build(nc, dram, out):
    with ExitStack() as ctx:
        def sb(name, shape, dt=FP32):
            return ctx.enter_context(nc.sbuf_tensor(name, shape, dt))
        T = {"X": sb("X", [P, B * TT, D]), "ident": sb("ident", [P, P]), "tri": sb("tri", [P, P]),
             "above": sb("above", [P, P]), "ones": sb("ones", [P, P]), "mhalf": sb("mhalf", [P, TT])}
        T["bank"] = [ctx.enter_context(nc.psum_tensor(f"bank{i}", [P, 512], FP32)) for i in range(8)]
        T["x_loaded"] = ctx.enter_context(nc.semaphore("x_loaded"))
        T["masks"] = ctx.enter_context(nc.semaphore("masks"))

        T["later"] = ctx.enter_context(nc.semaphore("later_weights"))
        raw, wv, wo = sb("raw", [P, 2, MX, H * KD]), sb("wv", [P, MX, H * KD]), sb("wo", [P, MX, D])
        bq, bk, bv, bo = sb("bq", [P, MX]), sb("bk", [P, MX]), sb("bv", [P, MX * H * KD]), sb("bo", [P, MX, D])
        rw, rb, ln1 = sb("rw", [P, MX]), sb("rb", [P, MX]), sb("ln1", [P, 2])
        f_rw, f_rb, f_ln = sb("f_rw", [P, NE]), sb("f_rb", [P, NE]), sb("f_ln", [P, 2])
        T.update(raw=raw, wv=wv, wo=wo, bq=bq, bk=bk, bv=bv, bo=bo, rw=rw, rb=rb, ln1=ln1, f_rw=f_rw, f_rb=f_rb, f_ln=f_ln)
        loads = []
        for m in range(MX):
            loads += [(raw[:, 0, m, :], dram["wq"][m].rearrange("d h k -> d (h k)")),
                      (raw[:, 1, m, :], dram["wk"][m].rearrange("d h k -> d (h k)")),
                      (wv[:, m, :], dram["wv"][m].rearrange("d h k -> d (h k)")),
                      (wo[:, m, :], dram["wo"][m].rearrange("h k d -> (h k) d")),
                      (bq[:, m:m + 1], dram["bq"][m].rearrange("h k -> k h")),
                      (bk[:, m:m + 1], dram["bk"][m].rearrange("h k -> k h")),
                      (bo[:, m, :], dram["bo"][m].partition_broadcast(P))]
        loads += [(bv[:, :], dram["bv"].rearrange("m h k -> (m h k)").partition_broadcast(P)),
                  (rw[:, :], dram["rw"]), (rb[:, :], dram["rb"].partition_broadcast(P)),
                  (ln1[:, 0:1], dram["ln1_g"].rearrange("(p o) -> p o", o=1)), (ln1[:, 1:2], dram["ln1_b"].rearrange("(p o) -> p o", o=1)),
                  (f_rw[:, :], dram["f_rw"]), (f_rb[:, :], dram["f_rb"].partition_broadcast(P)),
                  (f_ln[:, 0:1], dram["ln2_g"].rearrange("(p o) -> p o", o=1)), (f_ln[:, 1:2], dram["ln2_b"].rearrange("(p o) -> p o", o=1))]
        T["later_loads"] = len(loads)
        with ExitStack() as inner:
            build_mamba(nc, inner, T, dram, loads)
        T["X1"] = T["X"]
        T["X"] = sb("X2", [P, B * TT, D])
        with ExitStack() as inner:
            build_attention(nc, inner, T)
        with ExitStack() as inner:
            build_experts(nc, inner, T, dram, out)


_INS = {'x': 'L0_attn_x', 'w_in': 'L0_attn_w_in', 'conv_w': 'L0_attn_conv_w', 'conv_b': 'L0_attn_conv_b', 'dt_bias': 'L0_attn_dt_bias',
        'a_log': 'L0_attn_a_log', 'd_skip': 'L0_attn_d_skip', 'norm_w': 'L0_attn_norm_w', 'w_out': 'L0_attn_w_out', 'w_fc': 'L0_attn_w_fc', 'w_proj': 'L0_attn_w_proj',
        'ln1_g': 'L0_ffn_ln1_g', 'ln1_b': 'L0_ffn_ln1_b', 'wq': 'L0_ffn_mha_wq', 'wk': 'L0_ffn_mha_wk', 'wv': 'L0_ffn_mha_wv', 'wo': 'L0_ffn_mha_wo',
        'bq': 'L0_ffn_mha_bq', 'bk': 'L0_ffn_mha_bk', 'bv': 'L0_ffn_mha_bv', 'bo': 'L0_ffn_mha_bo', 'rw': 'L0_ffn_mha_rw', 'rb': 'L0_ffn_mha_rb',
        'ln2_g': 'L0_ffn_ln2_g', 'ln2_b': 'L0_ffn_ln2_b', 'f_rw': 'L0_ffn_ffn_rw', 'f_rb': 'L0_ffn_ffn_rb', 'fw1': 'L0_ffn_fw1', 'fw2': 'L0_ffn_fw2'}


def kernel(**inputs):
    import numpy as _np
    import concourse.bacc as _bacc
    from concourse import mybir as _mybir
    from concourse.bass_utils import run_bass_kernel_spmd as _run

    nc = _bacc.Bacc("TRN2", target_bir_lowering=False, num_devices=1)
    arrays, dram = {}, {}
    for short, name in _INS.items():
        a = _np.ascontiguousarray(inputs[name])
        arrays["in_" + short] = a
        dram[short] = nc.dram_tensor("in_" + short, a.shape, _mybir.dt.from_np(a.dtype), kind="ExternalInput").ap()
    out = nc.dram_tensor("out_0", (8, 512, 128), _mybir.dt.float32, kind="ExternalOutput").ap()
    build(nc, dram, out)
    r = _run(nc, [arrays], core_ids=[0])
    return r.results[0]["out_0"]
```

```python
import concourse.bass as bass
from concourse import mybir
from contextlib import ExitStack

FP32 = mybir.dt.float32
BF16 = mybir.dt.bfloat16
ALU = mybir.AluOpType
ACT = mybir.ActivationFunctionType
AX = mybir.AxisListType

P = 128
B, L, D = 8, 512, 128
TT = L // P
NH, HD = 4, 64
DI = NH * HD
CB = 4
KC = 4
FF = 4
EPS_RMS, EPS_GATE, EPS_LN, EPS_LN2 = 1.1920929e-07, 1e-05, 1e-05, 1e-06


class Count:

    def __init__(self, n, per):
        self.base, self.per, self.n = n * per + 1, per, 0

    def up(self):
        self.n += 1
        return 1

    def now(self):
        return self.base + self.n

    def end(self):
        assert self.n == self.per, (self.n, self.per)


def in_register(engine, count):
    return count if isinstance(count, int) else engine.to_reg(count)


def spread(ap, n):
    return ap.unsqueeze(len(ap.shape)).to_broadcast(list(ap.shape) + [n])


def build_mamba(nc, ctx, T, dram, later_loads):
    def sb(name, shape, dt=FP32):
        return ctx.enter_context(nc.sbuf_tensor(name, shape, dt))

    def two(name, shape, dt=FP32):
        return [sb(name + half, shape, dt) for half in ("_even", "_odd")]

    X, ident, tri, above, ones, mhalf = T["X"], T["ident"], T["tri"], T["above"], T["ones"], T["mhalf"]
    R = [T["bank"][0:4], T["bank"][4:8]]

    w_in = sb("w_in", [P, 2 * DI + 2 * P + NH])
    conv_w = sb("conv_w", [P, CB, KC])
    conv_b = sb("conv_b", [P, CB])
    dtb = sb("dtb", [P, NH])
    neg_a = sb("neg_a", [P, NH])
    dskip = sb("dskip", [P, NH])
    norm_w = sb("norm_w", [P, 2])
    w_out = sb("w_out", [P, 2, D])
    w_fc = sb("w_fc", [P, FF * P])
    w_proj = sb("w_proj", [P, FF, D])

    xsq = two("xsq", [P, TT, D])
    hsq = two("hsq", [P, TT, D])
    xn = two("xn", [P, TT, D])
    hn = two("hn", [P, TT, D])
    ms = sb("ms", [P, B * TT])
    rstd = sb("rstd", [P, B * TT])
    xnT = two("xnT", [P, L])
    xbcT = two("xbcT", [P, CB, L])
    sz = two("sz", [P, TT, DI])
    dtv = two("dtv", [P, TT, NH])
    dta = two("dta", [P, TT, NH])
    dte = two("dte", [P, TT, NH])
    dt = two("dt", [P, TT, NH])
    a = two("a", [P, TT, NH])
    dec = two("dec", [P, 2, TT, NH])
    aut = two("aut", [P, 2, NH, P])
    Lm = two("Lm", [P, 2, NH, P])
    Gm = two("Gm", [P, 2, P])
    M = two("M", [P, 2, NH, P])
    xB = two("xB", [P, 2, 4, P])
    u = two("u", [P, 2, DI])
    du = two("du", [P, 2, DI])
    xd = two("xd", [P, 2, DI])
    S = two("S", [P, DI])
    Sd = two("Sd", [P, DI])
    yo = two("yo", [P, DI])
    yd = two("yd", [P, DI])
    g = two("g", [P, TT, DI])
    gsq = two("gsq", [P, DI])
    gss = two("gss", [P, TT])
    gms = two("gms", [P, TT])
    grs = two("grs", [P, TT])
    gT = two("gT", [P, TT, 2, P])
    h = two("h", [P, TT, D])
    hms = two("hms", [P, TT])
    hrs = two("hrs", [P, TT])
    hnT = two("hnT", [P, L])
    rl = two("rl", [P, 2, L])
    mT = two("mT", [P, FF, L])
    r1 = two("r1", [P, TT, D])
    bst = two("bst", [P, TT, 6])
    mean = two("mean", [P, TT])
    dmean = two("dmean", [P, TT])
    vs = two("vs", [P, TT])
    lrs = two("lrs", [P, TT])

    names = ["xn", "pe_xnT", "xnT", "pe_conv", "tap", "conv", "silu", "pe_z", "sz", "pe_dt", "dt_read", "dt_abs",
             "dt_exp", "dt_ln", "a", "pe_cum", "dec", "aut", "pe_seg", "Lm", "Gm", "M", "pe_tok", "xB", "u", "xd", "du", "pe_y",
             "y_read", "pe_st", "S", "g", "gss", "gms", "grs", "pe_gT", "gT", "pe_out", "h", "sq_h", "ms_h", "rs_h", "hn",
             "pe_hnT", "hnT", "pe_fc", "relu", "mT", "pe_proj", "proj_read", "var", "lrs", "x1", "step_front", "step_chunks", "step_back"]
    sems = [{n: ctx.enter_context(nc.semaphore(f"{half}_{n}")) for n in names} for half in ("even", "odd")]
    sq_x, summed_x, ms_x, rs_x = (ctx.enter_context(nc.semaphore(n)) for n in ("sq_x", "summed_x", "ms_x", "rs_x"))
    weights = ctx.enter_context(nc.semaphore("weights"))
    neg_exp = ctx.enter_context(nc.semaphore("neg_exp"))
    FRONT_STEPS, CHUNKS_STEPS, BACK_STEPS = 10, 8, 12
    X_BANK, DT_BANK, G_BANK, OUT_BANK, CONV_BANK = 0, 0, (1, 0), 2, (3, 1, 0, 2)
    H_BANK, FC_BANK, Z_BANK, PROJ_BANK = 3, (1, 0, 2, 3), (0, 1), 2
    T["used"] = [weights, neg_exp, sq_x, summed_x, ms_x, rs_x] + [used for half in sems for used in half.values()]

    def heads(ap):
        return ap.rearrange("p (h e) -> p h e", e=HD)

    with nc.Block() as block:
        @block.scalar
        def _(act):
            loads = [
                (w_in[:, 0:NH], dram["w_in"][:, 2 * DI + 2 * P:]),
                (w_in[:, NH:], dram["w_in"][:, 0:2 * DI + 2 * P]),
                (conv_w[:, :, :], dram["conv_w"].rearrange("(j p) k -> p j k", p=P)),
                (conv_b[:, :], dram["conv_b"].rearrange("(j p) -> p j", p=P)),
                (dtb[:, :], dram["dt_bias"].partition_broadcast(P)),
                (neg_a[:, :], dram["a_log"].partition_broadcast(P)),
                (dskip[:, :], dram["d_skip"].partition_broadcast(P)),
                (norm_w[:, :], dram["norm_w"].rearrange("(j p) -> p j", p=P)),
                (w_out[:, :, :], dram["w_out"].rearrange("(j p) d -> p j d", p=P)),
                (w_fc[:, :], dram["w_fc"]),
                (w_proj[:, :, :], dram["w_proj"].rearrange("(j p) d -> p j d", p=P)),
            ]
            with nc.allow_non_contiguous_dma(reason="per-feature columns of a few bytes"):
                for dst, src in loads:
                    act.dma_start(dst, src).then_inc(weights, 16)
            act.wait_ge(T["x_first"], 16)
            for b in range(2):
                act.activation(xsq[b][:, :, :], X[:, b * TT:(b + 1) * TT, :], ACT.Square).then_inc(sq_x, 1)
            act.wait_ge(weights, 16 * len(loads))
            act.activation(neg_a[:, :], neg_a[:, :], ACT.Exp).then_inc(neg_exp, 1)

        @block.vector
        def _(dve):
            for b in range(2):
                dve.wait_ge(sq_x, b + 1)
                dve.tensor_reduce(ms[:, b * TT:(b + 1) * TT], xsq[b][:, :, :], AX.X, ALU.add).then_inc(summed_x, 1)
            dve.wait_ge(summed_x, 2)
            dve.tensor_scalar(ms[:, 0:2 * TT], ms[:, 0:2 * TT], 1.0 / D, EPS_RMS, ALU.mult, ALU.add).then_inc(ms_x, 1)
            dve.wait_ge(neg_exp, 1)
            dve.tensor_scalar(neg_a[:, :], neg_a[:, :], -1.0, None, ALU.mult)
            for j in range(2):
                dve.tensor_scalar(w_out[:, j, :], w_out[:, j, :], norm_w[:, j:j + 1], None, ALU.mult)

        @block.sync
        def _(sp):
            for lo, hi in ((0, 2), (2, B)):
                loaded = T["x_first"] if lo == 0 else T["x_rest"]
                sp.dma_start(X[:, lo * TT:hi * TT, :], dram["x"][lo:hi].rearrange("b (t p) d -> p (b t) d", p=P)).then_inc(loaded, 16)
            sp.wait_ge(T["x_first"], 16)
            sp.wait_ge(T["x_rest"], 16)

        @block.gpsimd
        def _(pool):
            pool.memset(ident[:, :], 0.0).then_inc(T["masks"], 1)
            for mask in (tri, above, ones):
                pool.memset(mask[:, :], 1.0).then_inc(T["masks"], 1)
            pool.memset(mhalf[:, :], -0.5).then_inc(T["masks"], 1)
            pool.wait_ge(T["masks"], 5)
            pool.affine_select(out=ident[:, :], in_=ident[:, :], compare_op=ALU.not_equal, fill=1.0,
                               base=0, pattern=[[-1, P]], channel_multiplier=1).then_inc(T["masks"], 1)
            pool.affine_select(out=tri[:, :], in_=tri[:, :], compare_op=ALU.is_ge, fill=0.0,
                               base=0, pattern=[[1, P]], channel_multiplier=-1).then_inc(T["masks"], 1)
            pool.affine_select(out=above[:, :], in_=above[:, :], compare_op=ALU.is_ge, fill=0.0,
                               base=-1, pattern=[[-1, P]], channel_multiplier=1).then_inc(T["masks"], 1)
            for half in sems:
                for started in half.values():
                    pool.sem_inc(started, 1)
            pool.wait_ge(T["masks"], 8)
            pool.wait_ge(ms_x, 1)
            pool.tensor_tensor(rstd[:, 0:2 * TT], ms[:, 0:2 * TT], mhalf[:, 0:1].to_broadcast([P, 2 * TT]), ALU.pow).then_inc(rs_x, 1)

    def two_before(q, c, per=TT):
        return q * per + max(c - 1, 0) + 1

    def halves(engine, half):
        half(1, None, None, 0)
        half(0, 0, None, 0)
        with engine.Fori(0, B // 2 - 1) as q:
            half(1, q, q, q + 1)
            half(0, q + 1, q, q + 1)
        half(1, B // 2 - 1, B // 2 - 1, None)
        half(0, None, B // 2 - 1, None)

    with nc.Block() as block:
        @block.sync
        def _(sp):
            with nc.allow_non_contiguous_dma(reason="per-feature columns of a few bytes"):
                for dst, src in later_loads:
                    sp.dma_start(dst, src).then_inc(T["later"], 16)

        @block.gpsimd
        def _(pool):
            def power(e, out, in_, name):
                pool.tensor_tensor(out[e][:, :], in_[e][:, :], mhalf[:, 0:TT], ALU.pow).then_inc(sems[e][name], 1)

            def segment_operand(q, e, c):
                s = sems[e]
                pool.wait_ge(s["a"], q + 2)
                pool.wait_ge(s["pe_seg"], two_before(q, c))
                pool.tensor_tensor(aut[e][:, c % 2], spread(a[e][:, c, :], P),
                                   tri[:, :].unsqueeze(1).to_broadcast([P, NH, P]), ALU.mult).then_inc(s["aut"], 1)

            def chunk_inputs(q, e, c):
                s = sems[e]
                pool.wait_ge(s["xB"], q * TT + c + 2)
                pool.wait_ge(s["pe_y"], two_before(q, c))
                pool.wait_ge(s["y_read"], two_before(q, c))
                xt = xB[e][:, c % 2, 0:2, :].rearrange("p a (h e) -> p (a h) e", e=HD)
                pool.tensor_tensor(heads(u[e][:, c % 2]), xt, spread(dt[e][:, c, :], HD), ALU.mult).then_inc(s["u"], 1)
                pool.tensor_tensor(heads(xd[e][:, c % 2]), xt, spread(dskip[:, :], HD), ALU.mult).then_inc(s["xd"], 1)

            def chunk_weights(q, e, c):
                s = sems[e]
                pool.wait_ge(s["Lm"], q * TT + c + 2)
                pool.wait_ge(s["Gm"], q * TT + c + 2)
                pool.tensor_tensor(M[e][:, c % 2], Lm[e][:, c % 2], Gm[e][:, c % 2, :].unsqueeze(1).to_broadcast([P, NH, P]),
                                   ALU.mult).then_inc(s["M"], 1)
                if c < TT - 1:
                    pool.wait_ge(s["pe_st"], q * (TT - 1) + max(c - 1, 0) + 1)
                    pool.wait_ge(s["u"], q * TT + c + 2)
                    pool.tensor_tensor(heads(du[e][:, c % 2]), heads(u[e][:, c % 2]),
                                       Lm[e][:, c % 2, :, P - 1:P].to_broadcast([P, NH, HD]), ALU.mult).then_inc(s["du"], 1)

            def norms(lo, hi):
                pool.wait_ge(ms_x, 2)
                pool.tensor_tensor(rstd[:, lo * TT:hi * TT], ms[:, lo * TT:hi * TT], mhalf[:, 0:1].to_broadcast([P, (hi - lo) * TT]), ALU.pow).then_inc(rs_x, 1)

            def half(e, q, back_q, front_q):
                o = 1 - e
                if q is None and back_q is None:
                    norms(2, B)
                for c in range(TT):
                    if q is not None and c < TT - 1:
                        chunk_inputs(q, e, c + 1)
                    if c == 0 and back_q is not None:
                        pool.wait_ge(sems[o]["gms"], back_q + 2)
                        power(o, grs, gms, "grs")
                    if c == 1 and back_q is not None:
                        pool.wait_ge(sems[o]["ms_h"], back_q + 2)
                        power(o, hrs, hms, "rs_h")
                    if q is not None and c < TT - 1:
                        chunk_weights(q, e, c + 1)
                    if q is not None and c == 0:
                        segment_operand(q, e, 2)
                        segment_operand(q, e, 3)
                if front_q is not None:
                    for c in range(2):
                        segment_operand(front_q, o, c)
                    chunk_inputs(front_q, o, 0)
                    chunk_weights(front_q, o, 0)
                if back_q is not None:
                    pool.wait_ge(sems[o]["var"], back_q + 2)
                    power(o, lrs, vs, "lrs")
            halves(pool, half)

        @block.scalar
        def _(act):
            def norms(lo, hi):
                for b in range(lo, hi):
                    if b >= 2:
                        act.wait_ge(summed_x, b - 1)
                    act.activation(xsq[b % 2][:, :, :], X[:, b * TT:(b + 1) * TT, :], ACT.Square).then_inc(sq_x, 1)

            def scale_x(q, e):
                s = sems[e]
                act.wait_ge(rs_x, 1 if isinstance(q, int) and q + e == 0 else 2)
                act.wait_ge(s["pe_xnT"], q + 1)
                for t in range(TT):
                    tile = bass.ds((2 * q + e) * TT + t, 1)
                    last = act.activation(xn[e][:, t, :], X[:, tile, :].rearrange("p o d -> p (o d)"), ACT.Copy, scale=rstd[:, tile])
                last.then_inc(s["xn"], 1)

            def copy_xnT(q, e):
                s = sems[e]
                act.wait_ge(s["pe_xnT"], q + 2)
                act.wait_ge(s["pe_z"], q * 2 + 1)
                act.activation(xnT[e][:, :], R[e][X_BANK][:, :], ACT.Copy).then_inc(s["xnT"], 1)

            def newest_tap(q, e, j):
                s = sems[e]
                act.wait_ge(s["pe_conv"], q * CB + j + 2)
                act.wait_ge(s["pe_y"], q * TT + 1)
                act.activation(xbcT[e][:, j, :], R[e][CONV_BANK[j]][:, :], ACT.Identity, scale=conv_w[:, j, KC - 1:KC],
                               bias=conv_b[:, j:j + 1]).then_inc(s["tap"], 1)

            def gate(q, e, i):
                s = sems[e]
                act.wait_ge(s["pe_z"], q * 2 + i + 2)
                act.wait_ge(s["g"], q * TT + 1)
                act.activation(sz[e][:, 2 * i:2 * i + 2, :], R[e][Z_BANK[i]][:, :].rearrange("p (t c) -> p t c", t=2), ACT.Silu).then_inc(s["sz"], 1)

            def silu(q, e, j):
                s = sems[e]
                act.wait_ge(s["conv"], q * CB + j + 2)
                act.activation(xbcT[e][:, j, :], xbcT[e][:, j, :], ACT.Silu).then_inc(s["silu"], 1)

            def chunk_copies(q, e, c):
                s = sems[e]
                act.wait_ge(s["pe_tok"], q * TT + c + 2)
                act.wait_ge(s["xd"], two_before(q, c))
                act.wait_ge(s["Gm"], two_before(q, c))
                act.wait_ge(s["pe_st"], q * (TT - 1) + max(c - 1, 0) + 1)
                act.activation(xB[e][:, c % 2, :, :], R[e][0][:, :].rearrange("p (a q) -> p a q", a=4), ACT.Copy).then_inc(s["xB"], 1)

            def chunk_decays(q, e, c):
                s = sems[e]
                act.wait_ge(s["pe_seg"], q * TT + c + 2)
                act.wait_ge(s["M"], two_before(q, c))
                act.wait_ge(s["du"], q * (TT - 1) + max(c - 1, 0) + 1)
                act.activation(Lm[e][:, c % 2], R[e][1][:, :].rearrange("p (h q) -> p h q", h=NH), ACT.Exp).then_inc(s["Lm"], 1)

            def square_g(q, e, c):
                s = sems[e]
                act.wait_ge(s["g"], q * TT + c + 2)
                act.wait_ge(s["gss"], q * TT + c + 1)
                if c == 0:
                    act.wait_ge(s["gms"], q + 1)
                act.activation(gsq[e][:, :], g[e][:, c, :], ACT.Square, accum_out=gss[e][:, c:c + 1]).then_inc(s["gss"], 1)

            def copy_gT(q, e, i):
                s = sems[e]
                act.wait_ge(s["pe_gT"], q * 2 + i + 2)
                act.wait_ge(s["pe_out"], q * 2 + 1)
                act.activation(gT[e][:, 2 * i:2 * i + 2], R[e][G_BANK[i]][:, :].rearrange("p (t a q) -> p t a q", t=2, a=2), ACT.Copy).then_inc(s["gT"], 1)

            def relu(q, e, j):
                s = sems[e]
                act.wait_ge(s["pe_fc"], q * FF + j + 2)
                act.wait_ge(s["mT"], two_before(q, j, FF))
                act.activation(rl[e][:, j % 2, :], R[e][FC_BANK[j]][:, :], ACT.Relu).then_inc(s["relu"], 1)

            def softplus(q, e):
                s = sems[e]
                act.wait_ge(s["dt_abs"], q + 2)
                act.activation(dte[e][:, :, :], dta[e][:, :, :], ACT.Exp, scale=-1.0).then_inc(s["dt_exp"], 1)
                act.wait_ge(s["dt_exp"], q + 2)
                act.activation(dta[e][:, :, :], dte[e][:, :, :], ACT.Ln, bias=1.0).then_inc(s["dt_ln"], 1)

            def decays(q, e):
                s = sems[e]
                act.wait_ge(s["pe_cum"], q + 2)
                act.wait_ge(s["y_read"], q * TT + 1)
                act.wait_ge(s["S"], q * (TT - 1) + 1)
                act.activation(dec[e][:, :, :, :], R[e][3][:, 0:2 * TT * NH].rearrange("p (a t h) -> p a t h", a=2, h=NH),
                               ACT.Exp).then_inc(s["dec"], 1)

            def square_h(q, e):
                s = sems[e]
                act.wait_ge(s["h"], q * TT + TT + 1)
                act.wait_ge(s["ms_h"], q + 1)
                act.activation(hsq[e][:, :, :], h[e][:, :, :], ACT.Square).then_inc(s["sq_h"], 1)

            def copy_hnT(q, e):
                s = sems[e]
                act.wait_ge(s["pe_hnT"], q + 2)
                act.wait_ge(s["pe_fc"], q * FF + 1)
                act.activation(hnT[e][:, :], R[e][H_BANK][:, :], ACT.Copy).then_inc(s["hnT"], 1)

            def half(e, q, back_q, front_q):
                o = 1 - e
                for c in range(TT):
                    if c == 0 and front_q is not None:
                        scale_x(front_q, o)
                    if q is not None and c < TT - 1:
                        chunk_copies(q, e, c + 1)
                        chunk_decays(q, e, c + 1)
                    if c == 0 and front_q is not None:
                        copy_xnT(front_q, o)
                    if c == 0 and q is None and back_q is None:
                        norms(2, B)
                    if c == 0 and back_q is not None:
                        copy_gT(back_q, o, 0)
                    if c == 0 and front_q is not None:
                        newest_tap(front_q, o, 0)
                    if c == 0 and back_q is not None:
                        copy_gT(back_q, o, 1)
                    if c == 1 and back_q is not None:
                        square_h(back_q, o)
                    if c == 1 and front_q is not None:
                        for j in range(1, CB):
                            newest_tap(front_q, o, j)
                    if c == 2 and back_q is not None:
                        copy_hnT(back_q, o)
                    if c == 2 and front_q is not None:
                        softplus(front_q, o)
                    for j in range(FF):
                        if c == 2 and back_q is not None:
                            relu(back_q, o, j)
                        if c == 2 and front_q is not None:
                            silu(front_q, o, j)
                    if c == 3 and front_q is not None:
                        for i in range(2):
                            gate(front_q, o, i)
                    if q is not None:
                        square_g(q, e, c)
                if front_q is not None:
                    decays(front_q, o)
                    chunk_copies(front_q, o, 0)
                    chunk_decays(front_q, o, 0)
            halves(act, half)

        @block.vector
        def _(dve):
            def norms(lo, hi):
                for b in range(lo, hi):
                    dve.wait_ge(sq_x, b + 1)
                    dve.tensor_reduce(ms[:, b * TT:(b + 1) * TT], xsq[b % 2][:, :, :], AX.X, ALU.add).then_inc(summed_x, 1)
                dve.wait_ge(summed_x, hi)
                dve.tensor_scalar(ms[:, lo * TT:hi * TT], ms[:, lo * TT:hi * TT], 1.0 / D, EPS_RMS, ALU.mult, ALU.add).then_inc(ms_x, 1)

            def mean_squares_h(q, e, c_):
                s = sems[e]
                dve.wait_ge(s["sq_h"], q + 2)
                dve.tensor_reduce(hms[e][:, :], hsq[e][:, :, :], AX.X, ALU.add).then_inc(s["step_back"], c_.up())
                dve.wait_ge(s["step_back"], c_.now())
                dve.tensor_scalar(hms[e][:, :], hms[e][:, :], 1.0 / D, EPS_RMS, ALU.mult, ALU.add).then_inc(s["ms_h"], 1)

            def older_taps(q, e, c_, j):
                s = sems[e]
                for k in range(1, KC):
                    if k == 1:
                        dve.wait_ge(s["tap"], q * CB + j + 2)
                    else:
                        dve.wait_ge(s["step_front"], c_.now())
                    tap = dve.scalar_tensor_tensor(xbcT[e][:, j, k:L], R[e][CONV_BANK[j]][:, 0:L - k], conv_w[:, j, KC - 1 - k:KC - k],
                                                   xbcT[e][:, j, k:L], ALU.mult, ALU.add)
                    if k < KC - 1:
                        tap.then_inc(s["step_front"], c_.up())
                tap.then_inc(s["conv"], 1)

            def read_dt(q, e):
                s = sems[e]
                dve.wait_ge(s["pe_dt"], q + 2)
                dve.wait_ge(s["a"], q + 1)
                dve.tensor_tensor(dtv[e][:, :, :], R[e][DT_BANK][:, 0:TT * NH].rearrange("p (t h) -> p t h", h=NH),
                                  dtb[:, :].unsqueeze(1).to_broadcast([P, TT, NH]), ALU.add).then_inc(s["dt_read"], 1)

            def softplus_in(q, e, c_):
                s = sems[e]
                dve.wait_ge(s["dt_read"], q + 2)
                dve.scalar_tensor_tensor(dta[e][:, :, :], dtv[e][:, :, :], -1.0, dtv[e][:, :, :], ALU.mult, ALU.max).then_inc(s["step_front"], c_.up())
                dve.wait_ge(s["step_front"], c_.now())
                dve.tensor_scalar(dtv[e][:, :, :], dtv[e][:, :, :], 0.0, None, ALU.max).then_inc(s["dt_abs"], 1)

            def softplus_out(q, e, c_):
                s = sems[e]
                dve.wait_ge(s["dt_ln"], q + 2)
                dve.wait_ge(s["xd"], q * TT + 1)
                dve.tensor_tensor(dt[e][:, :, :], dtv[e][:, :, :], dta[e][:, :, :], ALU.add).then_inc(s["step_front"], c_.up())
                dve.wait_ge(s["step_front"], c_.now())
                dve.tensor_tensor(a[e][:, :, :], dt[e][:, :, :], neg_a[:, :].unsqueeze(1).to_broadcast([P, TT, NH]), ALU.mult).then_inc(s["a"], 1)

            def mask_scores(q, e, c):
                s = sems[e]
                dve.wait_ge(s["xB"], q * TT + c + 2)
                dve.wait_ge(s["M"], two_before(q, c))
                dve.tensor_tensor(Gm[e][:, c % 2, :], xB[e][:, c % 2, 3, :], tri[:, :], ALU.mult).then_inc(s["Gm"], 1)

            def state(q, e, c_, c):
                s = sems[e]
                if c == TT - 1:
                    return
                if c:
                    dve.wait_ge(s["S"], q * (TT - 1) + c + 1)
                    dve.wait_ge(s["dec"], q + 2)
                    dve.tensor_tensor(heads(Sd[e][:, :]), heads(S[e][:, :]), spread(dec[e][:, 1, c, :], HD), ALU.mult).then_inc(s["step_chunks"], c_.up())
                    dve.wait_ge(s["step_chunks"], c_.now())
                dve.wait_ge(s["pe_st"], q * (TT - 1) + c + 2)
                if c:
                    dve.tensor_tensor(S[e][:, :], R[e][3][:, 0:DI], Sd[e][:, :], ALU.add).then_inc(s["S"], 1)
                else:
                    dve.tensor_copy(S[e][:, :], R[e][3][:, 0:DI]).then_inc(s["S"], 1)

            def output(q, e, c_, c):
                s = sems[e]
                dve.wait_ge(s["pe_y"], q * TT + c + 2)
                dve.wait_ge(s["xd"], q * TT + c + 2)
                if c == 0:
                    dve.wait_ge(s["g"], q * TT + 1)
                    dve.tensor_tensor(yd[e][:, :], R[e][2][:, 0:DI], xd[e][:, 0, :], ALU.add).then_inc(s["y_read"], 1)
                else:
                    dve.wait_ge(s["dec"], q + 2)
                    dve.wait_ge(s["g"], q * TT + c + 1)
                    dve.tensor_tensor(heads(yo[e][:, :]), heads(R[e][2][:, DI:2 * DI]), spread(dec[e][:, 0, c, :], HD), ALU.mult).then_inc(s["step_chunks"], c_.up())
                    dve.tensor_tensor(yd[e][:, :], R[e][2][:, 0:DI], xd[e][:, c % 2, :], ALU.add).then_inc(s["y_read"], 1)
                    dve.wait_ge(s["step_chunks"], c_.now())
                    dve.wait_ge(s["y_read"], q * TT + c + 2)
                    dve.tensor_tensor(yd[e][:, :], yd[e][:, :], yo[e][:, :], ALU.add).then_inc(s["step_chunks"], c_.up())
                    dve.wait_ge(s["step_chunks"], c_.now())
                dve.wait_ge(s["sz"], q * 2 + c // 2 + 2)
                dve.wait_ge(s["y_read"], q * TT + c + 2)
                dve.wait_ge(s["pe_gT"], q * 2 + 1)
                dve.tensor_tensor(g[e][:, c, :], yd[e][:, :], sz[e][:, c, :], ALU.mult).then_inc(s["g"], 1)

            def residual(q, e, t):
                s = sems[e]
                dve.wait_ge(s["pe_out"], (q + 1) * 2 + 1)
                if t == 0:
                    dve.wait_ge(s["grs"], q + 2)
                dve.scalar_tensor_tensor(h[e][:, t, :], R[e][OUT_BANK][:, t * D:(t + 1) * D], grs[e][:, t:t + 1],
                                         X[:, bass.ds((2 * q + e) * TT + t, 1), :].rearrange("p o d -> p (o d)"), ALU.mult, ALU.add).then_inc(s["h"], 1)

            def scale_h(q, e):
                s = sems[e]
                dve.wait_ge(s["rs_h"], q + 2)
                dve.wait_ge(s["pe_hnT"], q + 1)
                dve.tensor_tensor(hn[e][:, :, :], h[e][:, :, :], spread(hrs[e][:, :], D), ALU.mult).then_inc(s["hn"], 1)

            def square_relu(q, e, j):
                s = sems[e]
                dve.wait_ge(s["relu"], q * FF + j + 2)
                dve.wait_ge(s["pe_proj"], q + 1)
                dve.scalar_tensor_tensor(mT[e][:, j, :], R[e][FC_BANK[j]][:, :], 0.0, rl[e][:, j % 2, :], ALU.max, ALU.mult).then_inc(s["mT"], 1)

            def sum_and_stats(q, e, c_):
                s = sems[e]
                dve.wait_ge(s["pe_proj"], q + 2)
                dve.wait_ge(s["x1"], q + 1)
                dve.tensor_tensor(r1[e][:, :, :], R[e][PROJ_BANK][:, :].rearrange("p (t d) -> p t d", t=TT), h[e][:, :, :], ALU.add).then_inc(s["proj_read"], 1)
                dve.wait_ge(s["proj_read"], q + 2)
                dve.tensor_tensor(r1[e][:, :, :], r1[e][:, :, :], X[:, bass.ds((2 * q + e) * TT, TT), :], ALU.add).then_inc(s["step_back"], c_.up())
                dve.wait_ge(s["step_back"], c_.now())
                for t in range(TT):
                    dve.bn_stats(bst[e][:, t, :], r1[e][:, t, :]).then_inc(s["step_back"], c_.up())
                dve.wait_ge(s["step_back"], c_.now())
                dve.tensor_tensor(mean[e][:, :], bst[e][:, :, 1], bst[e][:, :, 4], ALU.add).then_inc(s["step_back"], c_.up())
                dve.tensor_tensor(dmean[e][:, :], bst[e][:, :, 1], bst[e][:, :, 4], ALU.subtract).then_inc(s["step_back"], c_.up())
                dve.tensor_tensor(vs[e][:, :], bst[e][:, :, 2], bst[e][:, :, 5], ALU.add).then_inc(s["step_back"], c_.up())
                dve.wait_ge(s["step_back"], c_.now())
                dve.tensor_scalar(mean[e][:, :], mean[e][:, :], 0.5, None, ALU.mult).then_inc(s["step_back"], c_.up())
                dve.tensor_tensor(dmean[e][:, :], dmean[e][:, :], dmean[e][:, :], ALU.mult).then_inc(s["step_back"], c_.up())
                dve.tensor_scalar(vs[e][:, :], vs[e][:, :], 1.0 / D, EPS_LN, ALU.mult, ALU.add).then_inc(s["step_back"], c_.up())
                dve.wait_ge(s["step_back"], c_.now())
                dve.scalar_tensor_tensor(vs[e][:, :], dmean[e][:, :], 0.25, vs[e][:, :], ALU.mult, ALU.add).then_inc(s["var"], 1)

            def normalize(q, e):
                s = sems[e]
                dve.wait_ge(s["lrs"], q + 2)
                for t in range(TT):
                    last = dve.tensor_scalar(X[:, bass.ds((2 * q + e) * TT + t, 1), :].rearrange("p o d -> p (o d)"), r1[e][:, t, :],
                                             mean[e][:, t:t + 1], lrs[e][:, t:t + 1], ALU.subtract, ALU.mult)
                last.then_inc(s["x1"], 1)

            def gated_mean_squares(q, e):
                dve.wait_ge(sems[e]["gss"], q * TT + TT + 1)
                dve.tensor_scalar(gms[e][:, :], gss[e][:, :], 1.0 / DI, EPS_GATE, ALU.mult, ALU.add).then_inc(sems[e]["gms"], 1)

            def half(e, q, back_q, front_q):
                o = 1 - e
                if q is not None:
                    steps = Count(q, CHUNKS_STEPS)
                if back_q is not None:
                    back_steps = Count(back_q, BACK_STEPS)
                if front_q is not None:
                    front_steps = Count(front_q, FRONT_STEPS)
                if q is None and back_q is None:
                    norms(2, B)
                for c in range(TT):
                    if c == 0 and back_q is not None:
                        gated_mean_squares(back_q, o)
                    if q is not None and c < 2:
                        mask_scores(q, e, c + 1)
                    if c == 1 and back_q is not None:
                        mean_squares_h(back_q, o, back_steps)
                    if c == 1 and front_q is not None:
                        older_taps(front_q, o, front_steps, 1)
                    if c == 2 and front_q is not None:
                        softplus_out(front_q, o, front_steps)
                    if c == 1 and back_q is not None:
                        scale_h(back_q, o)
                    if c == 2 and back_q is not None:
                        square_relu(back_q, o, 0)
                        square_relu(back_q, o, 1)
                    if q is not None:
                        state(q, e, steps, c)
                        output(q, e, steps, c)
                    if c == 0 and front_q is not None:
                        read_dt(front_q, o)
                        softplus_in(front_q, o, front_steps)
                        older_taps(front_q, o, front_steps, 0)
                    if c == 0 and back_q is not None:
                        for t in range(TT):
                            residual(back_q, o, t)
                    if c == 1 and front_q is not None:
                        older_taps(front_q, o, front_steps, 2)
                    if q is not None and c == 1:
                        mask_scores(q, e, 3)
                    if c == 1 and front_q is not None:
                        older_taps(front_q, o, front_steps, 3)
                    if c == 2 and back_q is not None:
                        square_relu(back_q, o, 2)
                        square_relu(back_q, o, 3)
                if front_q is not None:
                    mask_scores(front_q, o, 0)
                if back_q is not None:
                    sum_and_stats(back_q, o, back_steps)
                if back_q is not None:
                    normalize(back_q, o)
                if q is not None:
                    steps.end()
                if back_q is not None:
                    back_steps.end()
                if front_q is not None:
                    front_steps.end()
            halves(dve, half)

        @block.tensor
        def _(pe):
            def mm(out, lhsT, rhs, first=True, last=True):
                return pe.matmul(out, lhsT, rhs, start=first, stop=last)

            def transpose_xn(q, e):
                pe.wait_ge(sems[e]["xn"], q + 2)
                pe.wait_ge(sems[e]["xB"], q * TT + 1)
                for t in range(TT):
                    last = pe.transpose(R[e][X_BANK][:, t * P:(t + 1) * P], xn[e][:, t, :], ident[:, :])
                last.then_inc(sems[e]["pe_xnT"], 1)

            def time_steps(q, e):
                pe.wait_ge(sems[e]["xnT"], q + 2)
                for t in range(TT):
                    last = mm(R[e][DT_BANK][:, t * NH:(t + 1) * NH], xnT[e][:, t * P:(t + 1) * P], w_in[:, 0:NH])
                last.then_inc(sems[e]["pe_dt"], 1)

            def convolved(q, e, j):
                s = sems[e]
                if j == 0:
                    pe.wait_ge(s["S"], q * (TT - 1) + 1)
                if j == 1:
                    pe.wait_ge(s["gT"], max(2 * q, 1) if isinstance(q, int) else 2 * q)
                if j == 2:
                    pe.wait_ge(s["gT"], 2 * q + 1)
                    pe.wait_ge(s["dt_read"], q + 2)
                if j == 3:
                    pe.wait_ge(s["h"], q * TT + 1)
                mm(R[e][CONV_BANK[j]][:, :], w_in[:, DI + NH + j * P:DI + NH + (j + 1) * P], xnT[e][:, :]).then_inc(s["pe_conv"], 1)

            def transpose_hn(q, e, front_q):
                s = sems[e]
                pe.wait_ge(s["hn"], q + 2)
                if front_q is not None:
                    pe.wait_ge(s["conv"], front_q * CB + 2)
                for t in range(TT):
                    last = pe.transpose(R[e][H_BANK][:, t * P:(t + 1) * P], hn[e][:, t, :], ident[:, :])
                last.then_inc(s["pe_hnT"], 1)

            def squared_relu(q, e, j, front_q):
                s = sems[e]
                if j == 0:
                    pe.wait_ge(s["hnT"], q + 2)
                if j < 3 and front_q is not None:
                    pe.wait_ge(s["conv"], front_q * CB + j + 3)
                mm(R[e][FC_BANK[j]][:, :], w_fc[:, j * P:(j + 1) * P], hnT[e][:, :]).then_inc(s["pe_fc"], 1)

            def gates(q, e, i):
                s = sems[e]
                if isinstance(q, int) and q == 0:
                    pe.wait_ge(s["conv"], (q + 1) * CB + 1)
                else:
                    pe.wait_ge(s["mT"], q * FF - 1)
                for t in range(2):
                    last = mm(R[e][Z_BANK[i]][:, t * DI:(t + 1) * DI], xnT[e][:, (2 * i + t) * P:(2 * i + t + 1) * P], w_in[:, NH:NH + DI])
                last.then_inc(s["pe_z"], 1)

            def cumulate(q, e, back_q):
                s, n = sems[e], TT * NH
                if back_q is None:
                    pe.wait_ge(s["conv"], (q + 1) * CB + 1)
                else:
                    pe.wait_ge(s["mT"], (back_q + 1) * FF + 1)
                pe.wait_ge(s["a"], q + 2)
                mm(R[e][3][:, 0:n], tri[:, :], a[e][:, :, :].rearrange("p t h -> p (t h)"))
                mm(R[e][3][:, n:2 * n], ones[:, :], a[e][:, :, :].rearrange("p t h -> p (t h)")).then_inc(s["pe_cum"], 1)

            def tokens_and_scores(q, e, c):
                s, tok = sems[e], slice(c * P, (c + 1) * P)
                if c == 0:
                    pe.wait_ge(s["silu"], q * CB + CB + 1)
                    pe.wait_ge(s["sz"], (q + 1) * 2 + 1)
                pe.wait_ge(s["xB"], q * TT + c + 1)
                for j in range(3):
                    pe.transpose(R[e][0][:, j * P:(j + 1) * P], xbcT[e][:, j, tok], ident[:, :])
                mm(R[e][0][:, 3 * P:4 * P], xbcT[e][:, 2, tok], xbcT[e][:, 3, tok]).then_inc(s["pe_tok"], 1)

            def segments(q, e, c):
                s = sems[e]
                pe.wait_ge(s["aut"], q * TT + c + 2)
                pe.wait_ge(s["Lm"], q * TT + c + 1)
                mm(R[e][1][:, :], above[:, :], aut[e][:, c % 2].rearrange("p h q -> p (h q)")).then_inc(s["pe_seg"], 1)

            def outputs(q, e, c):
                s, tok = sems[e], slice(c * P, (c + 1) * P)
                pe.wait_ge(s["y_read"], q * TT + c + 1)
                if c == 0:
                    pe.wait_ge(s["proj_read"], q + 1)
                if c:
                    pe.wait_ge(s["S"], q * (TT - 1) + c + 1)
                    mm(R[e][2][:, DI:2 * DI], xbcT[e][:, 3, tok], S[e][:, :])
                pe.wait_ge(s["M"], q * TT + c + 2)
                pe.wait_ge(s["u"], q * TT + c + 2)
                for hh in range(NH):
                    last = mm(R[e][2][:, hh * HD:(hh + 1) * HD], M[e][:, c % 2, hh, :], u[e][:, c % 2, hh * HD:(hh + 1) * HD])
                last.then_inc(s["pe_y"], 1)
                if c < TT - 1:
                    pe.wait_ge(s["du"], q * (TT - 1) + c + 2)
                    if c == 0:
                        pe.wait_ge(s["dec"], q + 2)
                    mm(R[e][3][:, 0:DI], xB[e][:, c % 2, 2, :], du[e][:, c % 2, :]).then_inc(s["pe_st"], 1)

            def transpose_g(q, e, i, front_q):
                s = sems[e]
                pe.wait_ge(s["g"], (q + 1) * TT + 1)
                if i == 1 and front_q is not None:
                    pe.wait_ge(s["dt_read"], front_q + 2)
                for t in range(2 * i, 2 * i + 2):
                    for j in range(2):
                        at = 2 * (t - 2 * i) + j
                        last = pe.transpose(R[e][G_BANK[i]][:, at * P:(at + 1) * P], g[e][:, t, j * P:(j + 1) * P], ident[:, :])
                last.then_inc(s["pe_gT"], 1)

            def project_out(q, e, i):
                s = sems[e]
                pe.wait_ge(s["gT"], q * 2 + i + 2)
                for t in range(2 * i, 2 * i + 2):
                    for j in range(2):
                        last = mm(R[e][OUT_BANK][:, t * D:(t + 1) * D], gT[e][:, t, j, :], w_out[:, j, :], j == 0, j == 1)
                last.then_inc(s["pe_out"], 1)

            def project(q, e):
                pe.wait_ge(sems[e]["mT"], (q + 1) * FF + 1)
                for t in range(TT):
                    for j in range(FF):
                        last = mm(R[e][PROJ_BANK][:, t * P:(t + 1) * P], mT[e][:, j, t * P:(t + 1) * P], w_proj[:, j, :], j == 0, j == FF - 1)
                last.then_inc(sems[e]["pe_proj"], 1)

            def half(e, q, back_q, front_q):
                o = 1 - e
                for c in range(TT):
                    if q is not None and c < TT - 1:
                        tokens_and_scores(q, e, c + 1)
                        segments(q, e, c + 1)
                    if c == 0 and front_q is not None:
                        transpose_xn(front_q, o)
                    if c == 0 and back_q is not None:
                        transpose_g(back_q, o, 0, front_q)
                    if c == 0 and front_q is not None:
                        time_steps(front_q, o)
                    if c == 1 and front_q is not None:
                        convolved(front_q, o, 1)
                        convolved(front_q, o, 2)
                    if c == 2 and back_q is not None:
                        transpose_hn(back_q, o, front_q)
                        squared_relu(back_q, o, 0, front_q)
                        squared_relu(back_q, o, 1, front_q)
                    if c == 3 and front_q is not None:
                        gates(front_q, o, 0)
                        gates(front_q, o, 1)
                    if q is not None:
                        outputs(q, e, c)
                    if c == 0 and front_q is not None:
                        convolved(front_q, o, 0)
                    if c == 0 and back_q is not None:
                        transpose_g(back_q, o, 1, front_q)
                        project_out(back_q, o, 0)
                        project_out(back_q, o, 1)
                    if c == 1 and front_q is not None:
                        convolved(front_q, o, 3)
                    if c == 2 and back_q is not None:
                        squared_relu(back_q, o, 2, front_q)
                        squared_relu(back_q, o, 3, front_q)
                if front_q is not None:
                    tokens_and_scores(front_q, o, 0)
                    cumulate(front_q, o, back_q)
                    segments(front_q, o, 0)
                if back_q is not None:
                    project(back_q, o)
            halves(pe, half)


MX = 2
H, KD = 16, 8
GH = 4
NG = MX * H // GH
GM = NG // MX
SL = 4
PAIRS = [(0, 0), (1, 0), (2, 0), (0, 1), (1, 1), (0, 2)]
QROWS = len(PAIRS) * KD
MROWS = 3
RING, PRING = 3, 8
UNITS = NG * SL * GH
SCALE = float(KD) ** -0.5
TWO_ONES = 1 + 16256 * 2.0 ** -23

SHARED = [(g, 1, "neg") for g in range(NG)] + [(g, 2, "ctx") for g in range(NG)] + [
    (0, 3, "ctxT1"), (1, 0, "wo"), (1, 3, "xT"), (2, 0, "q0"), (2, 3, "k0"), (3, 0, "v0"), (3, 3, "v1"),
    (4, 0, "v2"), (4, 3, "ctxT0"), (5, 0, "v3"), (5, 3, "q1"), (6, 0, "k1"), (6, 3, "logits"), (7, 0, "n2T")]
SHARED = sorted(SHARED)
READ_AT = {}
for use in SHARED:
    g, st = divmod(use[0] * SL + use[1] + 1, SL)
    READ_AT.setdefault((g, st, 1), []).append(use)
PREP = ["xT", "q0", "k0", "v0", "v1", "v2", "v3", "q1", "k1", "logits"]
BEFORE = [(0, 2, "ctx"), (0, 3, "ctxT1"), (1, 0, "wo")]
N2T = (7, 0, "n2T")


class Phase:

    def __init__(self, kind, b):
        self.kind, self.b = kind, b
        self.first, self.last = kind == "first", kind == "last"
        prologue = [(0, 0, n) for n in PREP] + [(0, 1, "neg")]
        if kind == "prologue":
            self.uses, self.base = prologue, 0
        elif kind == "epilogue":
            before = Phase("last", b - 1)
            self.uses, self.base = BEFORE, before.base + len(before.uses)
        else:
            self.uses = [x for x in SHARED
                         if not (self.first and x in BEFORE + [N2T])
                         and not (self.last and (x[2] in PREP or (x[2] == "neg" and x[0] >= NG - 1)))]
            self.base = len(prologue) + (0 if self.first else b * len(SHARED) - len(BEFORE + [N2T]))

    def has(self, use):
        return use in self.uses

    def number(self, use):
        return self.base + self.uses.index(use) + 1


def build_attention(nc, ctx, T):
    def sb(name, shape, dt=FP32):
        return ctx.enter_context(nc.sbuf_tensor(name, shape, dt))

    X, X1, bank, ident = T["X"], T["X1"], T["bank"], T["ident"]
    MAXB, EXPB, PVB, SH = (0, 1, 5), (2, 3, 4), 6, bank[7]
    shb = SH[:, :].bitcast(BF16)

    identb = sb("identb", [P, P], BF16)
    Q = [sb(f"Q{m}", [QROWS + MROWS, H, L], BF16) for m in range(MX)]
    K = [sb(f"K{m}", [QROWS + MROWS, H, L], BF16) for m in range(MX)]
    parts = [[sb(f"parts{m}{i}", [P, 3, L], BF16) for i in range(2)] for m in range(MX)]
    full = [sb(f"full{i}", [P, L]) for i in range(2)]; rest = sb("rest", [P, L])
    V = sb("V", [P, SL, MX * H, 32]); vtmp = sb("vtmp", [P, SL, MX * H, KD])
    E = sb("E", [P, PRING, L])
    top = sb("top", [P, 2, GH * TT]); negr = sb("negr", [P, 2, GH * TT]); neg = sb("neg", [P, 2, 3, GH * TT], BF16)
    negT = sb("negT", [3 * GH * TT, 2, P], BF16)
    ctxu = sb("ctxu", [P, L]); rl_ = sb("rsum", [P, TT, GH]); ctxn = sb("ctxn", [P, MX, TT, H, KD]); ctxT = sb("ctxT", [P, MX, L])
    wq = sb("wq", [P, MX, H * KD]); wk = sb("wk", [P, MX, H * KD]); wop = sb("wop", [P, MX, D]); bop = sb("bop", [P, D])
    wv, wo, bq, bk, bv, bo, rw, rb, lg_ = T["wv"], T["wo"], T["bq"], T["bk"], T["bv"], T["bo"], T["rw"], T["rb"], T["ln1"]
    n1T = sb("n1T", [P, L]); xh = sb("xh", [P, TT, D]); msum = sb("msum", [P, 1]); nmat = sb("nmat", [P, P])
    bst = sb("bst2", [P, TT, 6]); mean = sb("mean2", [P, TT]); dmean = sb("dmean2", [P, TT]); vs = sb("vs2", [P, TT]); lrs = sb("lrs2", [P, TT])
    lgt = sb("lgt", [P, MX]); lmx = sb("lmx", [P, 1]); pe_ = sb("pexp", [P, MX]); psm = sb("psm", [P, 1]); pr = sb("pr", [P, MX])
    t1 = sb("t1", [P, TT, D]); xh2 = sb("xh2", [P, TT, D])
    bst_2 = sb("bst_2", [P, TT, 6]); mean_2 = sb("mean_2", [P, TT]); dmean_2 = sb("dmean_2", [P, TT]); vs_2 = sb("vs_2", [P, TT]); lrs_2 = sb("lrs_2", [P, TT])

    primed = ["pe_max", "max_read", "pe_exp", "exp_done", "pv_done", "neg_ready", "neg_rows", "evac", "pe_shared",
              "shared_free", "var", "lrs", "xh", "split", "stack0", "stack1", "v_filled", "nmat", "lmax", "pexp", "pr", "wop",
              "t1", "x2", "x1_sum", "var2", "xh2", "c_dve_ln2", "c_pool_ln2", "c_dve_ln", "c_dve_ctx", "c_pool_neg", "c_pool_split", "c_dve_p"]
    s = {n: ctx.enter_context(nc.semaphore("t_" + n)) for n in primed}
    met = (T["masks"], 8)

    with nc.Block() as block:
        @block.gpsimd
        def _(pool):
            numbers = [used.num for used in T["used"]]
            assert max(numbers) - min(numbers) == len(numbers) - 1
            pool.sem_clear(range(min(numbers), max(numbers) + 1))
            for started in s.values():
                pool.sem_inc(started, 1)
            pool.memset(V[:, :, :, KD + 1:], 0.0)
            pool.memset(V[:, :, :, KD:KD + 1], 1.0)

        @block.vector
        def _(dve):
            dve.memset(K[0][32:, :, :].bitcast(FP32), TWO_ONES)
            dve.tensor_copy(identb[:, :], ident[:, :])
            dve.wait_ge(T["later"], 16 * T["later_loads"])
            dve.tensor_scalar(bq[:, :], bq[:, :], SCALE, None, ALU.mult)
            for i, w in enumerate((wq, wk)):
                for m in range(MX):
                    dve.tensor_copy(w[:, m, :].rearrange("p (k h) -> p k h", h=H), T["raw"][:, i, m, :].rearrange("p (h k) -> p k h", k=KD))

    LN_STEPS, CTX_STEPS, NEG_STEPS, SPLIT_STEPS, P_STEPS = 10, 1, 4, 3, 3

    def phases(engine, body):
        body(Phase("prologue", 0))
        body(Phase("first", 0))
        with engine.Fori(1, B - 1) as b:
            body(Phase("middle", b))
        body(Phase("last", B - 1))
        body(Phase("epilogue", B))

    with nc.Block() as block:
        @block.tensor
        def _(pe):
            def shared(ph, use, next_b):
                if not ph.has(use):
                    return
                what, b = use[2], ph.b
                if what == "neg":
                    count = in_register(pe, ph.number(use) - 1 + 1)
                    pe.wait_ge(*met)
                    pe.wait_ge(s["shared_free"], count)
                else:
                    pe.wait_ge(s["shared_free"], ph.number(use) - 1 + 1)
                if what == "neg":
                    n = b * NG + use[0] + 1 if ph.kind != "prologue" else 0
                    count = in_register(pe, n + 1 + 1)
                    pe.wait_ge(*met)
                    pe.wait_ge(s["neg_ready"], count)
                    par = (use[0] + 1) % 2 if ph.kind != "prologue" else 0
                    i = pe.transpose(shb[0:3 * GH * TT, 0:P], neg[:, par].rearrange("p a c -> p (a c)"), identb[:, :])
                elif what == "ctx":
                    n = b * NG + use[0]
                    pe.wait_ge(s["evac"], n + 1)
                    for t in range(TT):
                        i = pe.transpose(SH[:, t * P:(t + 1) * P], ctxu[:, t * P:(t + 1) * P], ident[:, :])
                elif what == "n2T":
                    pe.wait_ge(s["xh2"], b + 1)
                    for t in range(TT):
                        i = pe.transpose(SH[:, t * P:(t + 1) * P], xh2[:, t, :], ident[:, :])
                elif what in ("ctxT0", "ctxT1"):
                    m = int(what[-1])
                    for t in range(TT):
                        i = pe.transpose(SH[:, t * P:(t + 1) * P], ctxn[:, m, t].rearrange("p h k -> p (h k)"), ident[:, :])
                elif what == "wo":
                    pe.wait_ge(s["wop"], b + 1)
                    for t in range(TT):
                        for m in range(MX):
                            i = pe.matmul(SH[:, t * P:(t + 1) * P], ctxT[:, m, t * P:(t + 1) * P], wop[:, m, :], start=m == 0, stop=m == MX - 1)
                elif what == "xT":
                    pe.wait_ge(s["xh"], (next_b + 1) * TT + 1)
                    for t in range(TT):
                        i = pe.transpose(SH[:, t * P:(t + 1) * P], xh[:, t, :], ident[:, :])
                elif what[0] in "qk":
                    w = {"q": wq, "k": wk}[what[0]]
                    i = pe.matmul(SH[:, :], w[:, int(what[1]), :], n1T[:, :], start=True, stop=True)
                elif what[0] == "v":
                    t = int(what[1])
                    i = pe.matmul(SH[:, 0:MX * H * KD], n1T[:, t * P:(t + 1) * P], wv[:, :, :].rearrange("p m c -> p (m c)"), start=True, stop=True)
                else:
                    pe.wait_ge(s["nmat"], next_b + 1 + 1)
                    i = pe.matmul(SH[:, 0:MX], nmat[:, :], rw[:, :], start=True, stop=True)
                i.then_inc(s["pe_shared"], 1)

            def max_unit(b, g, i, stacks_of, at):
                m, h, t = (g % NG) // GM, (g % GM) * GH + i // TT, i % TT
                u = b * UNITS + g * 16 + i
                if i == 0:
                    pe.wait_ge(s[f"stack{m}"], 16 * 2 * len(PAIRS) * (stacks_of + 1) + 1)
                before = at if isinstance(b, int) and b == 0 and g < 2 else None
                if before is None or before >= len(MAXB):
                    pe.wait_ge(s["max_read"], (u - 1 if at < 2 else u - 2) + 1)
                pe.matmul(bank[MAXB[at % len(MAXB)]][:, :], Q[m][0:QROWS, h, t * P:(t + 1) * P], K[m][0:QROWS, h, :], start=True, stop=True).then_inc(s["pe_max"], 1)

            def values(b, slot):
                g, st = slot // SL, slot % SL
                if st == 0:
                    pe.wait_ge(s["evac"], b * NG + g + 1)
                    if g % GM == 0:
                        pe.wait_ge(s["v_filled"], b * MX + g // GM + 1 + 1)
                pe.wait_ge(s["exp_done"], b * UNITS + (slot + 1) * GH + 1)
                for i in range(GH):
                    u = slot * GH + i
                    last = pe.matmul(bank[PVB][32 * i:32 * i + 32, :], V[:, st, g * GH + i, :], E[:, u % PRING, :],
                                     start=st == 0, stop=st == SL - 1)
                last.then_inc(s["pv_done"], 1)

            def body(ph):
                b = ph.b
                if ph.kind == "prologue":
                    for what in PREP:
                        shared(ph, (0, 0, what), 0)
                    for i in range(16):
                        max_unit(0, 0, i, 0, i)
                    shared(ph, (0, 1, "neg"), 0)
                    for i in range(16):
                        max_unit(0, 1, i, 0, 16 + i)
                    return
                if ph.kind == "epilogue":
                    values(b - 1, NG * SL - 1)
                    for use in BEFORE:
                        shared(ph, use, 0)
                    return
                for g in range(NG):
                    for st in range(SL):
                        slot = g * SL + st
                        for i in range(GH):
                            if not (ph.last and g + 2 >= NG):
                                max_unit(b, g + 2, st * GH + i, b + (g + 2) // NG, g * 16 + st * GH + i)
                            m, u = g // GM, (g * SL + st) * GH + i
                            if st == 0 and i == 0:
                                pe.wait_ge(s["neg_rows"], 16 * (b * NG + g + 1) + 1)
                            pe.wait_ge(s["exp_done"], b * UNITS + max(u - RING + 1, 0) + 1)
                            pe.matmul(bank[EXPB[u % RING]][:, :], K[m][:, (g % GM) * GH + i, st * P:(st + 1) * P],
                                      Q[m][:, (g % GM) * GH + i, :], start=True, stop=True).then_inc(s["pe_exp"], 1)
                        if slot:
                            values(b, slot - 1)
                        elif not ph.first:
                            values(b - 1, NG * SL - 1)
                        for use in SHARED:
                            if use[:2] == (g, st):
                                shared(ph, use, b + 1)
            phases(pe, body)

        @block.scalar
        def _(act):
            def shared(ph, use, next_b):
                if not ph.has(use):
                    return
                what, b = use[2], ph.b
                if what in ("ctx", "wo", "logits") or what[0] == "v":
                    return
                act.wait_ge(s["pe_shared"], ph.number(use) + 1)
                if what == "neg":
                    n = b * NG + use[0] + 1 if ph.kind != "prologue" else 0
                    par = (use[0] + 1) % 2 if ph.kind != "prologue" else 0
                    act.wait_ge(s["neg_rows"], 16 * n + 1)
                    i = act.activation(negT[:, par, :], shb[0:3 * GH * TT, 0:P], ACT.Copy)
                elif what in ("ctxT0", "ctxT1"):
                    i = act.activation(ctxT[:, int(what[-1]), :], SH[:, :], ACT.Copy)
                elif what == "n2T":
                    n = bass.ds(b - 1, 1)
                    i = act.activation(T["n2T"][:, n, :].rearrange("p o t -> p (o t)"), SH[:, :], ACT.Identity,
                                       scale=T["f_ln"][:, 0:1], bias=T["f_ln"][:, 1:2], accum_out=T["sum_n2"][:, n])
                elif what == "xT":
                    act.wait_ge(s["nmat"], next_b + 1)
                    i = act.activation(n1T[:, :], SH[:, :], ACT.Identity, scale=lg_[:, 0:1], bias=lg_[:, 1:2], accum_out=msum[:, :])
                else:
                    m, k = int(what[1]), what[0] == "k"
                    act.wait_ge(s["split"], next_b * 4 + max(2 * m + k - 1, 0) + 1)
                    if k:
                        i = act.activation(full[1][:, :], SH[:, :], ACT.Identity, bias=bk[:, m:m + 1])
                    else:
                        i = act.activation(full[0][:, :], SH[:, :], ACT.Identity, scale=SCALE, bias=bq[:, m:m + 1])
                i.then_inc(s["shared_free"], 1)

            def evacuate(ph, b, g):
                act.wait_ge(s["pv_done"], b * NG * SL + (g + 1) * SL + 1)
                if g < 0 or ph.kind == "epilogue":
                    act.wait_ge(s["pe_shared"], ph.base + 1)
                elif ph.has((g, 2, "ctx")):
                    act.wait_ge(s["pe_shared"], ph.number((g, 2, "ctx")) + 1)
                act.activation(ctxu[:, :], bank[PVB][:, :], ACT.Copy).then_inc(s["evac"], 1)

            def body(ph):
                b = ph.b
                if ph.kind == "prologue":
                    for what in PREP:
                        shared(ph, (0, 0, what), 0)
                    shared(ph, (0, 1, "neg"), 0)
                    return
                if ph.kind == "epilogue":
                    evacuate(ph, b - 1, NG - 1)
                    for use in BEFORE:
                        shared(ph, use, 0)
                    return
                for g in range(NG):
                    for st in range(SL):
                        for i in range(GH):
                            u = (g * SL + st) * GH + i
                            act.wait_ge(s["pe_exp"], b * UNITS + u + 1 + 1)
                            if i == 0:
                                act.wait_ge(s["pv_done"], (b * NG * SL + g * SL + st - 1 if not (ph.first and g * SL + st < 1) else 0) + 1)
                            act.activation(E[:, u % PRING, :], bank[EXPB[u % RING]][:, :], ACT.Exp).then_inc(s["exp_done"], 1)
                            if st == 1 and i == 0 and not (ph.first and g == 0):
                                evacuate(ph, b, g - 1)
                            for use in READ_AT.get((g, st, i), ()):
                                shared(ph, use, b + 1)
                        if (g, st) == (2, 2):
                            act.wait_ge(s["lmax"], b + 1 + 1)
                            act.activation(pe_[:, :], lgt[:, :], ACT.Exp, bias=lmx[:, :], accum_out=psm[:, :]).then_inc(s["pexp"], 1)
            phases(act, body)

        @block.vector
        def _(dve):
            ln1 = (X1, bst, mean, dmean, vs, "c_dve_ln", "var")
            ln2 = (X, bst_2, mean_2, dmean_2, vs_2, "c_dve_ln2", "var2")

            def statistics(ln, n, t, c):
                source, b_, steps = ln[0], ln[1], ln[5]
                dve.bn_stats(b_[:, t, :], source[:, bass.ds(n * TT + t, 1), :].rearrange("p o d -> p (o d)")).then_inc(s[steps], c.up())

            def variance(ln, n, c):
                sums(ln, c)
                differences(ln, c)

            def sums(ln, c):
                _, b_, m_, d_, v_, steps, name = ln
                dve.wait_ge(s[steps], c.now())
                dve.tensor_tensor(m_[:, :], b_[:, :, 1], b_[:, :, 4], ALU.add).then_inc(s[steps], c.up())
                dve.tensor_tensor(d_[:, :], b_[:, :, 1], b_[:, :, 4], ALU.subtract).then_inc(s[steps], c.up())
                dve.tensor_tensor(v_[:, :], b_[:, :, 2], b_[:, :, 5], ALU.add).then_inc(s[steps], c.up())

            def differences(ln, c):
                _, b_, m_, d_, v_, steps, name = ln
                dve.wait_ge(s[steps], c.now())
                dve.tensor_scalar(m_[:, :], m_[:, :], 0.5, None, ALU.mult).then_inc(s[steps], c.up())
                dve.tensor_tensor(d_[:, :], d_[:, :], d_[:, :], ALU.mult).then_inc(s[steps], c.up())
                dve.tensor_scalar(v_[:, :], v_[:, :], 1.0 / D, EPS_LN2, ALU.mult, ALU.add).then_inc(s[steps], c.up())
                dve.wait_ge(s[steps], c.now())
                dve.scalar_tensor_tensor(v_[:, :], d_[:, :], 0.25, v_[:, :], ALU.mult, ALU.add).then_inc(s[name], 1)
                c.end()

            def normalize(n, t):
                if t == 0:
                    dve.wait_ge(s["lrs"], n + 1 + 1)
                dve.tensor_scalar(xh[:, t, :], X1[:, bass.ds(n * TT + t, 1), :].rearrange("p o d -> p (o d)"),
                                  mean[:, t:t + 1], lrs[:, t:t + 1], ALU.subtract, ALU.mult).then_inc(s["xh"], 1)

            def shared(ph, use, next_b):
                if not ph.has(use):
                    return
                what, b = use[2], ph.b
                if what == "ctx":
                    dve.wait_ge(s["pe_shared"], ph.number(use) + 1)
                    n = b * NG + use[0] - 1
                    g = (use[0] - 1) % NG
                    c = Count(n, CTX_STEPS)
                    sh = SH[:, :].rearrange("p (t h c) -> p t h c", t=TT, h=GH)
                    dve.reciprocal(rl_[:, :, :], sh[:, :, :, KD]).then_inc(s["c_dve_ctx"], c.up())
                    dve.wait_ge(s["c_dve_ctx"], c.now())
                    hs = (g % GM) * GH
                    dve.tensor_tensor(ctxn[:, g // GM, :, hs:hs + GH, :], sh[:, :, :, 0:KD], spread(rl_[:, :, :], KD), ALU.mult).then_inc(s["shared_free"], 1)
                    c.end()
                elif what == "wo":
                    dve.wait_ge(s["pe_shared"], ph.number(use) + 1)
                    dve.wait_ge(s["x2"], (b - 1 if not isinstance(b, int) or b > 0 else 0) + 1)
                    dve.tensor_tensor(t1[:, :, :], SH[:, :].rearrange("p (t d) -> p t d", t=TT), X1[:, bass.ds((b - 1) * TT, TT), :], ALU.add).then_inc(s["shared_free"], 1)
                    dve.wait_ge(s["shared_free"], ph.number(use) + 1)
                    dve.tensor_tensor(X[:, bass.ds((b - 1) * TT, TT), :], t1[:, :, :], bop[:, :].unsqueeze(1).to_broadcast([P, TT, D]), ALU.add).then_inc(s["x2"], 1)
                elif what == "logits":
                    dve.wait_ge(s["pe_shared"], ph.number(use) + 1)
                    dve.tensor_tensor(lgt[:, :], SH[:, 0:MX], rb[:, :], ALU.add).then_inc(s["shared_free"], 1)
                elif what[0] == "v":
                    dve.wait_ge(s["pe_shared"], ph.number(use) + 1)
                    dve.wait_ge(s["v_filled"], MX * next_b + 1)
                    dve.tensor_tensor(vtmp[:, int(what[1])].rearrange("p h k -> p (h k)"), SH[:, 0:MX * H * KD], bv[:, :], ALU.add).then_inc(s["shared_free"], 1)

            def max_unit(b, g, i, at):
                u = b * UNITS + g * 16 + i
                if i == 0:
                    n = b * NG + g
                    dve.wait_ge(s["neg_ready"], (n - 1 if not (isinstance(b, int) and n < 1) else 0) + 1)
                dve.wait_ge(s["pe_max"], u + 1 + 1)
                dve.tensor_reduce(top[:, g % 2, i:i + 1], bank[MAXB[at % len(MAXB)]][:, :], AX.X, ALU.max).then_inc(s["max_read"], 1)

            def body(ph):
                b = ph.b
                if ph.kind == "prologue":
                    ln_steps = Count(0, LN_STEPS)
                    for t in range(TT):
                        statistics(ln1, 0, t, ln_steps)
                    variance(ln1, 0, ln_steps)
                    for t in range(TT):
                        normalize(0, t)
                    for what in PREP:
                        shared(ph, (0, 0, what), 0)
                    for g in range(2):
                        for i in range(16):
                            max_unit(0, g, i, g * 16 + i)
                    return
                if ph.kind == "epilogue":
                    for use in BEFORE:
                        shared(ph, use, 0)
                    return
                ln_steps = Count(b + 1, LN_STEPS)
                ln2_steps = Count(b - 1, LN_STEPS)
                p_steps = Count(b, P_STEPS)
                for g in range(NG):
                    for st in range(SL):
                        for i in range(GH):
                            if not (ph.last and g + 2 >= NG):
                                max_unit(b, g + 2, st * GH + i, g * 16 + st * GH + i)
                            for use in READ_AT.get((g, st, i), ()):
                                shared(ph, use, b + 1)
                            if not ph.last:
                                if g == 0 and i == GH - 1:
                                    statistics(ln1, b + 1, st, ln_steps)
                                if (g, st, i) == (1, 0, 1):
                                    sums(ln1, ln_steps)
                                if (g, st, i) == (1, 0, 3):
                                    differences(ln1, ln_steps)
                            if not ph.first:
                                if (g, st, i) == (4, 0, 3):
                                    summed, used = in_register(dve, b + 1), in_register(dve, b)
                                    dve.wait_ge(*met)
                                    dve.wait_ge(s["x2"], summed)
                                    dve.wait_ge(s["xh2"], used)
                                if g == 4 and i == GH - 1:
                                    statistics(ln2, b - 1, st, ln2_steps)
                                if (g, st, i) == (5, 0, 2):
                                    sums(ln2, ln2_steps)
                                if (g, st, i) == (5, 1, 0):
                                    differences(ln2, ln2_steps)
                            if (g, st, i) == (2, 1, 3):
                                dve.tensor_reduce(lmx[:, :], lgt[:, :], AX.X, ALU.max, negate=True).then_inc(s["lmax"], 1)
                            if (g, st, i) == (2, 3, 0):
                                dve.wait_ge(s["pexp"], b + 1 + 1)
                                dve.reciprocal(psm[:, :], psm[:, :]).then_inc(s["c_dve_p"], p_steps.up())
                            if (g, st, i) == (2, 3, 1):
                                dve.wait_ge(s["c_dve_p"], p_steps.now())
                                dve.tensor_scalar(pr[:, :], pe_[:, :], psm[:, :], None, ALU.mult).then_inc(s["c_dve_p"], p_steps.up())
                            if (g, st, i) == (2, 3, 2):
                                dve.wait_ge(s["c_dve_p"], p_steps.now())
                                dve.tensor_scalar(bop[:, :], bo[:, 0, :], pr[:, 0:1], None, ALU.mult).then_inc(s["c_dve_p"], p_steps.up())
                            if (g, st, i) == (2, 3, 3):
                                dve.wait_ge(s["c_dve_p"], p_steps.now())
                                dve.scalar_tensor_tensor(bop[:, :], bo[:, 1, :], pr[:, 1:2], bop[:, :], ALU.mult, ALU.add).then_inc(s["pr"], 1)
                                p_steps.end()
                            if not ph.last and (g, st) == (1, 2):
                                normalize(b + 1, i)
            phases(dve, body)

        @block.gpsimd
        def _(pool):
            def negate(n, par):
                c = Count(n, NEG_STEPS)
                count = in_register(pool, 16 * (n + 1) + 1)
                pool.wait_ge(*met)
                pool.wait_ge(s["max_read"], count)
                pool.tensor_scalar(negr[:, par, :], top[:, par, :], -1.0, 0.0, ALU.mult, ALU.add).then_inc(s["c_pool_neg"], c.up())
                pool.tensor_scalar(neg[:, par, 0, :], top[:, par, :], -1.0, 0.0, ALU.mult, ALU.add).then_inc(s["c_pool_neg"], c.up())
                count = in_register(pool, c.now())
                pool.wait_ge(*met)
                pool.wait_ge(s["c_pool_neg"], count)
                pool.tensor_tensor(negr[:, par, :], negr[:, par, :], neg[:, par, 0, :], ALU.subtract).then_inc(s["c_pool_neg"], c.up())
                count = in_register(pool, c.now())
                pool.wait_ge(*met)
                pool.wait_ge(s["c_pool_neg"], count)
                pool.tensor_scalar(neg[:, par, 1, :], negr[:, par, :], 1.0, 0.0, ALU.mult, ALU.add).then_inc(s["c_pool_neg"], c.up())
                count = in_register(pool, c.now())
                pool.wait_ge(*met)
                pool.wait_ge(s["c_pool_neg"], count)
                pool.tensor_tensor(neg[:, par, 2, :], negr[:, par, :], neg[:, par, 1, :], ALU.subtract).then_inc(s["neg_ready"], 1)
                c.end()

            def split(ph, use, n):
                m, k = int(use[2][1]), int(use[2][0] == "k")
                c = Count(n * 4 + 2 * m + k, SPLIT_STEPS)
                count = in_register(pool, ph.number(use) + 1)
                pool.wait_ge(*met)
                pool.wait_ge(s["shared_free"], count)
                count = in_register(pool, 16 * 2 * len(PAIRS) * n + 1)
                pool.wait_ge(*met)
                pool.wait_ge(s[f"stack{m}"], count)
                a, f = parts[m][k], full[k]
                pool.tensor_scalar(a[:, 0, :], f[:, :], 1.0, 0.0, ALU.mult, ALU.add).then_inc(s["c_pool_split"], c.up())
                count = in_register(pool, c.now())
                pool.wait_ge(*met)
                pool.wait_ge(s["c_pool_split"], count)
                pool.tensor_tensor(rest[:, :], f[:, :], a[:, 0, :], ALU.subtract).then_inc(s["c_pool_split"], c.up())
                count = in_register(pool, c.now())
                pool.wait_ge(*met)
                pool.wait_ge(s["c_pool_split"], count)
                pool.tensor_scalar(a[:, 1, :], rest[:, :], 1.0, 0.0, ALU.mult, ALU.add).then_inc(s["c_pool_split"], c.up())
                count = in_register(pool, c.now())
                pool.wait_ge(*met)
                pool.wait_ge(s["c_pool_split"], count)
                pool.tensor_tensor(a[:, 2, :], rest[:, :], a[:, 1, :], ALU.subtract).then_inc(s["split"], 1)
                c.end()

            def fill_v(m, n, used):
                if used is not None:
                    count = in_register(pool, used + 1)
                    pool.wait_ge(*met)
                    pool.wait_ge(s["pv_done"], count)
                hs = slice(m * H, (m + 1) * H)
                pool.tensor_scalar(V[:, :, hs, 0:KD], vtmp[:, :, hs, :], 1.0, 0.0, ALU.mult, ALU.add).then_inc(s["v_filled"], 1)

            def rsqrt(n):
                count = in_register(pool, n + 1 + 1)
                pool.wait_ge(*met)
                pool.wait_ge(s["var"], count)
                pool.tensor_tensor(lrs[:, :], vs[:, :], T["mhalf"][:, 0:TT], ALU.pow).then_inc(s["lrs"], 1)

            def mean_tokens(ph, use, n):
                count = in_register(pool, ph.number(use) + 1)
                pool.wait_ge(*met)
                pool.wait_ge(s["shared_free"], count)
                pool.tensor_scalar(nmat[:, :], T["ones"][:, :], msum[:, :], 1.0 / L, ALU.mult, ALU.mult).then_inc(s["nmat"], 1)

            def normalize_x2(n, b):
                c = Count(n, 2)
                count = in_register(pool, n + 1 + 1)
                pool.wait_ge(*met)
                pool.wait_ge(s["var2"], count)
                pool.tensor_tensor(lrs_2[:, :], vs_2[:, :], T["mhalf"][:, 0:TT], ALU.pow).then_inc(s["c_pool_ln2"], c.up())
                count = in_register(pool, Phase("middle", b - 1).number(N2T) + 1)
                pool.wait_ge(*met)
                pool.wait_ge(s["pe_shared"], count)
                pool.tensor_tensor(xh2[:, :, :], X[:, bass.ds(n * TT, TT), :], spread(mean_2[:, :], D), ALU.subtract).then_inc(s["c_pool_ln2"], c.up())
                count = in_register(pool, c.now())
                pool.wait_ge(*met)
                pool.wait_ge(s["c_pool_ln2"], count)
                pool.tensor_tensor(xh2[:, :, :], xh2[:, :, :], spread(lrs_2[:, :], D), ALU.mult).then_inc(s["xh2"], 1)
                c.end()

            def x1_sum(n):
                count = in_register(pool, n + 1 + 1)
                pool.wait_ge(*met)
                pool.wait_ge(s["x2"], count)
                xs = bass.ds(n * TT, TT)
                pool.tensor_tensor(X1[:, xs, :], X1[:, xs, :], X[:, xs, :], ALU.add).then_inc(s["x1_sum"], 1)

            def body(ph):
                b = ph.b
                if ph.kind == "prologue":
                    rsqrt(0)
                    mean_tokens(ph, (0, 0, "xT"), 0)
                    for what in ("q0", "k0"):
                        split(ph, (0, 0, what), 0)
                    count = in_register(pool, ph.number((0, 0, "v3")) + 1)
                    pool.wait_ge(*met)
                    pool.wait_ge(s["shared_free"], count)
                    for m in range(MX):
                        fill_v(m, 0, None)
                    pool.wait_ge(s["v_filled"], MX + 1)
                    pool.memset(K[1][32:, :, :].bitcast(FP32), TWO_ONES).then_inc(T["masks"], 1)
                    pool.wait_ge(T["masks"], 9)
                    for what in ("q1", "k1"):
                        split(ph, (0, 0, what), 0)
                    negate(0, 0)
                    return
                if ph.kind == "epilogue":
                    x1_sum(b - 1)
                    return
                for g in range(NG):
                    if not (ph.last and g == NG - 1):
                        negate(b * NG + g + 1, (g + 1) % 2)
                    if g == 1 and not ph.last:
                        rsqrt(b + 1)
                    if g == 1 and not ph.first:
                        fill_v(1, b, b * NG * SL)
                        x1_sum(b - 1)
                    if g == 2 and not ph.last:
                        mean_tokens(ph, (1, 3, "xT"), b + 1)
                        split(ph, (2, 0, "q0"), b + 1)
                    if g == 3:
                        if not ph.last:
                            split(ph, (2, 3, "k0"), b + 1)
                        count = in_register(pool, b + 1 + 1)
                        pool.wait_ge(*met)
                        pool.wait_ge(s["pr"], count)
                        if not ph.first:
                            count = in_register(pool, ph.number((1, 0, "wo")) + 1)
                            pool.wait_ge(*met)
                            pool.wait_ge(s["shared_free"], count)
                        for m in range(MX):
                            i = pool.tensor_scalar(wop[:, m, :], wo[:, m, :], pr[:, m:m + 1], 0.0, ALU.mult, ALU.add)
                        i.then_inc(s["wop"], 1)
                    if g == 5 and not ph.last:
                        count = in_register(pool, ph.number((5, 0, "v3")) + 1)
                        pool.wait_ge(*met)
                        pool.wait_ge(s["shared_free"], count)
                        fill_v(0, b + 1, b * NG * SL + GM * SL)
                    if g == 5 and not ph.first:
                        normalize_x2(b - 1, b)
                    if g == 6 and not ph.last:
                        split(ph, (5, 3, "q1"), b + 1)
                        split(ph, (6, 0, "k1"), b + 1)
            phases(pool, body)

        @block.sync
        def _(sp):
            def fill(m, n, used):
                count = in_register(sp, 4 * n + 2 * m + 2 + 1)
                sp.wait_ge(*met)
                sp.wait_ge(s["split"], count)
                if used is not None:
                    count = in_register(sp, used + 1)
                    sp.wait_ge(*met)
                    sp.wait_ge(s["pv_done"], count)
                for i, stack in enumerate((Q[m], K[m])):
                    for j, pair in enumerate(PAIRS):
                        src = parts[m][i][:, pair[i], :]
                        sp.dma_start(stack[j * KD:(j + 1) * KD, :, :], src).then_inc(s[f"stack{m}"], 16)

            def send(ph, use, n, g):
                count = in_register(sp, ph.number(use) + 1)
                sp.wait_ge(*met)
                sp.wait_ge(s["shared_free"], count)
                count = in_register(sp, 16 * n + 1)
                sp.wait_ge(*met)
                sp.wait_ge(s["neg_rows"], count)
                m, h = (g % NG) // GM, (g % GM) * GH
                dst = Q[m][QROWS:QROWS + MROWS, h:h + GH, :].rearrange("a h (t p) -> a (h t) p", p=P)
                sp.dma_start(dst, negT[:, g % 2, :]).then_inc(s["neg_rows"], 16)

            def body(ph):
                b = ph.b
                if ph.kind == "prologue":
                    for m in range(MX):
                        fill(m, 0, None)
                    send(ph, (0, 1, "neg"), 0, 0)
                    return
                if ph.kind == "epilogue":
                    return
                for g in range(NG):
                    if ph.has((g, 1, "neg")):
                        send(ph, (g, 1, "neg"), b * NG + g + 1, g + 1)
                    if g == 0 and not ph.first:
                        fill(1, b, b * NG * SL)
                    if g == 4 and not ph.last:
                        fill(0, b + 1, b * NG * SL + GM * SL)
            phases(sp, body)


NE, TOP = 8, 2
FE = 2
HB = TOP * FE


def build_experts(nc, ctx, T, dram, out):
    def sb(name, shape, dt=FP32):
        return ctx.enter_context(nc.sbuf_tensor(name, shape, dt))

    X, X1, bank, ident, ones = T["X"], T["X1"], T["bank"], T["ident"], T["ones"]
    rw, rb, ln = T["f_rw"], T["f_rb"], T["f_ln"]
    bst = sb("f_bst", [P, TT, 6]); mean = sb("f_mean", [P, TT]); dmean = sb("f_dmean", [P, TT]); vs = sb("f_vs", [P, TT]); rs = sb("f_rs", [P, TT])
    xh = sb("f_xh", [P, TT, D]); n2T, msum = T["n2T"], T["sum_n2"]; mtok = sb("f_mtok", [P, B])
    lg = sb("f_lg", [B, NE]); lmx = sb("f_lmx", [B, 1]); pexp = sb("f_pexp", [B, NE]); psm = sb("f_psm", [B, 1]); pr = sb("f_pr", [B, NE])
    best = sb("f_best", [B, 8]); which = sb("f_which", [B, 8], mybir.dt.uint32); bsum = sb("f_bsum", [B, 1]); share = sb("f_share", [B, TOP])
    diag = sb("f_diag", [B, B, TOP]); weight = sb("f_weight", [P, B * TOP]); chosen = sb("f_chosen", [1, B * TOP], mybir.dt.uint32)
    w1 = sb("f_w1", [P, 2, TOP, FE * P]); w2 = sb("f_w2", [P, 2, TOP, FE, D]); w2p = sb("f_w2p", [P, 2, HB, D])
    hid = sb("f_hid", [P, 2, HB, L]); y = sb("f_y", [P, TT, D]); res = sb("f_res", [P, 2, TT, D])
    bst_y = sb("f_bst_y", [P, TT, 6]); mean_y = sb("f_mean_y", [P, TT]); dmean_y = sb("f_dmean_y", [P, TT])
    vs_y = sb("f_vs_y", [P, TT]); rs_y = sb("f_rs_y", [P, TT])

    names = ["var", "rs", "xh", "pe_T", "n2T", "mtok", "pe_lg", "lmx", "pexp", "which", "chosen", "diag", "pe_weight", "weight",
             "w1_in0", "w1_in1", "w2_in0", "w2_in1", "w2p", "pe_up", "gelu", "pe_down", "y", "yvar", "yrs", "res",
             "stored0", "stored1", "c_var", "c_pick", "c_y"]
    s = {n: ctx.enter_context(nc.semaphore("f_" + n)) for n in names}
    met = (T["masks"], 8)

    with nc.Block() as block:
        @block.gpsimd
        def _(pool):
            for started in s.values():
                pool.sem_inc(started, 1)
            pool.wait_ge(T["later"], 16 * T["later_loads"])

    def rows(ap, n):
        return ap[:, bass.ds(n, 1), :].rearrange("p o d -> p (o d)")

    def combine(dve, b_, m_, d_, v_, eps, counted, chain, name):
        dve.tensor_tensor(m_, b_[:, :, 1], b_[:, :, 4], ALU.add).then_inc(s[counted], chain.up())
        dve.tensor_tensor(d_, b_[:, :, 1], b_[:, :, 4], ALU.subtract).then_inc(s[counted], chain.up())
        dve.tensor_tensor(v_, b_[:, :, 2], b_[:, :, 5], ALU.add).then_inc(s[counted], chain.up())
        dve.wait_ge(s[counted], chain.now())
        dve.tensor_scalar(m_, m_, 0.5, None, ALU.mult).then_inc(s[counted], chain.up())
        dve.tensor_tensor(d_, d_, d_, ALU.mult).then_inc(s[counted], chain.up())
        dve.tensor_scalar(v_, v_, 1.0 / D, eps, ALU.mult, ALU.add).then_inc(s[counted], chain.up())
        dve.wait_ge(s[counted], chain.now())
        dve.scalar_tensor_tensor(v_, d_, 0.25, v_, ALU.mult, ALU.add).then_inc(s[name], 1)

    def used(b):
        return 1 if isinstance(b, int) and b < 2 else b

    with nc.Block() as block:
        @block.vector
        def _(dve):
            c = Count(0, 10)
            for t in range(TT):
                dve.bn_stats(bst[:, t, :], X[:, (B - 1) * TT + t, :]).then_inc(s["c_var"], c.up())
            dve.wait_ge(s["c_var"], c.now())
            combine(dve, bst, mean[:, :], dmean[:, :], vs[:, :], EPS_LN2, "c_var", c, "var")
            c.end()
            dve.wait_ge(s["rs"], 2)
            for t in range(TT):
                last = dve.tensor_scalar(xh[:, t, :], X[:, (B - 1) * TT + t, :], mean[:, t:t + 1], rs[:, t:t + 1], ALU.subtract, ALU.mult)
            last.then_inc(s["xh"], 1)

            c = Count(0, 9)
            dve.wait_ge(s["n2T"], 2)
            dve.tensor_scalar(mtok[:, :], msum[:, :], 1.0 / L, None, ALU.mult).then_inc(s["mtok"], 1)
            dve.wait_ge(s["pe_lg"], 2)
            dve.tensor_tensor(lg[:, :], bank[2][0:B, 0:NE], rb[0:B, :], ALU.add).then_inc(s["c_pick"], c.up())
            dve.wait_ge(s["c_pick"], c.now())
            dve.tensor_reduce(lmx[:, :], lg[:, :], AX.X, ALU.max, negate=True).then_inc(s["lmx"], 1)
            dve.wait_ge(s["pexp"], 2)
            dve.reciprocal(psm[:, :], psm[:, :]).then_inc(s["c_pick"], c.up())
            dve.wait_ge(s["c_pick"], c.now())
            dve.tensor_scalar(pr[:, :], pexp[:, :], psm[:, :], None, ALU.mult).then_inc(s["c_pick"], c.up())
            dve.wait_ge(s["c_pick"], c.now())
            dve.max(best[:, :], pr[:, :]).then_inc(s["c_pick"], c.up())
            dve.wait_ge(s["c_pick"], c.now())
            dve.max_index(which[:, :], best[:, :], pr[:, :]).then_inc(s["which"], 1)
            dve.tensor_tensor(bsum[:, :], best[:, 0:1], best[:, 1:2], ALU.add).then_inc(s["c_pick"], c.up())
            dve.wait_ge(s["c_pick"], c.now())
            dve.reciprocal(bsum[:, :], bsum[:, :]).then_inc(s["c_pick"], c.up())
            dve.wait_ge(s["c_pick"], c.now())
            dve.tensor_scalar(share[:, :], best[:, 0:TOP], bsum[:, :], None, ALU.mult).then_inc(s["c_pick"], c.up())
            dve.wait_ge(s["c_pick"], c.now())
            dve.tensor_tensor(diag[:, :, :], share[:, :].unsqueeze(1).to_broadcast([B, B, TOP]), spread(ident[0:B, 0:B], TOP), ALU.mult).then_inc(s["diag"], 1)
            dve.wait_ge(s["pe_weight"], 2)
            dve.tensor_copy(weight[:, :], bank[3][:, 0:B * TOP]).then_inc(s["weight"], 1)

            def sum_and_normalize(b, par, q):
                c = Count(b, 10)
                dve.wait_ge(s["pe_down"], b + 2)
                dve.wait_ge(s["res"], b + 1)
                dve.tensor_tensor(y[:, :, :], bank[4 + par][:, :].rearrange("p (t d) -> p t d", t=TT), X1[:, bass.ds(b * TT, TT), :], ALU.add).then_inc(s["y"], 1)
                dve.wait_ge(s["y"], b + 2)
                for t in range(TT):
                    dve.bn_stats(bst_y[:, t, :], y[:, t, :]).then_inc(s["c_y"], c.up())
                dve.wait_ge(s["c_y"], c.now())
                combine(dve, bst_y, mean_y[:, :], dmean_y[:, :], vs_y[:, :], EPS_LN, "c_y", c, "yvar")
                c.end()
                dve.wait_ge(s["yrs"], b + 2)
                dve.wait_ge(s[f"stored{par}"], 16 * q + 1)
                for t in range(TT):
                    last = dve.tensor_scalar(res[:, par, t, :], y[:, t, :], mean_y[:, t:t + 1], rs_y[:, t:t + 1], ALU.subtract, ALU.mult)
                last.then_inc(s["res"], 1)
            with dve.Fori(0, B // 2) as q:
                sum_and_normalize(2 * q, 0, q)
                sum_and_normalize(2 * q + 1, 1, q)

        @block.gpsimd
        def _(pool):
            def weigh(b, par, q):
                count = in_register(pool, 32 * (q + 1) + 1)
                pool.wait_ge(*met)
                pool.wait_ge(s[f"w2_in{par}"], count)
                count = in_register(pool, used(b))
                pool.wait_ge(*met)
                pool.wait_ge(s["pe_down"], count)
                for e in range(TOP):
                    share_of_e = weight[:, bass.ds(b * TOP + e, 1)].unsqueeze(2).to_broadcast([P, FE, D])
                    last = pool.tensor_tensor(w2p[:, par, e * FE:(e + 1) * FE, :], w2[:, par, e], share_of_e, ALU.mult)
                last.then_inc(s["w2p"], 1)

            def scale(b):
                count = in_register(pool, b + 2)
                pool.wait_ge(*met)
                pool.wait_ge(s["yvar"], count)
                pool.tensor_tensor(rs_y[:, :], vs_y[:, :], T["mhalf"][:, 0:TT], ALU.pow).then_inc(s["yrs"], 1)

            pool.wait_ge(s["var"], 2)
            pool.tensor_tensor(rs[:, :], vs[:, :], T["mhalf"][:, 0:TT], ALU.pow).then_inc(s["rs"], 1)
            pool.wait_ge(s["weight"], 2)
            weigh(0, 0, 0)
            weigh(1, 1, 0)
            with pool.Fori(1, B // 2) as q:
                for par in range(2):
                    scale(2 * q + par - 2)
                    weigh(2 * q + par, par, q)
            for b in range(B - 2, B):
                scale(b)

        @block.scalar
        def _(act):
            act.wait_ge(s["pe_T"], 2)
            act.activation(n2T[:, B - 1, :], bank[0][:, :], ACT.Identity, scale=ln[:, 0:1], bias=ln[:, 1:2], accum_out=msum[:, B - 1:B]).then_inc(s["n2T"], 1)
            act.wait_ge(s["lmx"], 2)
            act.activation(pexp[:, :], lg[:, :], ACT.Exp, bias=lmx[:, :], accum_out=psm[:, :]).then_inc(s["pexp"], 1)

            def gelu(b, par, q):
                act.wait_ge(s["pe_down"], used(b))
                for j in range(HB):
                    act.wait_ge(s["pe_up"], b * HB + j + 2)
                    act.activation(hid[:, par, j, :], bank[j][:, :], ACT.Gelu).then_inc(s["gelu"], 1)

            def store(b, par):
                act.wait_ge(s["res"], b + 2)
                act.dma_start(out[bass.ds(b, 1), :, :].rearrange("o (t p) d -> p (o t) d", p=P), res[:, par]).then_inc(s[f"stored{par}"], 16)
            gelu(0, 0, 0)
            gelu(1, 1, 0)
            with act.Fori(1, B // 2) as q:
                for par in range(2):
                    gelu(2 * q + par, par, q)
                    store(2 * q + par - 2, par)
            for par in range(2):
                store(B - 2 + par, par)
            for par in range(2):
                act.wait_ge(s[f"stored{par}"], 16 * (B // 2) + 1)

        @block.tensor
        def _(pe):
            pe.wait_ge(s["xh"], 2)
            for t in range(TT):
                last = pe.transpose(bank[0][:, t * P:(t + 1) * P], xh[:, t, :], ident[:, :])
            last.then_inc(s["pe_T"], 1)
            pe.wait_ge(s["mtok"], 2)
            pe.matmul(bank[2][0:B, 0:NE], mtok[:, :], rw[:, :], start=True, stop=True).then_inc(s["pe_lg"], 1)
            pe.wait_ge(s["diag"], 2)
            pe.matmul(bank[3][:, 0:B * TOP], ones[0:B, :], diag[:, :, :].rearrange("s b e -> s (b e)"), start=True, stop=True).then_inc(s["pe_weight"], 1)
            pe.wait_ge(s["weight"], 2)

            def up(b, par, q):
                pe.wait_ge(s[f"w1_in{par}"], 32 * (q + 1) + 1)
                for j in range(HB):
                    if isinstance(b, int) and b == 0:
                        pe.wait_ge(s["n2T"], 2)
                    else:
                        pe.wait_ge(s["gelu"], (b - 1) * HB + j + 2)
                    pe.matmul(bank[j][:, :], w1[:, par, j // FE, (j % FE) * P:(j % FE + 1) * P], rows(n2T, b), start=True, stop=True).then_inc(s["pe_up"], 1)

            def down(b, par):
                pe.wait_ge(s["gelu"], (b + 1) * HB + 1)
                pe.wait_ge(s["w2p"], b + 2)
                pe.wait_ge(s["y"], used(b))
                for t in range(TT):
                    for j in range(HB):
                        last = pe.matmul(bank[4 + par][:, t * P:(t + 1) * P], hid[:, par, j, t * P:(t + 1) * P], w2p[:, par, j, :], start=j == 0, stop=j == HB - 1)
                last.then_inc(s["pe_down"], 1)
            up(0, 0, 0)
            up(1, 1, 0)
            down(0, 0)
            with pe.Fori(1, B // 2) as q:
                up(2 * q, 0, q)
                down(2 * q - 1, 1)
                up(2 * q + 1, 1, q)
                down(2 * q, 0)
            down(B - 1, 1)

        @block.sync
        def _(sp):
            sp.wait_ge(s["which"], 2)
            sp.dma_start(chosen[:, :], which[:, 0:TOP]).then_inc(s["chosen"], 16)
            sp.wait_ge(s["chosen"], 17)

            def load(b, par, q):
                if not isinstance(b, int):
                    count = in_register(sp, (b - 1) * HB + 1)
                    sp.wait_ge(*met)
                    sp.wait_ge(s["pe_up"], count)
                    count = in_register(sp, b)
                    sp.wait_ge(*met)
                    sp.wait_ge(s["w2p"], count)
                experts = [sp.value_load(chosen[0:1, bass.ds(b * TOP + e, 1)], min_val=0, max_val=NE - 1) for e in range(TOP)]
                for e, x in enumerate(experts):
                    sp.dma_start(w1[:, par, e, :], dram["fw1"][bass.ds(x, 1), :, :].rearrange("o d f -> d (o f)")).then_inc(s[f"w1_in{par}"], 16)
                for e, x in enumerate(experts):
                    sp.dma_start(w2[:, par, e], dram["fw2"][bass.ds(x, 1), :, :].rearrange("o (j p) d -> p (o j) d", p=P)).then_inc(s[f"w2_in{par}"], 16)

            load(0, 0, 0)
            load(1, 1, 0)
            with sp.Fori(1, B // 2) as q:
                load(2 * q, 0, q)
                load(2 * q + 1, 1, q)


def build(nc, dram, out):
    with ExitStack() as ctx:
        def sb(name, shape, dt=FP32):
            return ctx.enter_context(nc.sbuf_tensor(name, shape, dt))
        T = {"X": sb("X", [P, B * TT, D]), "ident": sb("ident", [P, P]), "tri": sb("tri", [P, P]),
             "above": sb("above", [P, P]), "ones": sb("ones", [P, P]), "mhalf": sb("mhalf", [P, TT])}
        T["bank"] = [ctx.enter_context(nc.psum_tensor(f"bank{i}", [P, 512], FP32)) for i in range(8)]
        T["x_first"] = ctx.enter_context(nc.semaphore("x_first"))
        T["x_rest"] = ctx.enter_context(nc.semaphore("x_rest"))
        T["masks"] = ctx.enter_context(nc.semaphore("masks"))

        T["later"] = ctx.enter_context(nc.semaphore("later_weights"))
        raw, wv, wo = sb("raw", [P, 2, MX, H * KD]), sb("wv", [P, MX, H * KD]), sb("wo", [P, MX, D])
        bq, bk, bv, bo = sb("bq", [P, MX]), sb("bk", [P, MX]), sb("bv", [P, MX * H * KD]), sb("bo", [P, MX, D])
        rw, rb, ln1 = sb("rw", [P, MX]), sb("rb", [P, MX]), sb("ln1", [P, 2])
        f_rw, f_rb, f_ln = sb("f_rw", [P, NE]), sb("f_rb", [P, NE]), sb("f_ln", [P, 2])
        T.update(raw=raw, wv=wv, wo=wo, bq=bq, bk=bk, bv=bv, bo=bo, rw=rw, rb=rb, ln1=ln1, f_rw=f_rw, f_rb=f_rb, f_ln=f_ln)
        loads = []
        for m in range(MX):
            loads += [(raw[:, 0, m, :], dram["wq"][m].rearrange("d h k -> d (h k)")),
                      (raw[:, 1, m, :], dram["wk"][m].rearrange("d h k -> d (h k)")),
                      (wv[:, m, :], dram["wv"][m].rearrange("d h k -> d (h k)")),
                      (wo[:, m, :], dram["wo"][m].rearrange("h k d -> (h k) d")),
                      (bq[:, m:m + 1], dram["bq"][m].rearrange("h k -> k h")),
                      (bk[:, m:m + 1], dram["bk"][m].rearrange("h k -> k h")),
                      (bo[:, m, :], dram["bo"][m].partition_broadcast(P))]
        loads += [(bv[:, :], dram["bv"].rearrange("m h k -> (m h k)").partition_broadcast(P)),
                  (rw[:, :], dram["rw"]), (rb[:, :], dram["rb"].partition_broadcast(P)),
                  (ln1[:, 0:1], dram["ln1_g"].rearrange("(p o) -> p o", o=1)), (ln1[:, 1:2], dram["ln1_b"].rearrange("(p o) -> p o", o=1)),
                  (f_rw[:, :], dram["f_rw"]), (f_rb[:, :], dram["f_rb"].partition_broadcast(P)),
                  (f_ln[:, 0:1], dram["ln2_g"].rearrange("(p o) -> p o", o=1)), (f_ln[:, 1:2], dram["ln2_b"].rearrange("(p o) -> p o", o=1))]
        T["later_loads"] = len(loads)
        with ExitStack() as inner:
            build_mamba(nc, inner, T, dram, loads)
        T["X1"] = T["X"]
        T["X"] = sb("X2", [P, B * TT, D])
        T["n2T"], T["sum_n2"] = sb("n2T", [P, B, L]), sb("sum_n2", [P, B])
        with ExitStack() as inner:
            build_attention(nc, inner, T)
        with ExitStack() as inner:
            build_experts(nc, inner, T, dram, out)


_INS = {'x': 'L0_attn_x', 'w_in': 'L0_attn_w_in', 'conv_w': 'L0_attn_conv_w', 'conv_b': 'L0_attn_conv_b', 'dt_bias': 'L0_attn_dt_bias',
        'a_log': 'L0_attn_a_log', 'd_skip': 'L0_attn_d_skip', 'norm_w': 'L0_attn_norm_w', 'w_out': 'L0_attn_w_out', 'w_fc': 'L0_attn_w_fc', 'w_proj': 'L0_attn_w_proj',
        'ln1_g': 'L0_ffn_ln1_g', 'ln1_b': 'L0_ffn_ln1_b', 'wq': 'L0_ffn_mha_wq', 'wk': 'L0_ffn_mha_wk', 'wv': 'L0_ffn_mha_wv', 'wo': 'L0_ffn_mha_wo',
        'bq': 'L0_ffn_mha_bq', 'bk': 'L0_ffn_mha_bk', 'bv': 'L0_ffn_mha_bv', 'bo': 'L0_ffn_mha_bo', 'rw': 'L0_ffn_mha_rw', 'rb': 'L0_ffn_mha_rb',
        'ln2_g': 'L0_ffn_ln2_g', 'ln2_b': 'L0_ffn_ln2_b', 'f_rw': 'L0_ffn_ffn_rw', 'f_rb': 'L0_ffn_ffn_rb', 'fw1': 'L0_ffn_fw1', 'fw2': 'L0_ffn_fw2'}


def kernel(**inputs):
    import numpy as _np
    import concourse.bacc as _bacc
    from concourse import mybir as _mybir
    from concourse.bass_utils import run_bass_kernel_spmd as _run

    nc = _bacc.Bacc("TRN2", target_bir_lowering=False, num_devices=1)
    arrays, dram = {}, {}
    for short, name in _INS.items():
        a = _np.ascontiguousarray(inputs[name])
        arrays["in_" + short] = a
        dram[short] = nc.dram_tensor("in_" + short, a.shape, _mybir.dt.from_np(a.dtype), kind="ExternalInput").ap()
    out = nc.dram_tensor("out_0", (8, 512, 128), _mybir.dt.float32, kind="ExternalOutput").ap()
    build(nc, dram, out)
    r = _run(nc, [arrays], core_ids=[0])
    return r.results[0]["out_0"]
```
